# Optimizing a Trainium2 kernel written in Bass

```python
import numpy as np
import jax
import jax.numpy as jnp

def _softmax(x, axis=-1):
    return jax.nn.softmax(x, axis=axis)

def _gelu(x):
    return jax.nn.gelu(x, approximate=True)

def _silu(x):
    return jax.nn.silu(x)

def _sigmoid(x):
    return jax.nn.sigmoid(x)

def _layernorm(x, axis=-1, eps=1e-05):
    m = jnp.mean(x, axis=axis, keepdims=True)
    v = jnp.var(x, axis=axis, keepdims=True)
    return (x - m) / jnp.sqrt(v + eps)

def _scatter_add(tgt, idx, src, axis=0):
    return tgt.at[idx].add(src)

def _segment_sum(src, seg, n):
    return jax.ops.segment_sum(src, seg, n)
kernel_name = 'mk_recurrent_d1_jaxref_r4_30fdf0'

def setup_inputs(seed: int=0):
    np.random.seed(seed)
    _w = jnp.asarray

    def _L0_attn_setup():
        import jax, jax.numpy as jnp
        import numpy as np
        import math
        B, T, D = (2, 1024, 256)
        H = 16
        HEAD_DIM = D // H
        CHUNK = 64

        def chunked_attention(q, k, v, chunk_size, scale):
            Bq, Hq, Tq, hd = q.shape
            S = k.shape[2]
            nc = Tq // chunk_size
            q_chunks = q.reshape(Bq, Hq, nc, chunk_size, hd).transpose(2, 0, 1, 3, 4)
            starts = jnp.arange(nc, dtype=jnp.int32) * chunk_size
            k_pos = jnp.arange(S)

            def body(carry, xs):
                qc, start = xs
                scores = jnp.einsum('bhqd,bhkd->bhqk', qc, k) * scale
                q_pos = start + jnp.arange(chunk_size)
                causal_mask = k_pos[None, :] > q_pos[:, None]
                scores = jnp.where(causal_mask[None, None], -jnp.inf, scores)
                m = jnp.max(scores, axis=-1, keepdims=True)
                m = jnp.where(jnp.isinf(m), jnp.zeros_like(m), m)
                p = jax.nn.softmax(scores - m, axis=-1)
                oc = jnp.einsum('bhqk,bhkd->bhqd', p, v)
                return (carry, oc)
            _, outs = jax.lax.scan(body, None, (q_chunks, starts))
            return outs.transpose(1, 2, 0, 3, 4).reshape(Bq, Hq, Tq, hd)
        key = jax.random.key(seed)
        ks = jax.random.split(key, 9)
        s = 1.0 / math.sqrt(D)
        return {'x': jax.random.normal(ks[0], (B, T, D), dtype=jnp.float32), 'Wq': jax.random.normal(ks[1], (D, D), dtype=jnp.float32) * s, 'bq': jax.random.normal(ks[2], (D,), dtype=jnp.float32) * 0.01, 'Wk': jax.random.normal(ks[3], (D, D), dtype=jnp.float32) * s, 'bk': jax.random.normal(ks[4], (D,), dtype=jnp.float32) * 0.01, 'Wv': jax.random.normal(ks[5], (D, D), dtype=jnp.float32) * s, 'bv': jax.random.normal(ks[6], (D,), dtype=jnp.float32) * 0.01, 'Wo': jax.random.normal(ks[7], (D, D), dtype=jnp.float32) * s, 'bo': jax.random.normal(ks[8], (D,), dtype=jnp.float32) * 0.01}
    _L0_attn_in = _L0_attn_setup()

    def _L0_ffn_setup():
        import jax, jax.numpy as jnp
        import numpy as np
        DIM = 256
        DEPTH = 2
        HEADS = 8
        DIM_HEAD = 64
        WINDOW = 128
        INNER = HEADS * DIM_HEAD
        HID = int(DIM * 4 * 2 / 3)
        B, N = (2, 2048)
        QK_SCALE = 8.0

        def shift_token(t):
            t1, t2 = jnp.split(t, 2, axis=-1)
            t2 = jnp.pad(t2, ((0, 0), (1, 0), (0, 0)))[:, :-1]
            return jnp.concatenate([t1, t2], axis=-1)

        def l2norm(t):
            return t / jnp.clip(jnp.linalg.norm(t, axis=-1, keepdims=True), 1e-12)

        def rotate_half(x):
            x1, x2 = jnp.split(x, 2, axis=-1)
            return jnp.concatenate([-x2, x1], axis=-1)

        def rotary_xpos(q, k):
            n = q.shape[-2]
            half_idx = jnp.arange(0, DIM_HEAD, 2, dtype=jnp.float32)
            inv_freq = 1.0 / 10000.0 ** (half_idx / DIM_HEAD)
            t = jnp.arange(n, dtype=jnp.float32)
            freqs = t[:, None] * inv_freq[None, :]
            freqs = jnp.concatenate([freqs, freqs], axis=-1)
            base = (half_idx + 0.4 * DIM_HEAD) / (1.4 * DIM_HEAD)
            power = (t - n // 2) / float(WINDOW // 2)
            scale = base[None, :] ** power[:, None]
            scale = jnp.concatenate([scale, scale], axis=-1)
            cos, sin = (jnp.cos(freqs), jnp.sin(freqs))
            q = q * cos * scale + rotate_half(q) * sin * scale
            k = k * cos / scale + rotate_half(k) * sin / scale
            return (q, k)

        def local_attention(q, k, v):
            b, h, n, d = q.shape
            w = n // WINDOW
            bq = q.reshape(b, h, w, WINDOW, d) * QK_SCALE
            bk = k.reshape(b, h, w, WINDOW, d)
            bv = v.reshape(b, h, w, WINDOW, d)

            def look_around(t):
                p = jnp.pad(t, ((0, 0), (0, 0), (1, 0), (0, 0), (0, 0)))
                return jnp.concatenate([p[:, :, :w], p[:, :, 1:]], axis=3)
            bk, bv = (look_around(bk), look_around(bv))
            bt = jnp.arange(n).reshape(w, WINDOW)
            btp = jnp.pad(bt, ((1, 0), (0, 0)), constant_values=-1)
            btk = jnp.concatenate([btp[:w], btp[1:]], axis=1)
            sim = jnp.einsum('bhwid,bhwjd->bhwij', bq, bk)
            i = bt[:, :, None]
            j = btk[:, None, :]
            mask = (i < j) | (i > j + WINDOW) | (j == -1)
            sim = jnp.where(mask, -jnp.finfo(sim.dtype).max, sim)
            attn = jax.nn.softmax(sim, axis=-1)
            out = jnp.einsum('bhwij,bhwjd->bhwid', attn, bv)
            return out.reshape(b, h, n, d)

        def _layer(x, wqkv, qs, ksc, wo, lg, lb, w1, b1, w2, b2):
            b, n, _ = x.shape
            h = shift_token(x)
            qkv = h @ wqkv
            q, k, v = jnp.split(qkv, 3, axis=-1)
            to_heads = lambda t: t.reshape(b, n, HEADS, DIM_HEAD).transpose(0, 2, 1, 3)
            q, k, v = (to_heads(q), to_heads(k), to_heads(v))
            q = l2norm(q) * qs
            k = l2norm(k) * ksc
            q, k = rotary_xpos(q, k)
            o = local_attention(q, k, v)
            o = o.transpose(0, 2, 1, 3).reshape(b, n, INNER)
            x = x + o @ wo
            h = shift_token(x)
            mu = h.mean(-1, keepdims=True)
            var = h.var(-1, keepdims=True)
            h = (h - mu) / jnp.sqrt(var + 1e-05) * lg + lb
            h = h @ w1 + b1
            a, g = jnp.split(h, 2, axis=-1)
            h = a * jax.nn.gelu(g, approximate=False)
            x = x + h @ w2 + b2
            return x
        key = jax.random.key(seed)
        ks = jax.random.split(key, 6)
        return {'x': jax.random.normal(ks[0], (B, N, DIM), jnp.float32), 'wqkv': jax.random.normal(ks[1], (DEPTH, DIM, 3 * INNER), jnp.float32) * 0.02, 'q_scale': jnp.ones((DEPTH, DIM_HEAD), jnp.float32), 'k_scale': jnp.ones((DEPTH, DIM_HEAD), jnp.float32), 'wo': jax.random.normal(ks[2], (DEPTH, INNER, DIM), jnp.float32) * 0.02, 'ln_g': jnp.ones((DEPTH, DIM), jnp.float32), 'ln_b': jnp.zeros((DEPTH, DIM), jnp.float32), 'w1': jax.random.normal(ks[3], (DEPTH, DIM, 2 * HID), jnp.float32) * 0.02, 'b1': jnp.zeros((DEPTH, 2 * HID), jnp.float32), 'w2': jax.random.normal(ks[4], (DEPTH, HID, DIM), jnp.float32) * 0.02, 'b2': jnp.zeros((DEPTH, DIM), jnp.float32)}
    _L0_ffn_in = _L0_ffn_setup()
    _d = {'L0_attn_x': _L0_attn_in['x'], 'L0_attn_Wq': _L0_attn_in['Wq'], 'L0_attn_bq': _L0_attn_in['bq'], 'L0_attn_Wk': _L0_attn_in['Wk'], 'L0_attn_bk': _L0_attn_in['bk'], 'L0_attn_Wv': _L0_attn_in['Wv'], 'L0_attn_bv': _L0_attn_in['bv'], 'L0_attn_Wo': _L0_attn_in['Wo'], 'L0_attn_bo': _L0_attn_in['bo'], 'L0_ffn_wqkv': _L0_ffn_in['wqkv'], 'L0_ffn_q_scale': _L0_ffn_in['q_scale'], 'L0_ffn_k_scale': _L0_ffn_in['k_scale'], 'L0_ffn_wo': _L0_ffn_in['wo'], 'L0_ffn_ln_g': _L0_ffn_in['ln_g'], 'L0_ffn_ln_b': _L0_ffn_in['ln_b'], 'L0_ffn_w1': _L0_ffn_in['w1'], 'L0_ffn_b1': _L0_ffn_in['b1'], 'L0_ffn_w2': _L0_ffn_in['w2'], 'L0_ffn_b2': _L0_ffn_in['b2']}
    _x0 = _d['L0_attn_x']
    _d['L0_attn_x'] = jax.random.normal(jax.random.fold_in(jax.random.key(seed), 1), (4, 2048, 256), dtype=_x0.dtype)
    del _x0
    return _d

def reference(L0_attn_x, L0_attn_Wq, L0_attn_bq, L0_attn_Wk, L0_attn_bk, L0_attn_Wv, L0_attn_bv, L0_attn_Wo, L0_attn_bo, L0_ffn_wqkv, L0_ffn_q_scale, L0_ffn_k_scale, L0_ffn_wo, L0_ffn_ln_g, L0_ffn_ln_b, L0_ffn_w1, L0_ffn_b1, L0_ffn_w2, L0_ffn_b2):

    def _L0_attn_ref(x, Wq, bq, Wk, bk, Wv, bv, Wo, bo):
        import jax, jax.numpy as jnp
        import numpy as np
        import math
        B, T, D = (2, 1024, 256)
        H = 16
        HEAD_DIM = D // H
        CHUNK = 64

        def chunked_attention(q, k, v, chunk_size, scale):
            Bq, Hq, Tq, hd = q.shape
            S = k.shape[2]
            nc = Tq // chunk_size
            q_chunks = q.reshape(Bq, Hq, nc, chunk_size, hd).transpose(2, 0, 1, 3, 4)
            starts = jnp.arange(nc, dtype=jnp.int32) * chunk_size
            k_pos = jnp.arange(S)

            def body(carry, xs):
                qc, start = xs
                scores = jnp.einsum('bhqd,bhkd->bhqk', qc, k) * scale
                q_pos = start + jnp.arange(chunk_size)
                causal_mask = k_pos[None, :] > q_pos[:, None]
                scores = jnp.where(causal_mask[None, None], -jnp.inf, scores)
                m = jnp.max(scores, axis=-1, keepdims=True)
                m = jnp.where(jnp.isinf(m), jnp.zeros_like(m), m)
                p = jax.nn.softmax(scores - m, axis=-1)
                oc = jnp.einsum('bhqk,bhkd->bhqd', p, v)
                return (carry, oc)
            _, outs = jax.lax.scan(body, None, (q_chunks, starts))
            return outs.transpose(1, 2, 0, 3, 4).reshape(Bq, Hq, Tq, hd)
        Bx, Tx, Dx = x.shape
        scale = 1.0 / math.sqrt(HEAD_DIM)

        def proj(W, b):
            y = x @ W.T + b
            return y.reshape(Bx, Tx, H, HEAD_DIM).transpose(0, 2, 1, 3)
        q = proj(Wq, bq)
        k = proj(Wk, bk)
        v = proj(Wv, bv)
        out = chunked_attention(q, k, v, CHUNK, scale)
        out = out.transpose(0, 2, 1, 3).reshape(Bx, Tx, Dx)
        return out @ Wo.T + bo

    def _L0_ffn_ref(x, wqkv, q_scale, k_scale, wo, ln_g, ln_b, w1, b1, w2, b2):
        import jax, jax.numpy as jnp
        import numpy as np
        DIM = 256
        DEPTH = 2
        HEADS = 8
        DIM_HEAD = 64
        WINDOW = 128
        INNER = HEADS * DIM_HEAD
        HID = int(DIM * 4 * 2 / 3)
        B, N = (2, 2048)
        QK_SCALE = 8.0

        def shift_token(t):
            t1, t2 = jnp.split(t, 2, axis=-1)
            t2 = jnp.pad(t2, ((0, 0), (1, 0), (0, 0)))[:, :-1]
            return jnp.concatenate([t1, t2], axis=-1)

        def l2norm(t):
            return t / jnp.clip(jnp.linalg.norm(t, axis=-1, keepdims=True), 1e-12)

        def rotate_half(x):
            x1, x2 = jnp.split(x, 2, axis=-1)
            return jnp.concatenate([-x2, x1], axis=-1)

        def rotary_xpos(q, k):
            n = q.shape[-2]
            half_idx = jnp.arange(0, DIM_HEAD, 2, dtype=jnp.float32)
            inv_freq = 1.0 / 10000.0 ** (half_idx / DIM_HEAD)
            t = jnp.arange(n, dtype=jnp.float32)
            freqs = t[:, None] * inv_freq[None, :]
            freqs = jnp.concatenate([freqs, freqs], axis=-1)
            base = (half_idx + 0.4 * DIM_HEAD) / (1.4 * DIM_HEAD)
            power = (t - n // 2) / float(WINDOW // 2)
            scale = base[None, :] ** power[:, None]
            scale = jnp.concatenate([scale, scale], axis=-1)
            cos, sin = (jnp.cos(freqs), jnp.sin(freqs))
            q = q * cos * scale + rotate_half(q) * sin * scale
            k = k * cos / scale + rotate_half(k) * sin / scale
            return (q, k)

        def local_attention(q, k, v):
            b, h, n, d = q.shape
            w = n // WINDOW
            bq = q.reshape(b, h, w, WINDOW, d) * QK_SCALE
            bk = k.reshape(b, h, w, WINDOW, d)
            bv = v.reshape(b, h, w, WINDOW, d)

            def look_around(t):
                p = jnp.pad(t, ((0, 0), (0, 0), (1, 0), (0, 0), (0, 0)))
                return jnp.concatenate([p[:, :, :w], p[:, :, 1:]], axis=3)
            bk, bv = (look_around(bk), look_around(bv))
            bt = jnp.arange(n).reshape(w, WINDOW)
            btp = jnp.pad(bt, ((1, 0), (0, 0)), constant_values=-1)
            btk = jnp.concatenate([btp[:w], btp[1:]], axis=1)
            sim = jnp.einsum('bhwid,bhwjd->bhwij', bq, bk)
            i = bt[:, :, None]
            j = btk[:, None, :]
            mask = (i < j) | (i > j + WINDOW) | (j == -1)
            sim = jnp.where(mask, -jnp.finfo(sim.dtype).max, sim)
            attn = jax.nn.softmax(sim, axis=-1)
            out = jnp.einsum('bhwij,bhwjd->bhwid', attn, bv)
            return out.reshape(b, h, n, d)

        def _layer(x, wqkv, qs, ksc, wo, lg, lb, w1, b1, w2, b2):
            b, n, _ = x.shape
            h = shift_token(x)
            qkv = h @ wqkv
            q, k, v = jnp.split(qkv, 3, axis=-1)
            to_heads = lambda t: t.reshape(b, n, HEADS, DIM_HEAD).transpose(0, 2, 1, 3)
            q, k, v = (to_heads(q), to_heads(k), to_heads(v))
            q = l2norm(q) * qs
            k = l2norm(k) * ksc
            q, k = rotary_xpos(q, k)
            o = local_attention(q, k, v)
            o = o.transpose(0, 2, 1, 3).reshape(b, n, INNER)
            x = x + o @ wo
            h = shift_token(x)
            mu = h.mean(-1, keepdims=True)
            var = h.var(-1, keepdims=True)
            h = (h - mu) / jnp.sqrt(var + 1e-05) * lg + lb
            h = h @ w1 + b1
            a, g = jnp.split(h, 2, axis=-1)
            h = a * jax.nn.gelu(g, approximate=False)
            x = x + h @ w2 + b2
            return x
        for l in range(DEPTH):
            x = _layer(x, wqkv[l], q_scale[l], k_scale[l], wo[l], ln_g[l], ln_b[l], w1[l], b1[l], w2[l], b2[l])
        return x
    x = L0_attn_x
    xn = _layernorm(x, axis=-1)
    s = _L0_attn_ref(xn, L0_attn_Wq, L0_attn_bq, L0_attn_Wk, L0_attn_bk, L0_attn_Wv, L0_attn_bv, L0_attn_Wo, L0_attn_bo)
    g = _silu(_L0_ffn_ref(xn, L0_ffn_wqkv, L0_ffn_q_scale, L0_ffn_k_scale, L0_ffn_wo, L0_ffn_ln_g, L0_ffn_ln_b, L0_ffn_w1, L0_ffn_b1, L0_ffn_w2, L0_ffn_b2))
    x = x + s * g
    return x

_drawn_inputs = setup_inputs


def setup_inputs(seed=0):
    import zlib

    import numpy as np

    out = dict(_drawn_inputs(seed))
    spreads = {'L0_ffn_q_scale': (1.0, 0.6),
     'L0_ffn_k_scale': (1.0, 0.6),
     'L0_ffn_ln_g': (1.0, 0.6),
     'L0_ffn_ln_b': (0.0, 0.8),
     'L0_ffn_b1': (0.0, 0.8),
     'L0_ffn_b2': (0.0, 0.8)}
    factors = {'L0_attn_bq': 8.0,
     'L0_attn_bk': 8.0,
     'L0_attn_bv': 8.0,
     'L0_attn_bo': 8.0,
     'L0_ffn_wqkv': 8.0,
     'L0_ffn_wo': 8.0,
     'L0_ffn_w1': 8.0,
     'L0_ffn_w2': 8.0}
    for name, (base, spread) in spreads.items():
        noise = np.random.default_rng([zlib.crc32(name.encode()), seed]).standard_normal(out[name].shape)
        drawn = base * np.exp(spread * noise) if base else spread * noise
        out[name] = jnp.asarray(drawn.astype(out[name].dtype))
    for name, factor in factors.items():
        out[name] = (out[name] * factor).astype(out[name].dtype)
    return out
```

```python
from contextlib import ExitStack

import numpy as np

import concourse.bass as bass
from concourse import mybir

F32 = mybir.dt.float32
F32R = mybir.dt.float32r
BF16 = mybir.dt.bfloat16
ALU = mybir.AluOpType
ACT = mybir.ActivationFunctionType
AX = mybir.AxisListType

P = 128
BATCH, SEQ, DIM = 4, 2048, 256
ROWS = BATCH * SEQ
KT = DIM // P
CHUNK = 512
TPC = CHUNK // P
NCHUNK = ROWS // CHUNK
CPB = SEQ // CHUNK
EPS = 1e-5

A_HEADS, A_HD = 16, 16
GH = 4
NGROUP = A_HEADS // GH
A_SCALE = A_HD ** -0.5
STACK_Q = [0, 0, 1, 1, 0, 2]
STACK_K = [0, 1, 0, 1, 2, 0]
NSTACK = len(STACK_Q)
SROWS = NSTACK * A_HD
VW = 32

DEPTH, HEADS, HD = 2, 8, 64
WINDOW = 128
INNER = HEADS * HD
HID = 682
QK_SCALE = 8.0
MT = 6
MW = -(-HID // MT)
BIG = 1e30



class Tally:

    def __init__(self, sem, per=1, spare=0):
        self.sem, self.per, self.spare = sem, per, spare

    def at(self, n, k=None):
        return n * self.per + (self.per if k is None else k) + self.spare * self.per

    def at_turn(self, n, u):
        return (n - u) * (self.per // 2) + self.per + self.spare * self.per

    def before_turn(self, n, u):
        return (n - u) * (self.per // 2) + self.spare * self.per

    def open(self, eng):
        eng.sem_inc(self.sem, self.spare * self.per)


def staggered(eng, count, *stages):
    last = len(stages) - 1

    def turn(n, u):
        for j, stage in enumerate(stages):
            if not isinstance(n, int) or 0 <= n - j < count:
                stage(n - j, (u - j) % 2)

    lead = last + last % 2
    rounds = (count - lead) // 2
    for n in range(lead):
        turn(n, n % 2)
    with eng.Fori(0, rounds) as i:
        for u in range(2):
            turn(i * 2 + (lead + u), u)
    for n in range(lead + 2 * rounds, count + last):
        turn(n, n % 2)


def prepare(nc, x, wT, bias_cols, bv, ident_d, xn_d, qk_d, v_d):
    with ExitStack() as ctx:
        def sb(name, shape, dt=F32):
            return ctx.enter_context(nc.sbuf_tensor("p_" + name, shape, dt))

        def tally(name, per=1, spare=0):
            return Tally(ctx.enter_context(nc.semaphore("p_" + name)), per, spare)

        ident = sb("ident", [P, P])
        w_raw = sb("w_raw", [P, KT, 3 * DIM])
        w_hi = sb("w_hi", [P, KT, 3 * DIM], F32R)
        w_lo = sb("w_lo", [P, KT, 3 * DIM], F32R)
        bcol = sb("bcol", [P, 4])
        bcol_s = sb("bcol_s", [P, 4])
        bv_row = sb("bv_row", [P, DIM])
        half = sb("half", [P, TPC])
        gate = sb("gate", [P, 2])
        x_in = sb("x_in", [P, 2, TPC, DIM])
        stats = sb("stats", [P, 2, TPC, 6])
        mv = sb("mv", [P, 2, TPC, 2])
        var = sb("var", [P, 2, TPC])
        rstd = sb("rstd", [P, 2, TPC])
        xn = sb("xn", [P, 2, TPC, DIM])
        xt = sb("xt", [P, 2, KT, CHUNK])
        x_hi = sb("x_hi", [P, 2, KT, CHUNK], F32R)
        x_lo = sb("x_lo", [P, 2, KT, CHUNK], F32R)
        qf = sb("qf", [P, 4, CHUNK])
        rest = sb("rest", [P, 4, CHUNK])
        parts = sb("parts", [P, 2, 3, 4, CHUNK], BF16)
        vt = sb("vt", [P, 2, TPC, A_HEADS, VW])
        trp = ctx.enter_context(nc.psum_tensor("p_trp", [P, KT, CHUNK], F32))
        qkp = ctx.enter_context(nc.psum_tensor("p_qkp", [P, 4, CHUNK], F32))
        vp = ctx.enter_context(nc.psum_tensor("p_vp", [P, TPC, DIM], F32))

        consts = tally("consts").sem
        w_split = tally("w_split").sem
        init = tally("init").sem
        x_loaded = [tally(f"x_loaded{u}", 16) for u in range(2)]
        x_stored = [tally(f"x_stored{u}", 16, 1) for u in range(2)]
        parts_stored = [tally(f"parts_stored{u}", 16, 1) for u in range(2)]
        v_stored = [tally(f"v_stored{u}", 16, 1) for u in range(2)]
        stat_done = tally("stat_done", TPC)
        aggr_done = tally("aggr_done", TPC)
        var_ready = tally("var_ready")
        rstd_ready = tally("rstd_ready")
        xn_ready = tally("xn_ready", TPC, 2)
        tr_done = tally("tr_done")
        xt_ready = tally("xt_ready", 1, 1)
        hi_ready = tally("hi_ready")
        lo_ready = tally("lo_ready", 1, 2)
        qk_done = tally("qk_done")
        qf_ready = tally("qf_ready", 1, 1)
        part1 = tally("part1")
        rest_ready = tally("rest_ready", 1, 1)
        part2 = tally("part2")
        part3 = tally("part3", 1, 1)
        v_done = tally("v_done")
        v_ready = tally("v_ready", 1, 1)
        block = ctx.enter_context(nc.Block())

        x_v = x.rearrange("b (c t p) d -> p (b c) t d", p=P, t=TPC)
        xn_v = xn_d.rearrange("k p (c n) -> p k c n", n=CHUNK)
        qk_v = qk_d.rearrange("s o p (c n) -> p (s o) c n", n=CHUNK)
        v_v = v_d.rearrange("(c t p) d -> p c t d", p=P, t=TPC)

        @block.sync
        def _(sp):
            sp.dma_start(ident[:, :], ident_d).then_inc(consts, 16)
            for j in range(3):
                sp.dma_start(w_raw[:, :, j * DIM:(j + 1) * DIM],
                             wT[j].rearrange("(k p) n -> p k n", p=P)).then_inc(consts, 16)
            sp.dma_start(bcol[:, :], bias_cols).then_inc(consts, 16)
            sp.dma_start(bv_row[:, :], bv.partition_broadcast(P)).then_inc(consts, 16)
            for t in x_stored + parts_stored + v_stored:
                t.open(sp)

            def load(n, u):
                sp.wait_ge(xn_ready.sem, xn_ready.at(n - 2))
                sp.dma_start(x_in[:, u], x_v[:, n]).then_inc(x_loaded[u].sem, 16)

            def store(n, u):
                sp.wait_ge(xt_ready.sem, xt_ready.at(n))
                sp.dma_start(xn_v[:, :, n], xt[:, u]).then_inc(x_stored[u].sem, 16)
                sp.wait_ge(v_ready.sem, v_ready.at(n))
                sp.wait_ge(part3.sem, part3.at(n))
                sp.dma_start(v_v[:, n], vt[:, u].rearrange("p t h w -> p t (h w)"))\
                  .then_inc(v_stored[u].sem, 16)
                sp.dma_start(qk_v[:, :, n], parts[:, u].rearrange("p s o n -> p (s o) n"))\
                  .then_inc(parts_stored[u].sem, 16)

            staggered(sp, NCHUNK, load, lambda n, u: None, store)
            for u in range(2):
                for t in (x_stored[u], v_stored[u], parts_stored[u]):
                    sp.wait_ge(t.sem, t.at_turn(NCHUNK - 2 + u, u))

        @block.gpsimd
        def _(pool):
            pool.memset(half[:, :], -0.5).then_inc(init, 1)
            pool.memset(vt[:, :, :, :, A_HD:A_HD + 1], 1.0).then_inc(init, 1)
            pool.memset(vt[:, :, :, :, A_HD + 1:VW], 0.0).then_inc(init, 1)
            pool.wait_ge(init, 3)
            lo_ready.open(pool)

            def root(n, u):
                pool.wait_ge(var_ready.sem, var_ready.at(n))
                pool.tensor_tensor(out=rstd[:, u], in0=var[:, u], in1=half[:, :],
                                   op=ALU.pow).then_inc(rstd_ready.sem, 1)

            def low(n, u):
                pool.wait_ge(hi_ready.sem, hi_ready.at(n))
                pool.tensor_tensor(out=x_lo[:, u], in0=xt[:, u], in1=x_hi[:, u].bitcast(F32),
                                   op=ALU.subtract).then_inc(lo_ready.sem, 1)

            staggered(pool, NCHUNK, root, low)

        @block.scalar
        def _(act):
            xt_ready.open(act)
            qf_ready.open(act)
            act.wait_ge(w_split, 4)

            def first(n, u):
                act.wait_ge(tr_done.sem, tr_done.at(n))
                act.wait_ge(x_stored[u].sem, x_stored[u].before_turn(n, u))
                act.wait_ge(lo_ready.sem, lo_ready.at(n - 2))
                act.activation(xt[:, u], trp[:, :, :], ACT.Copy).then_inc(xt_ready.sem, 1)

            def second(n, u):
                act.wait_ge(qk_done.sem, qk_done.at(n))
                act.wait_ge(part3.sem, part3.at(n - 1))
                for o in range(4):
                    q = act.activation(qf[:, o], qkp[:, o], ACT.Identity, bias=bcol_s[:, o:o + 1],
                                       scale=A_SCALE if o < 2 else 1.0)
                q.then_inc(qf_ready.sem, 1)
                act.wait_ge(qf_ready.sem, qf_ready.at(n))
                act.wait_ge(parts_stored[u].sem, parts_stored[u].before_turn(n, u))
                act.activation(parts[:, u, 0], qf[:, :, :], ACT.Copy).then_inc(part1.sem, 1)
                act.wait_ge(rest_ready.sem, rest_ready.at(n))
                act.activation(parts[:, u, 1], rest[:, :, :], ACT.Copy).then_inc(part2.sem, 1)

            staggered(act, NCHUNK, lambda n, u: None, first, second)

        @block.vector
        def _(dve):
            dve.wait_ge(consts, 96)
            dve.tensor_copy(w_hi[:, :, :], w_raw[:, :, :]).then_inc(w_split, 1)
            dve.tensor_copy(bcol_s[:, 2:4], bcol[:, 2:4]).then_inc(w_split, 1)
            dve.tensor_scalar(bcol_s[:, 0:2], bcol[:, 0:2], A_SCALE, None, ALU.mult).then_inc(w_split, 1)
            dve.memset(gate[:, 0:1], 0.0).then_inc(w_split, 1)
            dve.wait_ge(w_split, 4)
            dve.tensor_tensor(out=w_lo[:, :, :], in0=w_raw[:, :, :], in1=w_hi[:, :, :].bitcast(F32),
                              op=ALU.subtract).then_inc(w_split, 1)
            dve.wait_ge(init, 3)
            for t in (xn_ready, rest_ready, v_ready, part3):
                t.open(dve)

            def norm(n, u):
                dve.wait_ge(x_loaded[u].sem, x_loaded[u].at_turn(n, u))
                for t in range(TPC):
                    dve.bn_stats(stats[:, u, t], x_in[:, u, t]).then_inc(stat_done.sem, 1)
                dve.wait_ge(stat_done.sem, stat_done.at(n))
                dve.tensor_copy(gate[:, 1:2], gate[:, 0:1])
                for t in range(TPC):
                    dve.bn_aggr(mv[:, u, t], stats[:, u, t]).then_inc(aggr_done.sem, 1)
                dve.wait_ge(aggr_done.sem, aggr_done.at(n))
                dve.tensor_scalar(var[:, u], mv[:, u, :, 1], EPS, None, ALU.add).then_inc(var_ready.sem, 1)
                dve.wait_ge(rstd_ready.sem, rstd_ready.at(n))
                for t in range(TPC):
                    dve.tensor_scalar(xn[:, u, t], x_in[:, u, t], mv[:, u, t, 0:1], rstd[:, u, t:t + 1],
                                      ALU.subtract, ALU.mult).then_inc(xn_ready.sem, 1)

            def first(n, u):
                dve.wait_ge(xt_ready.sem, xt_ready.at(n))
                dve.tensor_copy(x_hi[:, u], xt[:, u]).then_inc(hi_ready.sem, 1)

            def second(n, u):
                dve.wait_ge(part1.sem, part1.at(n))
                dve.tensor_tensor(out=rest[:, :, :], in0=qf[:, :, :], in1=parts[:, u, 0],
                                  op=ALU.subtract).then_inc(rest_ready.sem, 1)
                dve.wait_ge(v_done.sem, v_done.at(n))
                dve.wait_ge(v_stored[u].sem, v_stored[u].before_turn(n, u))
                for t in range(TPC):
                    v = dve.tensor_tensor(out=vt[:, u, t, :, 0:A_HD],
                                          in0=vp[:, t].rearrange("p (h d) -> p h d", d=A_HD),
                                          in1=bv_row[:, :].rearrange("p (h d) -> p h d", d=A_HD),
                                          op=ALU.add)
                v.then_inc(v_ready.sem, 1)
                dve.wait_ge(part2.sem, part2.at(n))
                dve.tensor_tensor(out=parts[:, u, 2], in0=rest[:, :, :], in1=parts[:, u, 1],
                                  op=ALU.subtract).then_inc(part3.sem, 1)

            staggered(dve, NCHUNK, norm, first, second)

        @block.tensor
        def _(pe):
            pe.wait_ge(consts, 96)
            pe.wait_ge(w_split, 5)

            def first(n, u):
                pe.wait_ge(xn_ready.sem, xn_ready.at(n))
                pe.wait_ge(xt_ready.sem, xt_ready.at(n - 1))
                for t in range(TPC):
                    for k in range(KT):
                        mm = pe.transpose(trp[:, k, t * P:(t + 1) * P], xn[:, u, t, k * P:(k + 1) * P],
                                          ident[:, :])
                mm.then_inc(tr_done.sem, 1)

            def second(n, u):
                pe.wait_ge(lo_ready.sem, lo_ready.at(n))
                pe.wait_ge(qf_ready.sem, qf_ready.at(n - 1))
                for o in range(4):
                    cols = slice(o * P, (o + 1) * P)
                    steps = [(w, x_, k) for k in range(KT)
                             for w, x_ in ((w_lo, x_hi), (w_hi, x_lo), (w_hi, x_hi))]
                    for j, (w, x_, k) in enumerate(steps):
                        mm = pe.matmul(qkp[:, o], w[:, k, cols], x_[:, u, k],
                                       start=j == 0, stop=j == len(steps) - 1)
                mm.then_inc(qk_done.sem, 1)
                pe.wait_ge(v_ready.sem, v_ready.at(n - 1))
                for t in range(TPC):
                    rows = slice(t * P, (t + 1) * P)
                    steps = [(x_, w, k) for k in range(KT)
                             for x_, w in ((x_lo, w_hi), (x_hi, w_lo), (x_hi, w_hi))]
                    for j, (x_, w, k) in enumerate(steps):
                        mm = pe.matmul(vp[:, t], x_[:, u, k, rows], w[:, k, 2 * DIM:3 * DIM],
                                       start=j == 0, stop=j == len(steps) - 1)
                mm.then_inc(v_done.sem, 1)

            staggered(pe, NCHUNK, lambda n, u: None, first, second)


def attend(nc, qk_d, v_d, mask_d, ident_d, o_d):
    with ExitStack() as ctx:
        def sb(name, shape, dt=F32):
            return ctx.enter_context(nc.sbuf_tensor("a_" + name, shape, dt))

        def tally(name, per=1, spare=0):
            return Tally(ctx.enter_context(nc.semaphore("a_" + name)), per, spare)

        TASKS = TPC * GH
        STEPS = sum(TPC * (c + 1) for c in range(CPB))
        UNITS = sum(TASKS * (c + 1) for c in range(CPB))
        NG = BATCH * NGROUP
        NSLOT = 3
        NPT = 3

        ident = sb("ident", [P, P])
        identb = sb("identb", [P, P], BF16)
        maskf = sb("maskf", [P, P])
        mask = sb("mask", [P, P], BF16)
        qs = sb("qs", [P, NSLOT, GH, SEQ], BF16)
        ks = sb("ks", [P, NSLOT, GH, SEQ], BF16)
        vt = sb("vt", [P, NSLOT, SEQ // P, GH * VW])
        pt = sb("pt", [P, NPT, GH, CHUNK])
        gate = sb("gate", [P, 2])
        mx = sb("mx", [P, TASKS, CPB])
        negm = sb("negm", [P, 2, TASKS])
        ntb = sb("ntb", [TASKS, CPB, P], BF16)
        os_ = sb("os", [P, CHUNK])
        rden = sb("rden", [P, TPC, GH])
        otok = sb("otok", [P, 2, TPC, GH, A_HD])
        st = ctx.enter_context(nc.psum_tensor("a_st", [P, GH, CHUNK], F32))
        mm_ = ctx.enter_context(nc.psum_tensor("a_mm", [P, 2, CHUNK], F32))
        ot = ctx.enter_context(nc.psum_tensor("a_ot", [P, CHUNK], F32))
        tr = ctx.enter_context(nc.psum_tensor("a_tr", [P, TPC, GH, VW], F32))

        consts = tally("consts").sem
        ones_set = tally("ones_set").sem
        gate_set = tally("gate_set").sem
        loaded = [tally(f"loaded{u}", 16 * (2 * NSTACK + 1)) for u in range(NSLOT)]
        m_stored = [tally(f"m_stored{c}", 16 * GH, 1) for c in range(CPB)]
        o_stored = [tally(f"o_stored{c}", 16 * CPB // 2, 1) for c in range(2)]
        st_done = tally("st_done", 2 * STEPS)
        exp_done = tally("exp_done", 2 * STEPS, 1)
        masked = tally("masked", 2 * TPC * CPB, 1)
        pv_done = tally("pv_done", STEPS, 1)
        mm_done = tally("mm_done", UNITS)
        mm_used = tally("mm_used", UNITS, 1)
        negm_ready = tally("negm_ready", CPB, 1)
        nt_done = tally("nt_done", CPB, 1)
        ntb_ready = tally("ntb_ready", CPB, 1)
        os_ready = tally("os_ready", CPB, 1)
        otr_done = tally("otr_done", CPB, 1)
        rden_ready = tally("rden_ready", CPB)
        otok_ready = tally("otok_ready", CPB, 1)
        block = ctx.enter_context(nc.Block())

        parts_v = qk_d.rearrange("s o (h d) (b n) -> s d (o h) b n", d=A_HD, n=SEQ)
        v_v = v_d.rearrange("(b t p) (g w) -> p b g t w", p=P, b=BATCH, g=NGROUP)
        o_v = o_d.rearrange("(b c t p) (g w) -> p b g c t w", p=P, t=TPC, b=BATCH, g=NGROUP)

        def body(step, unit, chunk_maxima, row_out, out, main, mx_):
            s = n = 0
            for c in range(CPB):
                for kt in range(TPC * (c + 1)):
                    for piece in range(TPC):
                        if main:
                            step(c, kt, s, piece)
                        if mx_:
                            task, kc = divmod(n - TASKS * c * (c + 1) // 2, c + 1)
                            unit(c, task, kc, n)
                            n += 1
                    if mx_ and kt == TPC * (c + 1) - 1:
                        chunk_maxima(c, n)
                    if kt == 1 and c and mx_:
                        row_out(c - 1)
                    if kt == 2 and c and main:
                        out(c - 1)
                    s += 1
            if mx_:
                row_out(CPB - 1)
            if main:
                out(CPB - 1)

        def groups(eng, run, last_looped=NG - 1):
            run(-1, NSLOT - 1, -1, False, True)
            rounds = last_looped // NSLOT
            with eng.Fori(0, rounds) as i:
                for u in range(NSLOT):
                    run(i * NSLOT + u, u, i, True, True)
            for g in range(rounds * NSLOT, NG):
                run(g, g % NSLOT, g // NSLOT, True, g < NG - 1)

        def following(u, r):
            return (u + 1) % NSLOT, r + (u + 1) // NSLOT

        def first_column(c, kt):
            return max(0, kt - TPC * c) * P

        @block.sync
        def _(sp):
            sp.dma_start(ident[:, :], ident_d).then_inc(consts, 16)
            sp.dma_start(maskf[:, :], mask_d).then_inc(consts, 16)
            for t in m_stored + o_stored:
                t.open(sp)

            def load(g, u):
                b, hg = g // NGROUP, g % NGROUP
                sp.dma_start(vt[:, u], v_v[:, b, hg]).then_inc(loaded[u].sem, 16)
                for dst, pick, o in ((qs, STACK_Q, 0), (ks, STACK_K, A_HEADS)):
                    for j, s in enumerate(pick):
                        src = parts_v[s, :, :, b][:, bass.ds(hg * GH + o, GH)]
                        sp.dma_start(dst[j * A_HD:(j + 1) * A_HD, u], src).then_inc(loaded[u].sem, 16)

            load(0, 0)
            load(1, 1)

            def run(g, u, r, main, mx_):
                if main and (not isinstance(g, int) or g + 2 < NG):
                    sp.wait_ge(pv_done.sem, pv_done.at(g - 1))
                    load(g + 2, (u + 2) % NSLOT)
                v, _ = following(u, r)

                def row_out(c):
                    sp.wait_ge(ntb_ready.sem, ntb_ready.at(g + 1, c + 1))
                    for j in range(GH):
                        sp.dma_start(qs[SROWS:SROWS + 1, v, j, c * CHUNK:(c + 1) * CHUNK],
                                     ntb[j * TPC:(j + 1) * TPC, c])\
                          .then_inc(m_stored[c].sem, 16)

                def out(c):
                    sp.wait_ge(otok_ready.sem, otok_ready.at(g, c + 1))
                    sp.dma_start(o_v[:, g // NGROUP, g % NGROUP, c],
                                 otok[:, c % 2].rearrange("p t h d -> p t (h d)"))\
                      .then_inc(o_stored[c % 2].sem, 16)

                none = lambda *a: None
                body(none, none, none, row_out, out, main, mx_)

            groups(sp, run, NG - 2)
            for t in o_stored:
                sp.wait_ge(t.sem, t.at(NG - 1))

        @block.gpsimd
        def _(pool):
            pool.memset(gate[:, :], 0.0).then_inc(gate_set, 1)
            pool.wait_ge(gate_set, 1)
            masked.open(pool)

            def run(g, u, r, main, mx_):
                def step(c, kt, s, piece):
                    if piece or kt < TPC * c:
                        return
                    q0 = first_column(c, kt)
                    for h in range(2):
                        pool.wait_ge(masked.sem, masked.at(g, 2 * kt + h))
                        tile = pt[:, (STEPS * u + s) % NPT, 2 * h:2 * h + 2, q0:q0 + P]
                        pool.wait_ge(exp_done.sem, exp_done.at(g, 2 * s + h + 1))
                        pool.tensor_tensor(out=gate[:, 1:2], in0=gate[:, 0:1], in1=gate[:, 0:1], op=ALU.add)
                        pool.affine_select(out=tile, in_=tile, compare_op=ALU.is_ge, fill=0.0, base=0,
                                           pattern=[[0, 2], [1, P]], channel_multiplier=-1)\
                            .then_inc(masked.sem, 1)

                none = lambda *a: None
                body(step, none, none, none, none, main, mx_)

            groups(pool, run)

        @block.scalar
        def _(act):
            for t in (exp_done, os_ready, ntb_ready):
                t.open(act)

            def run(g, u, r, main, mx_):
                def step(c, kt, s, piece):
                    if piece:
                        return
                    q0 = first_column(c, kt)
                    act.wait_ge(pv_done.sem, pv_done.at(g, s - NPT + 1))
                    for h in range(2):
                        act.wait_ge(st_done.sem, st_done.at(g, 2 * s + h + 1))
                        act.activation(pt[:, (STEPS * u + s) % NPT, 2 * h:2 * h + 2, q0:CHUNK],
                                       st[:, 2 * h:2 * h + 2, q0:CHUNK], ACT.Exp).then_inc(exp_done.sem, 1)
                    if kt == 0 and c:
                        raw_out(c - 1, s)

                def raw_out(c, s):
                    act.wait_ge(pv_done.sem, pv_done.at(g, s))
                    act.wait_ge(otr_done.sem, otr_done.at(g, c))
                    act.activation(os_[:, :], ot[:, :], ACT.Copy).then_inc(os_ready.sem, 1)

                def row_out(c):
                    act.wait_ge(nt_done.sem, nt_done.at(g + 1, c + 1))
                    act.wait_ge(m_stored[c].sem, m_stored[c].at(g))
                    act.activation(ntb[:, c], tr[0:TASKS, 0], ACT.Copy).then_inc(ntb_ready.sem, 1)

                none = lambda *a: None
                body(step, none, none, row_out, none, main, mx_)
                if main:
                    raw_out(CPB - 1, STEPS)

            groups(act, run)

        @block.vector
        def _(dve):
            two_ones = float(np.array([0x3F803F80], np.uint32).view(np.float32)[0])
            dve.memset(ks[SROWS:SROWS + 1, :, :, :].bitcast(F32), two_ones).then_inc(ones_set, 1)
            dve.wait_ge(consts, 32)
            dve.tensor_copy(identb[:, :], ident[:, :]).then_inc(ones_set, 1)
            dve.tensor_copy(mask[:, :], maskf[:, :]).then_inc(ones_set, 1)
            for t in (mm_used, negm_ready, otok_ready):
                t.open(dve)

            def run(g, u, r, main, mx_):
                def unit(c, task, kc, n):
                    w = CHUNK if kc < c else (task % TPC + 1) * P
                    scores = mm_[:, n % 2, 0:w]
                    dve.wait_ge(mm_done.sem, mm_done.at(g + 1, n + 1))
                    dve.tensor_reduce(mx[:, task, kc:kc + 1], scores, AX.X, ALU.max)\
                       .then_inc(mm_used.sem, 1)

                def chunk_maxima(c, n):
                    dve.wait_ge(mm_used.sem, mm_used.at(g + 1, n))
                    dve.wait_ge(nt_done.sem, nt_done.at(g + 1, c - 1))
                    dve.tensor_reduce(negm[:, c % 2], mx[:, :, 0:c + 1], AX.X, ALU.max, negate=True)\
                       .then_inc(negm_ready.sem, 1)
                    dve.wait_ge(negm_ready.sem, negm_ready.at(g + 1, c + 1))

                def out(c):
                    dve.wait_ge(otr_done.sem, otr_done.at(g, c + 1))
                    dve.reciprocal(rden[:, :, :], tr[:, :, :, A_HD]).then_inc(rden_ready.sem, 1)
                    dve.wait_ge(rden_ready.sem, rden_ready.at(g, c + 1))
                    dve.wait_ge(o_stored[c % 2].sem, o_stored[c % 2].at(g, 16 * (c // 2)))
                    dve.tensor_tensor(out=otok[:, c % 2].rearrange("p t h d -> p (t h) d"),
                                      in0=tr[:, :, :, 0:A_HD].rearrange("p t h d -> p (t h) d"),
                                      in1=rden[:, :, :].rearrange("p t h -> p (t h)").unsqueeze(2)
                                      .broadcast_to([P, TPC * GH, A_HD]),
                                      op=ALU.mult).then_inc(otok_ready.sem, 1)

                body(lambda *a: None, unit, chunk_maxima, lambda c: None, out, main, mx_)

            groups(dve, run)

        @block.tensor
        def _(pe):
            pe.wait_ge(consts, 32)
            pe.wait_ge(ones_set, 3)
            for t in (pv_done, nt_done, otr_done):
                t.open(pe)

            def run(g, u, r, main, mx_):
                v, rv = following(u, r)
                steps = [(c, kt) for c in range(CPB) for kt in range(TPC * (c + 1))]

                def weigh(s):
                    c, kt = steps[s]
                    q0 = first_column(c, kt)
                    if kt == 0:
                        pe.wait_ge(os_ready.sem, os_ready.at(g, c))
                    if kt >= TPC * c:
                        pe.wait_ge(masked.sem, masked.at(g, 2 * kt + 2))
                    else:
                        pe.wait_ge(exp_done.sem, exp_done.at(g, 2 * s + 2))
                    for j in range(GH):
                        mm = pe.matmul(ot[j * VW:(j + 1) * VW, q0:CHUNK],
                                       vt[:, u, kt, j * VW:(j + 1) * VW],
                                       pt[:, (STEPS * u + s) % NPT, j, q0:CHUNK],
                                       start=kt == 0, stop=kt == TPC * (c + 1) - 1)
                    mm.then_inc(pv_done.sem, 1)

                def step(c, kt, s, piece):
                    q0 = first_column(c, kt)
                    if kt == 0 and piece == 0:
                        pe.wait_ge(m_stored[c].sem, m_stored[c].at(g))
                    if piece < 2:
                        pe.wait_ge(exp_done.sem, exp_done.at(g, 2 * s + piece - 1))
                        for j in (2 * piece, 2 * piece + 1):
                            mm = pe.matmul(st[:, j, q0:CHUNK], ks[0:SROWS + 1, u, j, kt * P:(kt + 1) * P],
                                           qs[0:SROWS + 1, u, j, c * CHUNK + q0:(c + 1) * CHUNK],
                                           start=True, stop=True)
                        mm.then_inc(st_done.sem, 1)
                    if piece == 3 and s:
                        weigh(s - 1)

                def unit(c, task, kc, n):
                    j, t = divmod(task, TPC)
                    q0, w = c * CHUNK + t * P, CHUNK if kc < c else (t + 1) * P
                    pe.wait_ge(mm_used.sem, mm_used.at(g + 1, n - 1))
                    mm = pe.matmul(mm_[:, n % 2, 0:w], qs[0:SROWS, v, j, q0:q0 + P],
                              ks[0:SROWS, v, j, kc * CHUNK:kc * CHUNK + w],
                              start=True, stop=kc < c)
                    if kc == c:
                        mm = pe.matmul(mm_[:, n % 2, w - P:w], identb[:, :], mask[:, :],
                                       start=False, stop=True)
                    mm.then_inc(mm_done.sem, 1)

                def row_out(c):
                    pe.wait_ge(negm_ready.sem, negm_ready.at(g + 1, c + 1))
                    pe.wait_ge(ntb_ready.sem, ntb_ready.at(g + 1, c))
                    if main:
                        pe.wait_ge(otok_ready.sem, otok_ready.at(g, c))
                    pe.transpose(tr[0:TASKS, 0].rearrange("p h w -> p (h w)"), negm[:, c % 2],
                                 ident[:, :]).then_inc(nt_done.sem, 1)

                def out(c):
                    if c == CPB - 1:
                        weigh(STEPS - 1)
                    pe.wait_ge(os_ready.sem, os_ready.at(g, c + 1))
                    if mx_:
                        pe.wait_ge(ntb_ready.sem, ntb_ready.at(g + 1, c + 1))
                    else:
                        pe.wait_ge(otok_ready.sem, otok_ready.at(g, c))
                    for t in range(TPC):
                        mm = pe.transpose(tr[:, t].rearrange("p h w -> p (h w)"),
                                          os_[:, t * P:(t + 1) * P], ident[:, :])
                    mm.then_inc(otr_done.sem, 1)

                if mx_:
                    pe.wait_ge(loaded[v].sem, loaded[v].per * (rv + 1))
                body(step, unit, lambda c, n: None, row_out, out, main, mx_)

            groups(pe, run)


def layers(nc, x_d, wqkv_d, wo_d, w1_d, w2_d, b1_d, b2_d, lng_d, lnb_d, scales_d, rotary_d, wmask_d,
           ident_d):
    with ExitStack() as ctx:
        def sb(name, shape, dt=F32):
            return ctx.enter_context(nc.sbuf_tensor("l_" + name, shape, dt))

        def tally(name, per=1, spare=0):
            return Tally(ctx.enter_context(nc.semaphore("l_" + name)), per, spare)

        TILES = SEQ // P
        PAIRS = HEADS // 2
        UNITS = TILES * PAIRS
        HT = INNER // P
        RING = 4

        ident = sb("ident", [P, P])
        mean_mat = sb("mean_mat", [P, P])
        half = sb("half", [P, 2 * HEADS])
        gate = sb("gate", [P, 2])
        wmask = sb("wmask", [P, 2, 2 * P])
        wqkv_hi = sb("wqkv_hi", [P, KT, 3 * INNER], F32R)
        wqkv_lo = sb("wqkv_lo", [P, KT, 3 * INNER], F32R)
        wo_hi = sb("wo_hi", [P, HT, DIM], F32R)
        wo_lo = sb("wo_lo", [P, HT, DIM], F32R)
        w1_hi = sb("w1_hi", [P, KT, 2 * MT * MW], F32R)
        w1_lo = sb("w1_lo", [P, KT, 2 * MT * MW], F32R)
        w2_hi = sb("w2_hi", [MW, MT, DIM], F32R)
        w2_lo = sb("w2_lo", [MW, MT, DIM], F32R)
        rot = sb("rot", [P, TILES, 4, HD])
        scales = sb("scales", [P, 4 * HD])
        b1 = sb("b1", [MW, 2 * MT])
        b1raw = sb("b1raw", [MW, 2 * MT])
        b2 = sb("b2", [P, KT])
        lng = sb("lng", [P, KT])
        lnb = sb("lnb", [P, KT])
        xt = sb("xt", [P, 2, KT, 1 + CHUNK])
        h_hi = sb("h_hi", [P, KT, CHUNK], F32R)
        h_lo = sb("h_lo", [P, KT, CHUNK], F32R)
        work = sb("work", [P, 3, 2 * HEADS, HD])
        sq, qn, rt = work[:, 0], work[:, 1], work[:, 2]
        stage = work[:, :, :, :].rearrange("p a h d -> p (a h d)")
        ss = sb("ss", [P, 2 * HEADS])
        ssm = sb("ssm", [P, 2 * HEADS])
        rn = sb("rn", [P, 2 * HEADS])
        qh = sb("qh", [P, 2, HEADS, P], F32R)
        ql = sb("ql", [P, 2, HEADS, P], F32R)
        kh = sb("kh", [P, PAIRS, RING, P], F32R)
        kl = sb("kl", [P, PAIRS, RING, P], F32R)
        vr = sb("vr", [P, RING, INNER])
        pr = sb("pr", [P, 4, 2, 2 * P])
        negm = sb("negm", [P, 4, 2])
        den = sb("den", [P, 4, 2])
        rden = sb("rden", [P, 4, 2])
        pts = sb("pts", [P, 2, 4, P])
        o_hi = sb("o_hi", [P, HT, CHUNK], F32R)
        o_lo = sb("o_lo", [P, HT, CHUNK], F32R)
        u_hi, u_lo = o_hi[:, 0:2], o_lo[:, 0:2]
        x1 = sb("x1", [P, 2, KT, 1 + CHUNK])
        dx = sb("dx", [P, KT, CHUNK])
        gl = sb("gl", [P, 2, CHUNK])
        var = sb("var", [P, TPC])
        rstd = sb("rstd", [P, TPC])
        n_hi = sb("n_hi", [P, KT, CHUNK], F32R)
        n_lo = sb("n_lo", [P, KT, CHUNK], F32R)

        banks = ctx.enter_context(nc.psum_tensor("l_banks", [P, 8, CHUNK], F32))
        qkp, vp, xp = banks[:, 0:2], banks[:, 2], banks[:, 3:5]
        sp_, ptp, otp = banks[:, 5], banks[:, 6], banks[:, 7]
        wop, meanp, varp, w2p = banks[:, 5:7], banks[:, 7], banks[:, 2, 0:TPC], banks[:, 3:5]
        ag = [(banks[:, 5], banks[:, 6]), (banks[:, 7], banks[:, 2])]

        consts = tally("consts", 48).sem
        init = tally("init").sem
        staged = tally("staged", 16 * 10)
        split = tally("split", 11)
        folded = tally("folded")
        fold_done = tally("fold_done")
        x_loaded = [tally(f"x_loaded{u}", 16 * CPB // 2) for u in range(2)]
        x_stored = tally("x_stored", 16 * CPB, 1)
        names = dict(
            h_hi_ready=CPB, h_ready=CPB, qk_done=TILES, v_done=TILES, sq_ready=TILES, sum_ready=TILES,
            ssm_ready=TILES, rn_ready=TILES, qn_ready=TILES, rt_ready=TILES, cos_ready=TILES,
            r_ready=TILES, v_ready=TILES, xq_done=TILES, xk_done=TILES, qh_ready=TILES,
            ql_ready=TILES, kh_ready=TILES, k_ready=TILES, s_done=UNITS, sm_ready=UNITS,
            exp_done=UNITS, rden_ready=UNITS, p_ready=UNITS, pt_done=UNITS, pts_ready=UNITS,
            pv_done=UNITS, oh_ready=TILES, ol_ready=TILES, wo_done=CPB, x1_ready=CPB, mean_done=CPB,
            dx_ready=CPB, sq2_ready=CPB, var_done=CPB, var_ready=CPB, rstd_ready=CPB, bc_done=CPB,
            nx_ready=CPB, n_hi_ready=CPB, n_ready=CPB, ag_done=CPB * MT, gelu_ready=CPB * MT,
            u_ready=CPB * MT, u_hi_ready=CPB * MT, u_lo_ready=CPB * MT, w2m_done=CPB * MT,
            x2_ready=CPB)
        S = {n: tally(n, per, 1) for n, per in names.items()}
        block = ctx.enter_context(nc.Block())

        x_v = x_d.rearrange("l k p (b n) -> p l b k n", n=SEQ)

        def key_tiles(T):
            if T == 0:
                return [0], slice(0, 1), wmask[:, 0, P:2 * P]
            if T % RING:
                return [T % RING - 1, T % RING], slice(T % RING - 1, T % RING + 1), wmask[:, 0]
            return [0, RING - 1], slice(0, RING, RING - 1), wmask[:, 1]

        def sequence(do):
            for T in range(-2, TILES):
                c, t = divmod(T, TPC)
                if (T + 2) % TPC == 0 and T + 2 < TILES:
                    do("load", (T + 2) // TPC)
                for p in range(PAIRS):
                    i = T * PAIRS + p
                    if T >= 0:
                        do("scores", i)
                        if t or p:
                            do("norm", i - 1)
                    if p == 0 and T + 2 < TILES:
                        do("project_qk", T + 2)
                    if p == 1 and 0 <= T + 1 < TILES:
                        do("turn_q", T + 1)
                    if p == 2 and T + 2 < TILES:
                        do("project_v", T + 2)
                        do("rotate", T + 2)
                    if p == 3 and 0 <= T + 1 < TILES:
                        do("turn_k", T + 1)
                    if T >= 0:
                        if i - 2 >= c * TPC * PAIRS:
                            do("turn_p", i - 2)
                        if i - 3 >= c * TPC * PAIRS:
                            do("weigh", i - 3)
                            if (i - 3) % PAIRS == PAIRS - 1:
                                do("part_o", (i - 3) // PAIRS)
                if T + 2 < TILES:
                    do("keep_v", T + 2)
                if T >= 0 and t == TPC - 1:
                    i = (T + 1) * PAIRS
                    do("norm", i - 1)
                    do("turn_p", i - 2)
                    do("weigh", i - 3)
                    do("turn_p", i - 1)
                    do("weigh", i - 2)
                    do("weigh", i - 1)
                    do("part_o", T)
                    do("network", c)

        def program(eng, prepare_layer, events):
            with eng.Fori(0, DEPTH) as l:
                prepare_layer(l)
                with eng.Fori(0, BATCH) as b:
                    B = l * BATCH + b

                    def do(event, n):
                        if event in events:
                            events[event](B, l, b, n)

                    sequence(do)

        def wait(eng, name, B, k):
            eng.wait_ge(S[name].sem, S[name].at(B, k))

        @block.sync
        def _(sp):
            sp.dma_start(ident[:, :], ident_d).then_inc(consts, 16)
            sp.dma_start(wmask[:, :, :], wmask_d).then_inc(consts, 16)
            x_stored.open(sp)

            def prepare_layer(l):
                def get(dst, src):
                    sp.dma_start(dst, src).then_inc(staged.sem, 16)

                sp.wait_ge(x_stored.sem, x_stored.at(l * BATCH - 1))
                get(stage[:, 0:KT * 3 * INNER].rearrange("p (k n) -> p k n", k=KT),
                    wqkv_d[:, l].rearrange("(k p) n -> p k n", p=P))
                get(rot[:, :, :, :].rearrange("p t a d -> p t (a d)"),
                    rotary_d.rearrange("(t p) n -> p t n", p=P))
                get(scales[:, :], scales_d[l].partition_broadcast(P))
                get(b1raw[:, :], b1_d[:, l])
                get(b2[:, :], b2_d[:, l])
                get(lng[:, :], lng_d[:, l])
                get(lnb[:, :], lnb_d[:, l])
                sp.wait_ge(split.sem, split.at(l, 3))
                get(stage[:, 0:KT * 2 * MT * MW].rearrange("p (k n) -> p k n", k=KT),
                    w1_d[:, l].rearrange("(k p) n -> p k n", p=P))
                sp.wait_ge(split.sem, split.at(l, 7))
                get(stage[:, 0:HT * DIM].rearrange("p (k n) -> p k n", k=HT),
                    wo_d[:, l].rearrange("(k p) n -> p k n", p=P))
                get(stage[0:MW, HT * DIM:(HT + MT) * DIM].rearrange("p (k n) -> p k n", k=MT),
                    w2_d[:, l].rearrange("(k p) n -> p k n", p=MW))

            def load(B, l, b, c):
                wait(sp, "x1_ready", B, c - 1)
                first = 0 if c else 1
                sp.dma_start(xt[:, c % 2, :, first:], x_v[:, l, b, :, c * CHUNK - 1 + first:(c + 1) * CHUNK])\
                  .then_inc(x_loaded[c % 2].sem, 16)

            def network(B, l, b, c):
                wait(sp, "x2_ready", B, c + 1)
                sp.dma_start(x_v[:, l + 1, b, :, c * CHUNK:(c + 1) * CHUNK], dx[:, :, :])\
                  .then_inc(x_stored.sem, 16)

            program(sp, prepare_layer, dict(load=load, network=network))
            sp.wait_ge(x_stored.sem, x_stored.at(DEPTH * BATCH - 1))

        @block.gpsimd
        def _(pool):
            pool.memset(half[:, :], -0.5).then_inc(init, 1)
            pool.memset(mean_mat[:, :], 1.0 / DIM).then_inc(init, 1)
            pool.memset(qh[:, :, :, :].bitcast(F32), 0.0).then_inc(init, 1)
            pool.memset(ql[:, :, :, :].bitcast(F32), 0.0).then_inc(init, 1)
            pool.wait_ge(init, 5)
            for n in ("h_ready", "rn_ready", "cos_ready", "r_ready", "p_ready", "rstd_ready", "n_ready",
                      "u_lo_ready"):
                S[n].open(pool)

            def prepare_layer(l):
                pass

            def load(B, l, b, c):
                wait(pool, "h_hi_ready", B, c + 1)
                pool.tensor_tensor(out=h_lo[:, 0], in0=xt[:, c % 2, 0, 1:], in1=h_hi[:, 0].bitcast(F32),
                                   op=ALU.subtract)
                if c == 0:
                    pool.memset(h_lo[:, 1, 0:1].bitcast(F32), 0.0)
                f = 0 if c else 1
                pool.tensor_tensor(out=h_lo[:, 1, f:], in0=xt[:, c % 2, 1, f:CHUNK],
                                   in1=h_hi[:, 1, f:].bitcast(F32), op=ALU.subtract)\
                    .then_inc(S["h_ready"].sem, 1)

            def project_qk(B, l, b, T):
                wait(pool, "ssm_ready", B, T + 1)
                pool.tensor_tensor(out=rn[:, :], in0=ssm[:, :], in1=half[:, :], op=ALU.pow)\
                    .then_inc(S["rn_ready"].sem, 1)

            def rotate(B, l, b, T):
                wait(pool, "rt_ready", B, T + 1)
                cos = rot[:, T, 0:2].unsqueeze(2).broadcast_to([P, 2, HEADS, HD])
                pool.tensor_tensor(out=qn.rearrange("p (a h) d -> p a h d", a=2),
                                   in0=qn.rearrange("p (a h) d -> p a h d", a=2), in1=cos,
                                   op=ALU.mult).then_inc(S["cos_ready"].sem, 1)
                wait(pool, "cos_ready", B, T + 1)
                pool.tensor_tensor(out=rt, in0=rt, in1=qn, op=ALU.add).then_inc(S["r_ready"].sem, 1)

            def norm(B, l, b, i):
                n = len(key_tiles(i // PAIRS)[0]) * P
                wait(pool, "rden_ready", B, i + 1)
                pool.tensor_tensor(out=pr[:, i % 4, :, 0:n], in0=pr[:, i % 4, :, 0:n],
                                   in1=rden[:, i % 4].unsqueeze(2).broadcast_to([P, 2, n]),
                                   op=ALU.mult).then_inc(S["p_ready"].sem, 1)

            def network(B, l, b, c):
                wait(pool, "var_ready", B, c + 1)
                pool.tensor_tensor(out=rstd[:, :], in0=var[:, :], in1=half[:, 0:TPC], op=ALU.pow)\
                    .then_inc(S["rstd_ready"].sem, 1)
                wait(pool, "n_hi_ready", B, c + 1)
                pool.tensor_tensor(out=n_lo[:, :, :], in0=dx[:, :, :], in1=n_hi[:, :, :].bitcast(F32),
                                   op=ALU.subtract).then_inc(S["n_ready"].sem, 1)
                for m in range(MT):
                    k = c * MT + m
                    wait(pool, "u_hi_ready", B, k + 1)
                    pool.tensor_tensor(out=u_lo[0:MW, k % 2], in0=gl[0:MW, k % 2],
                                       in1=u_hi[0:MW, k % 2].bitcast(F32), op=ALU.subtract)\
                        .then_inc(S["u_lo_ready"].sem, 1)

            program(pool, prepare_layer, dict(load=load, project_qk=project_qk, rotate=rotate,
                                              norm=norm, network=network))

        @block.scalar
        def _(act):
            for n in ("h_hi_ready", "sq_ready", "v_ready", "qh_ready", "kh_ready", "exp_done", "pts_ready",
                      "oh_ready", "sq2_ready", "n_hi_ready", "gelu_ready", "u_hi_ready"):
                S[n].open(act)

            def load(B, l, b, c):
                act.wait_ge(x_loaded[c % 2].sem, x_loaded[c % 2].at(B, 16 * (c // 2 + 1)))
                wait(act, "qk_done", B, c * TPC)
                wait(act, "v_done", B, c * TPC)
                f = 0 if c else 1
                if c == 0:
                    act.activation(h_hi[:, 1, 0:1], gate[:, 0:1], ACT.Copy)
                act.activation(h_hi[:, 0], xt[:, c % 2, 0, 1:], ACT.Copy)
                act.activation(h_hi[:, 1, f:], xt[:, c % 2, 1, f:CHUNK], ACT.Copy)\
                   .then_inc(S["h_hi_ready"].sem, 1)

            def project_qk(B, l, b, T):
                wait(act, "sum_ready", B, T)
                wait(act, "qk_done", B, T + 1)
                act.activation(sq.rearrange("p h d -> p (h d)"), qkp.rearrange("p a n -> p (a n)"),
                               ACT.Square).then_inc(S["sq_ready"].sem, 1)

            def keep_v(B, l, b, T):
                wait(act, "v_done", B, T + 1)
                wait(act, "pv_done", B, (T - RING + 2) * PAIRS)
                act.activation(vr[:, T % RING], vp, ACT.Copy).then_inc(S["v_ready"].sem, 1)

            def turn_q(B, l, b, T):
                wait(act, "xq_done", B, T + 1)
                for h, half_ in enumerate((slice(0, HD), slice(HD, P))):
                    q = act.activation(qh[half_, T % 2, h::2], xp[half_, 0].rearrange("p (a n) -> p a n", n=P),
                                       ACT.Copy)
                q.then_inc(S["qh_ready"].sem, 1)

            def turn_k(B, l, b, T):
                wait(act, "xk_done", B, T + 1)
                act.activation(kh[:, :, T % RING], xp[:, 1].rearrange("p (a n) -> p a n", n=P), ACT.Copy)\
                   .then_inc(S["kh_ready"].sem, 1)

            def scores(B, l, b, i):
                n = len(key_tiles(i // PAIRS)[0]) * P
                wait(act, "sm_ready", B, i + 1)
                for h in range(2):
                    e = act.activation(pr[:, i % 4, h, 0:n], pr[:, i % 4, h, 0:n], ACT.Exp, scale=-1.0,
                                       bias=negm[:, i % 4, h:h + 1], accum_out=den[:, i % 4, h:h + 1])
                e.then_inc(S["exp_done"].sem, 1)

            def turn_p(B, l, b, i):
                n = 2 * len(key_tiles(i // PAIRS)[0])
                wait(act, "pv_done", B, i - 1)
                wait(act, "pt_done", B, i + 1)
                act.activation(pts[:, i % 2, 0:n].rearrange("p a n -> p (a n)"), ptp[:, 0:n * P], ACT.Copy)\
                   .then_inc(S["pts_ready"].sem, 1)

            def part_o(B, l, b, T):
                t = T % TPC
                wait(act, "pv_done", B, (T + 1) * PAIRS)
                act.activation(o_hi[:, :, t * P:(t + 1) * P], otp.rearrange("p (a n) -> p a n", n=P), ACT.Copy)\
                   .then_inc(S["oh_ready"].sem, 1)

            def network(B, l, b, c):
                wait(act, "dx_ready", B, c + 1)
                act.activation(gl[:, :, :], dx[:, :, :], ACT.Square).then_inc(S["sq2_ready"].sem, 1)
                wait(act, "nx_ready", B, c + 1)
                act.activation(n_hi[:, :, :], dx[:, :, :], ACT.Copy).then_inc(S["n_hi_ready"].sem, 1)
                for m in range(MT + 1):
                    k = c * MT + m
                    if m < MT:
                        wait(act, "u_lo_ready", B, k - 1)
                        wait(act, "ag_done", B, k + 1)
                        act.activation(gl[0:MW, k % 2], ag[k % 2][1][0:MW], ACT.Gelu,
                                       bias=b1[:, MT + m:MT + m + 1]).then_inc(S["gelu_ready"].sem, 1)
                    if m:
                        k -= 1
                        wait(act, "w2m_done", B, k - 1)
                        wait(act, "u_ready", B, k + 1)
                        act.activation(u_hi[0:MW, k % 2], gl[0:MW, k % 2], ACT.Copy)\
                           .then_inc(S["u_hi_ready"].sem, 1)

            act.wait_ge(init, 5)
            program(act, lambda l: act.wait_ge(split.sem, split.at(l)), dict(
                load=load, project_qk=project_qk, keep_v=keep_v, turn_q=turn_q, turn_k=turn_k,
                scores=scores, turn_p=turn_p, part_o=part_o, network=network))

        @block.vector
        def _(dve):
            dve.memset(gate[:, :], 0.0).then_inc(init, 1)
            dve.wait_ge(init, 5)
            dve.wait_ge(consts, 32)
            for n in ("sum_ready", "ssm_ready", "qn_ready", "rt_ready", "ql_ready", "k_ready", "sm_ready",
                      "rden_ready", "ol_ready", "x1_ready", "dx_ready", "var_ready", "nx_ready",
                      "u_ready", "x2_ready"):
                S[n].open(dve)

            def prepare_layer(l):
                def parts(hi, lo, raw, k):
                    dve.tensor_copy(hi, raw).then_inc(split.sem, 1)
                    dve.wait_ge(split.sem, split.at(l, k + 1))
                    dve.tensor_tensor(out=lo, in0=raw, in1=hi.bitcast(F32), op=ALU.subtract)\
                       .then_inc(split.sem, 1)
                    if k + 2 < split.per:
                        dve.wait_ge(split.sem, split.at(l, k + 2))

                dve.wait_ge(staged.sem, staged.at(l, 7 * 16))
                parts(wqkv_hi[:, :, :], wqkv_lo[:, :, :],
                      stage[:, 0:KT * 3 * INNER].rearrange("p (k n) -> p k n", k=KT), 0)
                dve.tensor_tensor(out=rot[:, :, :, :].rearrange("p t a d -> p t (a d)"),
                                  in0=rot[:, :, :, :].rearrange("p t a d -> p t (a d)"),
                                  in1=scales[:, :].unsqueeze(1).broadcast_to([P, TILES, 4 * HD]),
                                  op=ALU.mult).then_inc(split.sem, 1)
                w1s = stage[:, 0:KT * 2 * MT * MW].rearrange("p (k n) -> p k n", k=KT)
                dve.wait_ge(fold_done.sem, fold_done.at(l))
                dve.tensor_tensor(out=b1[:, :], in0=banks[0:MW, 0, 0:2 * MT], in1=b1raw[:, :], op=ALU.add)\
                   .then_inc(split.sem, 1)
                for k in range(KT):
                    f = dve.tensor_scalar(w1s[:, k], w1s[:, k], lng[:, k:k + 1], None, ALU.mult)
                f.then_inc(folded.sem, 1)
                dve.wait_ge(folded.sem, folded.at(l))
                parts(w1_hi[:, :, :], w1_lo[:, :, :], w1s, 4)
                dve.tensor_copy(gate[:, 1:2], gate[:, 0:1]).then_inc(split.sem, 1)
                dve.wait_ge(staged.sem, staged.at(l, 10 * 16))
                parts(wo_hi[:, :, :], wo_lo[:, :, :],
                      stage[:, 0:HT * DIM].rearrange("p (k n) -> p k n", k=HT), 7)
                parts(w2_hi[:, :, :], w2_lo[:, :, :],
                      stage[0:MW, HT * DIM:(HT + MT) * DIM].rearrange("p (k n) -> p k n", k=MT), 9)

            def project_qk(B, l, b, T):
                wait(dve, "sq_ready", B, T + 1)
                dve.tensor_reduce(ss[:, :], sq, AX.X, ALU.add).then_inc(S["sum_ready"].sem, 1)
                wait(dve, "sum_ready", B, T + 1)
                dve.tensor_scalar(ssm[:, :], ss[:, :], 1e-24, None, ALU.max).then_inc(S["ssm_ready"].sem, 1)

            def rotate(B, l, b, T):
                wait(dve, "r_ready", B, T)
                wait(dve, "rn_ready", B, T + 1)
                dve.tensor_tensor(out=qn, in0=qkp.rearrange("p a (h d) -> p (a h) d", d=HD),
                                  in1=rn[:, :].unsqueeze(2).broadcast_to([P, 2 * HEADS, HD]),
                                  op=ALU.mult).then_inc(S["qn_ready"].sem, 1)
                wait(dve, "xk_done", B, T)
                wait(dve, "qn_ready", B, T + 1)
                for a in range(2):
                    dst, src = slice(a * HD // 2, (a + 1) * HD // 2), slice((1 - a) * HD // 2, (2 - a) * HD // 2)
                    r = dve.tensor_tensor(
                        out=rt.rearrange("p (a h) d -> p a h d", a=2)[:, :, :, dst],
                        in0=qn.rearrange("p (a h) d -> p a h d", a=2)[:, :, :, src],
                        in1=rot[:, T, 2:4, dst].unsqueeze(2).broadcast_to([P, 2, HEADS, HD // 2]),
                        op=ALU.mult)
                r.then_inc(S["rt_ready"].sem, 1)

            def turn_q(B, l, b, T):
                wait(dve, "qh_ready", B, T + 1)
                for h, half_ in enumerate((slice(0, HD), slice(HD, P))):
                    q = dve.tensor_tensor(out=ql[half_, T % 2, h::2],
                                          in0=xp[half_, 0].rearrange("p (a n) -> p a n", n=P),
                                          in1=qh[half_, T % 2, h::2].bitcast(F32), op=ALU.subtract)
                q.then_inc(S["ql_ready"].sem, 1)

            def turn_k(B, l, b, T):
                wait(dve, "kh_ready", B, T + 1)
                dve.tensor_tensor(out=kl[:, :, T % RING], in0=xp[:, 1].rearrange("p (a n) -> p a n", n=P),
                                  in1=kh[:, :, T % RING].bitcast(F32), op=ALU.subtract)\
                   .then_inc(S["k_ready"].sem, 1)

            def scores(B, l, b, i):
                tiles, _, m = key_tiles(i // PAIRS)
                n = len(tiles) * P
                wait(dve, "pt_done", B, i - 3)
                wait(dve, "sm_ready", B, i)
                wait(dve, "s_done", B, i + 1)
                dve.tensor_copy(gate[:, 1:2], gate[:, 0:1])
                for h in range(2):
                    r = dve.tensor_tensor_reduce(pr[:, i % 4, h, 0:n], sp_[:, h * 2 * P:h * 2 * P + n], m,
                                                 -1.0, 3e38, ALU.add, ALU.min, negm[:, i % 4, h:h + 1])
                r.then_inc(S["sm_ready"].sem, 1)

            def norm(B, l, b, i):
                wait(dve, "exp_done", B, i + 1)
                dve.reciprocal(rden[:, i % 4], den[:, i % 4]).then_inc(S["rden_ready"].sem, 1)

            def part_o(B, l, b, T):
                t = T % TPC
                wait(dve, "oh_ready", B, T + 1)
                dve.tensor_tensor(out=o_lo[:, :, t * P:(t + 1) * P], in0=otp.rearrange("p (a n) -> p a n", n=P),
                                  in1=o_hi[:, :, t * P:(t + 1) * P].bitcast(F32), op=ALU.subtract)\
                   .then_inc(S["ol_ready"].sem, 1)

            def network(B, l, b, c):
                u = c % 2
                shifted = (x1[:, u, 0, 1:], x1[:, u, 1, 0:CHUNK])
                if c:
                    dve.tensor_copy(x1[:, u, 1, 0:1], x1[:, 1 - u, 1, CHUNK:])
                else:
                    dve.memset(x1[:, u, 1, 0:1], 0.0)
                wait(dve, "wo_done", B, c + 1)
                dve.tensor_tensor(out=x1[:, u, :, 1:], in0=wop, in1=xt[:, u, :, 1:], op=ALU.add)\
                   .then_inc(S["x1_ready"].sem, 1)
                dve.wait_ge(x_stored.sem, x_stored.at(B, 16 * c))
                wait(dve, "mean_done", B, c + 1)
                for k in range(KT):
                    d = dve.tensor_tensor(out=dx[:, k], in0=shifted[k], in1=meanp, op=ALU.subtract)
                d.then_inc(S["dx_ready"].sem, 1)
                wait(dve, "var_done", B, c + 1)
                dve.tensor_scalar(var[:, :], varp, EPS, None, ALU.add).then_inc(S["var_ready"].sem, 1)
                wait(dve, "bc_done", B, c + 1)
                for k in range(KT):
                    d = dve.tensor_tensor(out=dx[:, k], in0=dx[:, k], in1=meanp, op=ALU.mult)
                d.then_inc(S["nx_ready"].sem, 1)
                for m in range(MT):
                    k = c * MT + m
                    wait(dve, "gelu_ready", B, k + 1)
                    dve.scalar_tensor_tensor(out=gl[0:MW, k % 2], in0=ag[k % 2][0][0:MW],
                                             scalar=b1[:, m:m + 1], in1=gl[0:MW, k % 2],
                                             op0=ALU.add, op1=ALU.mult).then_inc(S["u_ready"].sem, 1)
                wait(dve, "w2m_done", B, (c + 1) * MT)
                wait(dve, "n_ready", B, c + 1)
                for k in range(KT):
                    d = dve.scalar_tensor_tensor(out=dx[:, k], in0=w2p[:, k], scalar=b2[:, k:k + 1],
                                                 in1=x1[:, u, k, 1:], op0=ALU.add, op1=ALU.add)
                d.then_inc(S["x2_ready"].sem, 1)

            program(dve, prepare_layer, dict(
                project_qk=project_qk, rotate=rotate, turn_q=turn_q, turn_k=turn_k, scores=scores,
                norm=norm, part_o=part_o, network=network))

        @block.tensor
        def _(pe):
            pe.wait_ge(consts, 32)
            pe.wait_ge(init, 5)
            for n in ("qk_done", "v_done", "xq_done", "xk_done", "s_done", "pt_done", "pv_done", "wo_done",
                      "mean_done", "var_done", "bc_done", "ag_done", "w2m_done"):
                S[n].open(pe)

            def products(out, steps):
                for j, (w, x_) in enumerate(steps):
                    mm = pe.matmul(out, w, x_, start=j == 0, stop=j == len(steps) - 1)
                return mm

            def three(w_hi, w_lo, x_hi_, x_lo_):
                return [(w_lo, x_hi_), (w_hi, x_lo_), (w_hi, x_hi_)]

            def prepare_layer(l):
                pe.wait_ge(staged.sem, staged.at(l, 8 * 16))
                pe.wait_ge(split.sem, split.at(l, 3))
                for m in range(2 * MT):
                    for k in range(KT):
                        o = k * 2 * MT * MW + m * MW
                        mm = pe.matmul(banks[0:MW, 0, m:m + 1], stage[:, o:o + MW], lnb[:, k:k + 1],
                                       start=k == 0, stop=k == KT - 1)
                mm.then_inc(fold_done.sem, 1)

            def project_qk(B, l, b, T):
                c, t = divmod(T, TPC)
                if T == 0:
                    pe.wait_ge(split.sem, split.at(l))
                if t == 0:
                    wait(pe, "h_ready", B, c + 1)
                wait(pe, "qn_ready", B, T)
                rows = slice(t * P, (t + 1) * P)
                for a in range(2):
                    cols = slice(a * INNER, (a + 1) * INNER)
                    mm = products(qkp[:, a], [s for k in range(KT) for s in three(
                        h_hi[:, k, rows], h_lo[:, k, rows], wqkv_hi[:, k, cols], wqkv_lo[:, k, cols])])
                mm.then_inc(S["qk_done"].sem, 1)

            def project_v(B, l, b, T):
                t = T % TPC
                rows, cols = slice(t * P, (t + 1) * P), slice(2 * INNER, 3 * INNER)
                wait(pe, "v_ready", B, T)
                if t == 2 and T > 2:
                    wait(pe, "u_ready", B, (T // TPC) * MT)
                products(vp, [s for k in range(KT) for s in three(
                    h_hi[:, k, rows], h_lo[:, k, rows], wqkv_hi[:, k, cols], wqkv_lo[:, k, cols])])\
                    .then_inc(S["v_done"].sem, 1)

            def turn(bank, first, sem):
                for p in range(PAIRS):
                    mm = pe.transpose(bank[:, p * P:(p + 1) * P],
                                      rt[:, first + 2 * p:first + 2 * p + 2].rearrange("p h d -> p (h d)"),
                                      ident[:, :])
                mm.then_inc(sem, 1)

            def turn_q(B, l, b, T):
                wait(pe, "r_ready", B, T + 1)
                wait(pe, "ql_ready", B, T)
                turn(xp[:, 0], 0, S["xq_done"].sem)

            def turn_k(B, l, b, T):
                wait(pe, "k_ready", B, T)
                turn(xp[:, 1], HEADS, S["xk_done"].sem)

            def scores(B, l, b, i):
                T, p = divmod(i, PAIRS)
                tiles, at, _ = key_tiles(T)
                n = len(tiles) * P
                if p == 0:
                    wait(pe, "k_ready", B, T + 1)
                wait(pe, "sm_ready", B, i)
                for h in range(2):
                    mm = products(sp_[:, h * 2 * P:h * 2 * P + n], three(
                        qh[:, T % 2, 2 * p + h], ql[:, T % 2, 2 * p + h], kh[:, p, at], kl[:, p, at]))
                mm.then_inc(S["s_done"].sem, 1)

            def turn_p(B, l, b, i):
                n = len(key_tiles(i // PAIRS)[0])
                wait(pe, "pts_ready", B, i)
                wait(pe, "p_ready", B, i + 1)
                for h in range(2):
                    for k in range(n):
                        mm = pe.transpose(ptp[:, (h * n + k) * P:(h * n + k + 1) * P],
                                          pr[:, i % 4, h, k * P:(k + 1) * P], ident[:, :])
                mm.then_inc(S["pt_done"].sem, 1)

            def weigh(B, l, b, i):
                T, p = divmod(i, PAIRS)
                tiles = key_tiles(T)[0]
                if p == 0:
                    wait(pe, "ol_ready", B, T)
                    wait(pe, "v_ready", B, T + 1)
                wait(pe, "pts_ready", B, i + 1)
                for k, slot in enumerate(tiles):
                    for h in range(2):
                        mm = pe.matmul(otp[h * HD:(h + 1) * HD, p * P:(p + 1) * P],
                                       vr[:, slot, (2 * p + h) * HD:(2 * p + h + 1) * HD],
                                       pts[:, i % 2, h * len(tiles) + k], start=k == 0,
                                       stop=k == len(tiles) - 1)
                mm.then_inc(S["pv_done"].sem, 1)

            def network(B, l, b, c):
                u = c % 2
                wait(pe, "ol_ready", B, (c + 1) * TPC)
                for m in range(KT):
                    cols = slice(m * P, (m + 1) * P)
                    mm = products(wop[:, m], [s for k in range(HT) for s in three(
                        wo_hi[:, k, cols], wo_lo[:, k, cols], o_hi[:, k], o_lo[:, k])])
                mm.then_inc(S["wo_done"].sem, 1)
                wait(pe, "x1_ready", B, c + 1)
                products(meanp, [(mean_mat[:, :], x1[:, u, 0, 1:]), (mean_mat[:, :], x1[:, u, 1, 0:CHUNK])])\
                    .then_inc(S["mean_done"].sem, 1)
                wait(pe, "v_ready", B, min((c + 1) * TPC + 2, TILES))
                wait(pe, "sq2_ready", B, c + 1)
                for t in range(TPC):
                    mm = products(varp[:, t:t + 1], [(gl[:, k, t * P:(t + 1) * P], mean_mat[:, 0:1])
                                                     for k in range(KT)])
                mm.then_inc(S["var_done"].sem, 1)
                wait(pe, "rstd_ready", B, c + 1)
                for t in range(TPC):
                    mm = pe.matmul(meanp[:, t * P:(t + 1) * P], rstd[:, t:t + 1].broadcast_to([P, P]),
                                   ident[:, :], start=True, stop=True)
                mm.then_inc(S["bc_done"].sem, 1)
                wait(pe, "n_ready", B, c + 1)
                wait(pe, "k_ready", B, min((c + 1) * TPC + 1, TILES))
                for m in range(MT + 1):
                    k = c * MT + m
                    if m < MT:
                        wait(pe, "u_ready", B, k - 1)
                        for half_, bank in ((0, 0), (1, 1)):
                            cols = slice((half_ * MT + m) * MW, (half_ * MT + m + 1) * MW)
                            mm = products(ag[k % 2][bank][0:MW], [s for j in range(KT) for s in three(
                                w1_hi[:, j, cols], w1_lo[:, j, cols], n_hi[:, j], n_lo[:, j])])
                        mm.then_inc(S["ag_done"].sem, 1)
                    if m:
                        k, m_ = k - 1, m - 1
                        wait(pe, "u_lo_ready", B, k + 1)
                        for o in range(KT):
                            cols = slice(o * P, (o + 1) * P)
                            steps = three(w2_hi[:, m_, cols], w2_lo[:, m_, cols],
                                          u_hi[0:MW, k % 2], u_lo[0:MW, k % 2])
                            for j, (w, x_) in enumerate(steps):
                                mm = pe.matmul(w2p[:, o], w, x_, start=m_ == 0 and j == 0,
                                               stop=m_ == MT - 1 and j == 2)
                        mm.then_inc(S["w2m_done"].sem, 1)

            program(pe, prepare_layer, dict(
                project_qk=project_qk, project_v=project_v, turn_q=turn_q, turn_k=turn_k,
                scores=scores, turn_p=turn_p, weigh=weigh, network=network))


def combine(nc, x, x2_d, o_d, wo_d, bo_d, ident_d, out):
    with ExitStack() as ctx:
        def sb(name, shape, dt=F32):
            return ctx.enter_context(nc.sbuf_tensor("c_" + name, shape, dt))

        def tally(name, per=1, spare=0):
            return Tally(ctx.enter_context(nc.semaphore("c_" + name)), per, spare)

        ident = sb("ident", [P, P])
        w_raw = sb("w_raw", [P, KT, DIM])
        w_hi = sb("w_hi", [P, KT, DIM], F32R)
        w_lo = sb("w_lo", [P, KT, DIM], F32R)
        bo = sb("bo", [P, DIM])
        o_in = sb("o_in", [P, 2, TPC, DIM])
        x2 = sb("x2", [P, 2, KT, CHUNK])
        x_in = sb("x_in", [P, 2, TPC, DIM])
        o_hi = sb("o_hi", [P, 2, KT, CHUNK], F32R)
        o_lo = sb("o_lo", [P, 2, KT, CHUNK], F32R)
        g = sb("g", [P, 2, TPC, DIM])
        y = sb("y", [P, 2, TPC, DIM])
        otp = ctx.enter_context(nc.psum_tensor("c_otp", [P, KT, CHUNK], F32))
        x2p = ctx.enter_context(nc.psum_tensor("c_x2p", [P, TPC, DIM], F32))
        sp_ = ctx.enter_context(nc.psum_tensor("c_sp", [P, TPC, DIM], F32))

        consts = tally("consts").sem
        w_split = tally("w_split").sem
        loaded = [tally(f"loaded{u}", 48) for u in range(2)]
        stored = [tally(f"stored{u}", 16, 1) for u in range(2)]
        tr_done = tally("tr_done", 1, 2)
        oh_ready = tally("oh_ready")
        ol_ready = tally("ol_ready", 1, 1)
        g_ready = tally("g_ready", 1, 1)
        s_done = tally("s_done", 1, 2)
        y1_ready = tally("y1_ready", 1, 1)
        y2_ready = tally("y2_ready")
        y_ready = tally("y_ready", 1, 2)
        block = ctx.enter_context(nc.Block())

        rows = lambda a: a.rearrange("(c t p) d -> p c t d", p=P, t=TPC)
        x_v, out_v = (a.rearrange("b (c t p) d -> p (b c) t d", p=P, t=TPC) for a in (x, out))
        o_v = rows(o_d)
        x2_v = x2_d.rearrange("k p (c n) -> p c k n", n=CHUNK)

        @block.sync
        def _(sp):
            sp.dma_start(ident[:, :], ident_d).then_inc(consts, 16)
            sp.dma_start(w_raw[:, :, :], wo_d.rearrange("(k p) n -> p k n", p=P)).then_inc(consts, 16)
            sp.dma_start(bo[:, :], bo_d.partition_broadcast(P)).then_inc(consts, 16)
            for t in stored:
                t.open(sp)

            def load(n, u):
                sp.wait_ge(tr_done.sem, tr_done.at(n - 2))
                sp.wait_ge(y_ready.sem, y_ready.at(n - 2))
                sp.dma_start(o_in[:, u], o_v[:, n]).then_inc(loaded[u].sem, 16)
                sp.dma_start(x2[:, u], x2_v[:, n]).then_inc(loaded[u].sem, 16)
                sp.dma_start(x_in[:, u], x_v[:, n]).then_inc(loaded[u].sem, 16)

            def store(n, u):
                sp.wait_ge(y_ready.sem, y_ready.at(n))
                sp.dma_start(out_v[:, n], y[:, u]).then_inc(stored[u].sem, 16)

            staggered(sp, NCHUNK, load, lambda n, u: None, store)
            for u in range(2):
                sp.wait_ge(stored[u].sem, stored[u].at_turn(NCHUNK - 2 + u, u))

        @block.scalar
        def _(act):
            g_ready.open(act)

            def first(n, u):
                act.wait_ge(tr_done.sem, tr_done.at(n))
                act.wait_ge(s_done.sem, s_done.at(n - 2))
                act.activation(o_hi[:, u], otp[:, :, :], ACT.Copy).then_inc(oh_ready.sem, 1)
                act.wait_ge(y_ready.sem, y_ready.at(n - 2))
                act.activation(g[:, u], x2p[:, :, :], ACT.Silu).then_inc(g_ready.sem, 1)

            staggered(act, NCHUNK, lambda n, u: None, first, lambda n, u: None)

        @block.vector
        def _(dve):
            dve.wait_ge(consts, 48)
            dve.tensor_copy(w_hi[:, :, :], w_raw[:, :, :]).then_inc(w_split, 1)
            dve.wait_ge(w_split, 1)
            dve.tensor_tensor(out=w_lo[:, :, :], in0=w_raw[:, :, :], in1=w_hi[:, :, :].bitcast(F32),
                              op=ALU.subtract).then_inc(w_split, 1)
            for t in (ol_ready, y1_ready, y_ready):
                t.open(dve)

            def first(n, u):
                dve.wait_ge(oh_ready.sem, oh_ready.at(n))
                dve.tensor_tensor(out=o_lo[:, u], in0=otp[:, :, :], in1=o_hi[:, u].bitcast(F32),
                                  op=ALU.subtract).then_inc(ol_ready.sem, 1)

            def second(n, u):
                dve.wait_ge(stored[u].sem, stored[u].before_turn(n, u))
                dve.wait_ge(s_done.sem, s_done.at(n))
                dve.tensor_tensor(out=y[:, u], in0=sp_[:, :, :],
                                  in1=bo[:, :].unsqueeze(1).broadcast_to([P, TPC, DIM]),
                                  op=ALU.add).then_inc(y1_ready.sem, 1)
                dve.wait_ge(g_ready.sem, g_ready.at(n))
                dve.wait_ge(y1_ready.sem, y1_ready.at(n))
                dve.tensor_tensor(out=y[:, u], in0=y[:, u], in1=g[:, u], op=ALU.mult).then_inc(y2_ready.sem, 1)
                dve.wait_ge(y2_ready.sem, y2_ready.at(n))
                dve.tensor_tensor(out=y[:, u], in0=y[:, u], in1=x_in[:, u], op=ALU.add)\
                   .then_inc(y_ready.sem, 1)

            staggered(dve, NCHUNK, lambda n, u: None, first, second)

        @block.tensor
        def _(pe):
            pe.wait_ge(consts, 48)
            pe.wait_ge(w_split, 2)
            tr_done.open(pe)
            s_done.open(pe)

            def first(n, u):
                pe.wait_ge(loaded[u].sem, loaded[u].at_turn(n, u))
                pe.wait_ge(ol_ready.sem, ol_ready.at(n - 1))
                pe.wait_ge(g_ready.sem, g_ready.at(n - 1))
                for t in range(TPC):
                    for k in range(KT):
                        pe.transpose(otp[:, k, t * P:(t + 1) * P], o_in[:, u, t, k * P:(k + 1) * P],
                                     ident[:, :])
                        mm = pe.transpose(x2p[:, t, k * P:(k + 1) * P], x2[:, u, k, t * P:(t + 1) * P],
                                          ident[:, :])
                mm.then_inc(tr_done.sem, 1)

            def second(n, u):
                pe.wait_ge(ol_ready.sem, ol_ready.at(n))
                pe.wait_ge(y1_ready.sem, y1_ready.at(n - 1))
                for t in range(TPC):
                    r = slice(t * P, (t + 1) * P)
                    steps = [(o, w, k) for k in range(KT)
                             for o, w in ((o_lo, w_hi), (o_hi, w_lo), (o_hi, w_hi))]
                    for j, (o, w, k) in enumerate(steps):
                        mm = pe.matmul(sp_[:, t], o[:, u, k, r], w[:, k],
                                       start=j == 0, stop=j == len(steps) - 1)
                mm.then_inc(s_done.sem, 1)

            staggered(pe, NCHUNK, lambda n, u: None, first, second)


def program(nc, i, out):
    def scratch(name, shape, dt=F32):
        return nc.dram_tensor(name, shape, dt).ap()

    x_d = scratch("x_d", (DEPTH + 1, KT, P, ROWS))
    qk_d = scratch("qk_d", (3, 4, P, ROWS), BF16)
    v_d = scratch("v_d", (ROWS, A_HEADS * VW))
    o_d = scratch("o_d", (ROWS, DIM))
    prepare(nc, i["x"], [i["wq"], i["wk"], i["wv"]], i["bqk"], i["bv"], i["ident"], x_d[0], qk_d, v_d)
    attend(nc, qk_d, v_d, i["causal"], i["ident"], o_d)
    layers(nc, x_d, i["wqkv"], i["wo_l"], i["w1"], i["w2"], i["b1"], i["b2"], i["ln_g"], i["ln_b"],
           i["scales"], i["rotary"], i["window"], i["ident"])
    combine(nc, i["x"], x_d[DEPTH], o_d, i["wo"], i["bo"], i["ident"], out)


def constants():
    f = np.float32
    at = np.arange(P)
    causal = np.where(at[None] > at[:, None], -BIG, 0.0)
    previous = np.where(at[None] >= at[:, None], 0.0, -BIG)
    own = np.where(at[None] <= at[:, None], 0.0, -BIG)
    window = np.stack([np.concatenate([previous, own], 1), np.concatenate([own, previous], 1)], 1)
    pos = np.arange(SEQ, dtype=f)
    even = np.arange(0, HD, 2, dtype=f)
    freq = pos[:, None] * (f(1.0) / f(10000.0) ** (even / f(HD)))[None]
    base = (even + f(0.4 * HD)) / f(1.4 * HD)
    xpos = base[None] ** ((pos - f(SEQ // 2)) / f(WINDOW // 2))[:, None]
    freq, xpos = (np.concatenate([a, a], 1) for a in (freq, xpos))
    turned = np.where(np.arange(HD) < HD // 2, f(-1.0), f(1.0))
    cos, sin = np.cos(freq), np.sin(freq) * turned
    tables = [cos * xpos * f(QK_SCALE), cos / xpos, sin * xpos * f(QK_SCALE), sin / xpos]
    return {"ident": np.eye(P, dtype=f), "causal": causal.astype(f), "window": window.astype(f),
            "rotary": np.concatenate(tables, 1).astype(f)}


def lay_out(a):
    def columns(v):
        return v.reshape(DEPTH, KT, P).transpose(2, 0, 1)

    q, k = a["L0_ffn_q_scale"], a["L0_ffn_k_scale"]
    swap = lambda s: np.concatenate([s[:, HD // 2:], s[:, :HD // 2]], 1)
    w1 = np.zeros((DIM, DEPTH, 2, MT * MW), np.float32)
    w1[..., :HID] = a["L0_ffn_w1"].reshape(DEPTH, DIM, 2, HID).transpose(1, 0, 2, 3)
    b1 = np.zeros((DEPTH, 2, MT * MW), np.float32)
    b1[..., :HID] = a["L0_ffn_b1"].reshape(DEPTH, 2, HID)
    w2 = np.zeros((MT * MW, DEPTH, DIM), np.float32)
    w2[:HID] = a["L0_ffn_w2"].transpose(1, 0, 2)
    return {
        "x": a["L0_attn_x"], "wq": a["L0_attn_Wq"].T, "wk": a["L0_attn_Wk"].T, "wv": a["L0_attn_Wv"].T,
        "bqk": np.concatenate([a["L0_attn_bq"], a["L0_attn_bk"]]).reshape(4, P).T,
        "bv": a["L0_attn_bv"], "wo": a["L0_attn_Wo"].T, "bo": a["L0_attn_bo"],
        "wqkv": a["L0_ffn_wqkv"].transpose(1, 0, 2), "wo_l": a["L0_ffn_wo"].transpose(1, 0, 2),
        "w1": w1.reshape(DIM, DEPTH, 2 * MT * MW), "w2": w2,
        "b1": b1.reshape(DEPTH, 2 * MT, MW).transpose(2, 0, 1), "b2": columns(a["L0_ffn_b2"]),
        "ln_g": columns(a["L0_ffn_ln_g"]), "ln_b": columns(a["L0_ffn_ln_b"]),
        "scales": np.concatenate([q, k, swap(q), swap(k)], 1),
    }


def kernel(**inputs):
    import concourse.bacc as bacc
    from concourse.bass_utils import run_bass_kernel_spmd

    nc = bacc.Bacc("TRN2", target_bir_lowering=False, num_devices=1)
    arrays = {**lay_out({n: np.asarray(v) for n, v in inputs.items()}), **constants()}
    arrays = {n: np.ascontiguousarray(v) for n, v in arrays.items()}
    tensors = {n: nc.dram_tensor(n, v.shape, mybir.dt.from_np(v.dtype), kind="ExternalInput").ap()
               for n, v in arrays.items()}
    out = nc.dram_tensor("out", (BATCH, SEQ, DIM), F32, kind="ExternalOutput")
    program(nc, tensors, out.ap())
    r = run_bass_kernel_spmd(nc, [arrays], core_ids=[0])
    return r.results[0]["out"]
```

```python
from contextlib import ExitStack

import numpy as np

import concourse.bass as bass
from concourse import mybir

F32 = mybir.dt.float32
F32R = mybir.dt.float32r
BF16 = mybir.dt.bfloat16
ALU = mybir.AluOpType
ACT = mybir.ActivationFunctionType
AX = mybir.AxisListType

P = 128
BATCH, SEQ, DIM = 4, 2048, 256
ROWS = BATCH * SEQ
KT = DIM // P
CHUNK = 512
TPC = CHUNK // P
NCHUNK = ROWS // CHUNK
CPB = SEQ // CHUNK
EPS = 1e-5

A_HEADS, A_HD = 16, 16
GH = 4
NGROUP = A_HEADS // GH
A_SCALE = A_HD ** -0.5
STACK_Q = [0, 0, 1, 1, 0, 2]
STACK_K = [0, 1, 0, 1, 2, 0]
NSTACK = len(STACK_Q)
SROWS = NSTACK * A_HD
VW = 32

DEPTH, HEADS, HD = 2, 8, 64
WINDOW = 128
INNER = HEADS * HD
HID = 682
QK_SCALE = 8.0
MT = 6
MW = -(-HID // MT)
BIG = 1e30



class Tally:

    def __init__(self, sem, per=1, spare=0):
        self.sem, self.per, self.spare = sem, per, spare

    def at(self, n, k=None):
        return n * self.per + (self.per if k is None else k) + self.spare * self.per

    def at_turn(self, n, u):
        return (n - u) * (self.per // 2) + self.per + self.spare * self.per

    def before_turn(self, n, u):
        return (n - u) * (self.per // 2) + self.spare * self.per

    def open(self, eng):
        eng.sem_inc(self.sem, self.spare * self.per)


def staggered(eng, count, *stages):
    last = len(stages) - 1

    def turn(n, u):
        for j, stage in enumerate(stages):
            if not isinstance(n, int) or 0 <= n - j < count:
                stage(n - j, (u - j) % 2)

    lead = last + last % 2
    rounds = (count - lead) // 2
    for n in range(lead):
        turn(n, n % 2)
    with eng.Fori(0, rounds) as i:
        for u in range(2):
            turn(i * 2 + (lead + u), u)
    for n in range(lead + 2 * rounds, count + last):
        turn(n, n % 2)


def prepare(nc, x, wT, bias_cols, bv, ident_d, xn_d, qk_d, v_d):
    with ExitStack() as ctx:
        def sb(name, shape, dt=F32):
            return ctx.enter_context(nc.sbuf_tensor("p_" + name, shape, dt))

        def tally(name, per=1, spare=0):
            return Tally(ctx.enter_context(nc.semaphore("p_" + name)), per, spare)

        ident = sb("ident", [P, P])
        w_raw = sb("w_raw", [P, KT, 3 * DIM])
        w_hi = sb("w_hi", [P, KT, 3 * DIM], F32R)
        w_lo = sb("w_lo", [P, KT, 3 * DIM], F32R)
        bcol = sb("bcol", [P, 4])
        bcol_s = sb("bcol_s", [P, 4])
        bv_row = sb("bv_row", [P, DIM])
        half = sb("half", [P, TPC])
        gate = sb("gate", [P, 2])
        x_in = sb("x_in", [P, 2, TPC, DIM])
        stats = sb("stats", [P, 2, TPC, 6])
        mv = sb("mv", [P, 2, TPC, 2])
        var = sb("var", [P, 2, TPC])
        rstd = sb("rstd", [P, 2, TPC])
        xn = sb("xn", [P, 2, TPC, DIM])
        xt = sb("xt", [P, 2, KT, CHUNK])
        x_hi = sb("x_hi", [P, 2, KT, CHUNK], F32R)
        x_lo = sb("x_lo", [P, 2, KT, CHUNK], F32R)
        qf = sb("qf", [P, 4, CHUNK])
        rest = sb("rest", [P, 4, CHUNK])
        parts = sb("parts", [P, 2, 3, 4, CHUNK], BF16)
        vt = sb("vt", [P, 2, TPC, A_HEADS, VW])
        trp = ctx.enter_context(nc.psum_tensor("p_trp", [P, KT, CHUNK], F32))
        qkp = ctx.enter_context(nc.psum_tensor("p_qkp", [P, 4, CHUNK], F32))
        vp = ctx.enter_context(nc.psum_tensor("p_vp", [P, TPC, DIM], F32))

        consts = tally("consts").sem
        w_split = tally("w_split").sem
        init = tally("init").sem
        x_loaded = [tally(f"x_loaded{u}", 16) for u in range(2)]
        x_stored = [tally(f"x_stored{u}", 16, 1) for u in range(2)]
        parts_stored = [tally(f"parts_stored{u}", 16, 1) for u in range(2)]
        v_stored = [tally(f"v_stored{u}", 16, 1) for u in range(2)]
        stat_done = tally("stat_done", TPC)
        aggr_done = tally("aggr_done", TPC)
        var_ready = tally("var_ready")
        rstd_ready = tally("rstd_ready")
        xn_ready = tally("xn_ready", TPC, 2)
        tr_done = tally("tr_done")
        xt_ready = tally("xt_ready", 1, 1)
        hi_ready = tally("hi_ready")
        lo_ready = tally("lo_ready", 1, 2)
        qk_done = tally("qk_done")
        qf_ready = tally("qf_ready", 1, 1)
        part1 = tally("part1")
        rest_ready = tally("rest_ready", 1, 1)
        part2 = tally("part2")
        part3 = tally("part3", 1, 1)
        v_done = tally("v_done")
        v_ready = tally("v_ready", 1, 1)
        block = ctx.enter_context(nc.Block())

        x_v = x.rearrange("b (c t p) d -> p (b c) t d", p=P, t=TPC)
        xn_v = xn_d.rearrange("k p (c n) -> p k c n", n=CHUNK)
        qk_v = qk_d.rearrange("s o p (c n) -> p (s o) c n", n=CHUNK)
        v_v = v_d.rearrange("(c t p) d -> p c t d", p=P, t=TPC)

        @block.sync
        def _(sp):
            sp.dma_start(ident[:, :], ident_d).then_inc(consts, 16)
            for j in range(3):
                sp.dma_start(w_raw[:, :, j * DIM:(j + 1) * DIM],
                             wT[j].rearrange("(k p) n -> p k n", p=P)).then_inc(consts, 16)
            sp.dma_start(bcol[:, :], bias_cols).then_inc(consts, 16)
            sp.dma_start(bv_row[:, :], bv.partition_broadcast(P)).then_inc(consts, 16)
            for t in x_stored + parts_stored + v_stored:
                t.open(sp)

            def load(n, u):
                sp.wait_ge(xn_ready.sem, xn_ready.at(n - 2))
                sp.dma_start(x_in[:, u], x_v[:, n]).then_inc(x_loaded[u].sem, 16)

            def store(n, u):
                sp.wait_ge(xt_ready.sem, xt_ready.at(n))
                sp.dma_start(xn_v[:, :, n], xt[:, u]).then_inc(x_stored[u].sem, 16)
                sp.wait_ge(v_ready.sem, v_ready.at(n))
                sp.wait_ge(part3.sem, part3.at(n))
                sp.dma_start(v_v[:, n], vt[:, u].rearrange("p t h w -> p t (h w)"))\
                  .then_inc(v_stored[u].sem, 16)
                sp.dma_start(qk_v[:, :, n], parts[:, u].rearrange("p s o n -> p (s o) n"))\
                  .then_inc(parts_stored[u].sem, 16)

            staggered(sp, NCHUNK, load, lambda n, u: None, store)
            for u in range(2):
                for t in (x_stored[u], v_stored[u], parts_stored[u]):
                    sp.wait_ge(t.sem, t.at_turn(NCHUNK - 2 + u, u))

        @block.gpsimd
        def _(pool):
            pool.memset(half[:, :], -0.5).then_inc(init, 1)
            pool.memset(vt[:, :, :, :, A_HD:A_HD + 1], 1.0).then_inc(init, 1)
            pool.memset(vt[:, :, :, :, A_HD + 1:VW], 0.0).then_inc(init, 1)
            pool.wait_ge(init, 3)
            lo_ready.open(pool)

            def root(n, u):
                pool.wait_ge(var_ready.sem, var_ready.at(n))
                pool.tensor_tensor(out=rstd[:, u], in0=var[:, u], in1=half[:, :],
                                   op=ALU.pow).then_inc(rstd_ready.sem, 1)

            def low(n, u):
                pool.wait_ge(hi_ready.sem, hi_ready.at(n))
                pool.tensor_tensor(out=x_lo[:, u], in0=xt[:, u], in1=x_hi[:, u].bitcast(F32),
                                   op=ALU.subtract).then_inc(lo_ready.sem, 1)

            staggered(pool, NCHUNK, root, low)

        @block.scalar
        def _(act):
            xt_ready.open(act)
            qf_ready.open(act)
            act.wait_ge(w_split, 4)

            def first(n, u):
                act.wait_ge(tr_done.sem, tr_done.at(n))
                act.wait_ge(x_stored[u].sem, x_stored[u].before_turn(n, u))
                act.wait_ge(lo_ready.sem, lo_ready.at(n - 2))
                act.activation(xt[:, u], trp[:, :, :], ACT.Copy).then_inc(xt_ready.sem, 1)

            def second(n, u):
                act.wait_ge(qk_done.sem, qk_done.at(n))
                act.wait_ge(part3.sem, part3.at(n - 1))
                for o in range(4):
                    q = act.activation(qf[:, o], qkp[:, o], ACT.Identity, bias=bcol_s[:, o:o + 1],
                                       scale=A_SCALE if o < 2 else 1.0)
                q.then_inc(qf_ready.sem, 1)
                act.wait_ge(qf_ready.sem, qf_ready.at(n))
                act.wait_ge(parts_stored[u].sem, parts_stored[u].before_turn(n, u))
                act.activation(parts[:, u, 0], qf[:, :, :], ACT.Copy).then_inc(part1.sem, 1)
                act.wait_ge(rest_ready.sem, rest_ready.at(n))
                act.activation(parts[:, u, 1], rest[:, :, :], ACT.Copy).then_inc(part2.sem, 1)

            staggered(act, NCHUNK, lambda n, u: None, first, second)

        @block.vector
        def _(dve):
            dve.wait_ge(consts, 96)
            dve.tensor_copy(w_hi[:, :, :], w_raw[:, :, :]).then_inc(w_split, 1)
            dve.tensor_copy(bcol_s[:, 2:4], bcol[:, 2:4]).then_inc(w_split, 1)
            dve.tensor_scalar(bcol_s[:, 0:2], bcol[:, 0:2], A_SCALE, None, ALU.mult).then_inc(w_split, 1)
            dve.memset(gate[:, 0:1], 0.0).then_inc(w_split, 1)
            dve.wait_ge(w_split, 4)
            dve.tensor_tensor(out=w_lo[:, :, :], in0=w_raw[:, :, :], in1=w_hi[:, :, :].bitcast(F32),
                              op=ALU.subtract).then_inc(w_split, 1)
            dve.wait_ge(init, 3)
            for t in (xn_ready, rest_ready, v_ready, part3):
                t.open(dve)

            def norm(n, u):
                dve.wait_ge(x_loaded[u].sem, x_loaded[u].at_turn(n, u))
                for t in range(TPC):
                    dve.bn_stats(stats[:, u, t], x_in[:, u, t]).then_inc(stat_done.sem, 1)
                dve.wait_ge(stat_done.sem, stat_done.at(n))
                dve.tensor_copy(gate[:, 1:2], gate[:, 0:1])
                for t in range(TPC):
                    dve.bn_aggr(mv[:, u, t], stats[:, u, t]).then_inc(aggr_done.sem, 1)
                dve.wait_ge(aggr_done.sem, aggr_done.at(n))
                dve.tensor_scalar(var[:, u], mv[:, u, :, 1], EPS, None, ALU.add).then_inc(var_ready.sem, 1)
                dve.wait_ge(rstd_ready.sem, rstd_ready.at(n))
                for t in range(TPC):
                    dve.tensor_scalar(xn[:, u, t], x_in[:, u, t], mv[:, u, t, 0:1], rstd[:, u, t:t + 1],
                                      ALU.subtract, ALU.mult).then_inc(xn_ready.sem, 1)

            def first(n, u):
                dve.wait_ge(xt_ready.sem, xt_ready.at(n))
                dve.tensor_copy(x_hi[:, u], xt[:, u]).then_inc(hi_ready.sem, 1)

            def second(n, u):
                dve.wait_ge(part1.sem, part1.at(n))
                dve.tensor_tensor(out=rest[:, :, :], in0=qf[:, :, :], in1=parts[:, u, 0],
                                  op=ALU.subtract).then_inc(rest_ready.sem, 1)
                dve.wait_ge(v_done.sem, v_done.at(n))
                dve.wait_ge(v_stored[u].sem, v_stored[u].before_turn(n, u))
                for t in range(TPC):
                    v = dve.tensor_tensor(out=vt[:, u, t, :, 0:A_HD],
                                          in0=vp[:, t].rearrange("p (h d) -> p h d", d=A_HD),
                                          in1=bv_row[:, :].rearrange("p (h d) -> p h d", d=A_HD),
                                          op=ALU.add)
                v.then_inc(v_ready.sem, 1)
                dve.wait_ge(part2.sem, part2.at(n))
                dve.tensor_tensor(out=parts[:, u, 2], in0=rest[:, :, :], in1=parts[:, u, 1],
                                  op=ALU.subtract).then_inc(part3.sem, 1)

            staggered(dve, NCHUNK, norm, first, second)

        @block.tensor
        def _(pe):
            pe.wait_ge(consts, 96)
            pe.wait_ge(w_split, 5)

            def first(n, u):
                pe.wait_ge(xn_ready.sem, xn_ready.at(n))
                pe.wait_ge(xt_ready.sem, xt_ready.at(n - 1))
                for t in range(TPC):
                    for k in range(KT):
                        mm = pe.transpose(trp[:, k, t * P:(t + 1) * P], xn[:, u, t, k * P:(k + 1) * P],
                                          ident[:, :])
                mm.then_inc(tr_done.sem, 1)

            def second(n, u):
                pe.wait_ge(lo_ready.sem, lo_ready.at(n))
                pe.wait_ge(qf_ready.sem, qf_ready.at(n - 1))
                for o in range(4):
                    cols = slice(o * P, (o + 1) * P)
                    steps = [(w, x_, k) for k in range(KT)
                             for w, x_ in ((w_lo, x_hi), (w_hi, x_lo), (w_hi, x_hi))]
                    for j, (w, x_, k) in enumerate(steps):
                        mm = pe.matmul(qkp[:, o], w[:, k, cols], x_[:, u, k],
                                       start=j == 0, stop=j == len(steps) - 1)
                mm.then_inc(qk_done.sem, 1)
                pe.wait_ge(v_ready.sem, v_ready.at(n - 1))
                for t in range(TPC):
                    rows = slice(t * P, (t + 1) * P)
                    steps = [(x_, w, k) for k in range(KT)
                             for x_, w in ((x_lo, w_hi), (x_hi, w_lo), (x_hi, w_hi))]
                    for j, (x_, w, k) in enumerate(steps):
                        mm = pe.matmul(vp[:, t], x_[:, u, k, rows], w[:, k, 2 * DIM:3 * DIM],
                                       start=j == 0, stop=j == len(steps) - 1)
                mm.then_inc(v_done.sem, 1)

            staggered(pe, NCHUNK, lambda n, u: None, first, second)


def attend(nc, qk_d, v_d, mask_d, ident_d, o_d):
    with ExitStack() as ctx:
        def sb(name, shape, dt=F32):
            return ctx.enter_context(nc.sbuf_tensor("a_" + name, shape, dt))

        def tally(name, per=1, spare=0):
            return Tally(ctx.enter_context(nc.semaphore("a_" + name)), per, spare)

        TASKS = TPC * GH
        STEPS = sum(TPC * (c + 1) for c in range(CPB))
        UNITS = sum(TASKS * (c + 1) for c in range(CPB))
        NG = BATCH * NGROUP
        NSLOT = 3
        NPT = 3

        ident = sb("ident", [P, P])
        identb = sb("identb", [P, P], BF16)
        maskf = sb("maskf", [P, P])
        mask = sb("mask", [P, P], BF16)
        qs = sb("qs", [P, NSLOT, GH, SEQ], BF16)
        ks = sb("ks", [P, NSLOT, GH, SEQ], BF16)
        vt = sb("vt", [P, NSLOT, SEQ // P, GH * VW])
        pt = sb("pt", [P, NPT, GH, CHUNK])
        gate = sb("gate", [P, 2])
        mx = sb("mx", [P, TASKS, CPB])
        negm = sb("negm", [P, 2, TASKS])
        ntb = sb("ntb", [TASKS, CPB, P], BF16)
        os_ = sb("os", [P, CHUNK])
        rden = sb("rden", [P, TPC, GH])
        otok = sb("otok", [P, 2, TPC, GH, A_HD])
        st = ctx.enter_context(nc.psum_tensor("a_st", [P, GH, CHUNK], F32))
        mm_ = ctx.enter_context(nc.psum_tensor("a_mm", [P, 2, CHUNK], F32))
        ot = ctx.enter_context(nc.psum_tensor("a_ot", [P, CHUNK], F32))
        tr = ctx.enter_context(nc.psum_tensor("a_tr", [P, TPC, GH, VW], F32))

        consts = tally("consts").sem
        ones_set = tally("ones_set").sem
        gate_set = tally("gate_set").sem
        loaded = [tally(f"loaded{u}", 16 * (2 * NSTACK + 1)) for u in range(NSLOT)]
        m_stored = [tally(f"m_stored{c}", 16 * GH, 1) for c in range(CPB)]
        o_stored = [tally(f"o_stored{c}", 16 * CPB // 2, 1) for c in range(2)]
        st_done = tally("st_done", 2 * STEPS)
        exp_done = tally("exp_done", 2 * STEPS, 1)
        masked = tally("masked", 2 * TPC * CPB, 1)
        pv_done = tally("pv_done", STEPS, 1)
        mm_done = tally("mm_done", UNITS)
        mm_used = tally("mm_used", UNITS, 1)
        negm_ready = tally("negm_ready", CPB, 1)
        nt_done = tally("nt_done", CPB, 1)
        ntb_ready = tally("ntb_ready", CPB, 1)
        os_ready = tally("os_ready", CPB, 1)
        otr_done = tally("otr_done", CPB, 1)
        rden_ready = tally("rden_ready", CPB)
        otok_ready = tally("otok_ready", CPB, 1)
        block = ctx.enter_context(nc.Block())

        parts_v = qk_d.rearrange("s o (h d) (b n) -> s d (o h) b n", d=A_HD, n=SEQ)
        v_v = v_d.rearrange("(b t p) (g w) -> p b g t w", p=P, b=BATCH, g=NGROUP)
        o_v = o_d.rearrange("(b c t p) (g w) -> p b g c t w", p=P, t=TPC, b=BATCH, g=NGROUP)

        def body(step, unit, chunk_maxima, row_out, out, main, mx_):
            s = n = 0
            for c in range(CPB):
                for kt in range(TPC * (c + 1)):
                    for piece in range(TPC):
                        if main:
                            step(c, kt, s, piece)
                        if mx_:
                            task, kc = divmod(n - TASKS * c * (c + 1) // 2, c + 1)
                            unit(c, task, kc, n)
                            n += 1
                    if mx_ and kt == TPC * (c + 1) - 1:
                        chunk_maxima(c, n)
                    if kt == 1 and c and mx_:
                        row_out(c - 1)
                    if kt == 2 and c and main:
                        out(c - 1)
                    s += 1
            if mx_:
                row_out(CPB - 1)
            if main:
                out(CPB - 1)

        def groups(eng, run, last_looped=NG - 1):
            run(-1, NSLOT - 1, -1, False, True)
            rounds = last_looped // NSLOT
            with eng.Fori(0, rounds) as i:
                for u in range(NSLOT):
                    run(i * NSLOT + u, u, i, True, True)
            for g in range(rounds * NSLOT, NG):
                run(g, g % NSLOT, g // NSLOT, True, g < NG - 1)

        def following(u, r):
            return (u + 1) % NSLOT, r + (u + 1) // NSLOT

        def first_column(c, kt):
            return max(0, kt - TPC * c) * P

        @block.sync
        def _(sp):
            sp.dma_start(ident[:, :], ident_d).then_inc(consts, 16)
            sp.dma_start(maskf[:, :], mask_d).then_inc(consts, 16)
            for t in m_stored + o_stored:
                t.open(sp)

            def load(g, u):
                b, hg = g // NGROUP, g % NGROUP
                sp.dma_start(vt[:, u], v_v[:, b, hg]).then_inc(loaded[u].sem, 16)
                for dst, pick, o in ((qs, STACK_Q, 0), (ks, STACK_K, A_HEADS)):
                    for j, s in enumerate(pick):
                        src = parts_v[s, :, :, b][:, bass.ds(hg * GH + o, GH)]
                        sp.dma_start(dst[j * A_HD:(j + 1) * A_HD, u], src).then_inc(loaded[u].sem, 16)

            load(0, 0)
            load(1, 1)

            def run(g, u, r, main, mx_):
                if main and (not isinstance(g, int) or g + 2 < NG):
                    sp.wait_ge(pv_done.sem, pv_done.at(g - 1))
                    load(g + 2, (u + 2) % NSLOT)
                v, _ = following(u, r)

                def row_out(c):
                    sp.wait_ge(ntb_ready.sem, ntb_ready.at(g + 1, c + 1))
                    for j in range(GH):
                        sp.dma_start(qs[SROWS:SROWS + 1, v, j, c * CHUNK:(c + 1) * CHUNK],
                                     ntb[j * TPC:(j + 1) * TPC, c])\
                          .then_inc(m_stored[c].sem, 16)

                def out(c):
                    sp.wait_ge(otok_ready.sem, otok_ready.at(g, c + 1))
                    sp.dma_start(o_v[:, g // NGROUP, g % NGROUP, c],
                                 otok[:, c % 2].rearrange("p t h d -> p t (h d)"))\
                      .then_inc(o_stored[c % 2].sem, 16)

                none = lambda *a: None
                body(none, none, none, row_out, out, main, mx_)

            groups(sp, run, NG - 2)
            for t in o_stored:
                sp.wait_ge(t.sem, t.at(NG - 1))

        @block.gpsimd
        def _(pool):
            pool.memset(gate[:, :], 0.0).then_inc(gate_set, 1)
            pool.wait_ge(gate_set, 1)
            masked.open(pool)

            def run(g, u, r, main, mx_):
                def step(c, kt, s, piece):
                    if piece or kt < TPC * c:
                        return
                    q0 = first_column(c, kt)
                    for h in range(2):
                        pool.wait_ge(masked.sem, masked.at(g, 2 * kt + h))
                        tile = pt[:, (STEPS * u + s) % NPT, 2 * h:2 * h + 2, q0:q0 + P]
                        pool.wait_ge(exp_done.sem, exp_done.at(g, 2 * s + h + 1))
                        pool.tensor_tensor(out=gate[:, 1:2], in0=gate[:, 0:1], in1=gate[:, 0:1], op=ALU.add)
                        pool.affine_select(out=tile, in_=tile, compare_op=ALU.is_ge, fill=0.0, base=0,
                                           pattern=[[0, 2], [1, P]], channel_multiplier=-1)\
                            .then_inc(masked.sem, 1)

                none = lambda *a: None
                body(step, none, none, none, none, main, mx_)

            groups(pool, run)

        @block.scalar
        def _(act):
            for t in (exp_done, os_ready, ntb_ready):
                t.open(act)

            def run(g, u, r, main, mx_):
                def step(c, kt, s, piece):
                    if piece:
                        return
                    q0 = first_column(c, kt)
                    act.wait_ge(pv_done.sem, pv_done.at(g, s - NPT + 1))
                    for h in range(2):
                        act.wait_ge(st_done.sem, st_done.at(g, 2 * s + h + 1))
                        act.activation(pt[:, (STEPS * u + s) % NPT, 2 * h:2 * h + 2, q0:CHUNK],
                                       st[:, 2 * h:2 * h + 2, q0:CHUNK], ACT.Exp).then_inc(exp_done.sem, 1)
                    if kt == 0 and c:
                        raw_out(c - 1, s)

                def raw_out(c, s):
                    act.wait_ge(pv_done.sem, pv_done.at(g, s))
                    act.wait_ge(otr_done.sem, otr_done.at(g, c))
                    act.activation(os_[:, :], ot[:, :], ACT.Copy).then_inc(os_ready.sem, 1)

                def row_out(c):
                    act.wait_ge(nt_done.sem, nt_done.at(g + 1, c + 1))
                    act.wait_ge(m_stored[c].sem, m_stored[c].at(g))
                    act.activation(ntb[:, c], tr[0:TASKS, 0], ACT.Copy).then_inc(ntb_ready.sem, 1)

                none = lambda *a: None
                body(step, none, none, row_out, none, main, mx_)
                if main:
                    raw_out(CPB - 1, STEPS)

            groups(act, run)

        @block.vector
        def _(dve):
            two_ones = float(np.array([0x3F803F80], np.uint32).view(np.float32)[0])
            dve.memset(ks[SROWS:SROWS + 1, :, :, :].bitcast(F32), two_ones).then_inc(ones_set, 1)
            dve.wait_ge(consts, 32)
            dve.tensor_copy(identb[:, :], ident[:, :]).then_inc(ones_set, 1)
            dve.tensor_copy(mask[:, :], maskf[:, :]).then_inc(ones_set, 1)
            for t in (mm_used, negm_ready, otok_ready):
                t.open(dve)

            def run(g, u, r, main, mx_):
                def unit(c, task, kc, n):
                    w = CHUNK if kc < c else (task % TPC + 1) * P
                    scores = mm_[:, n % 2, 0:w]
                    dve.wait_ge(mm_done.sem, mm_done.at(g + 1, n + 1))
                    dve.tensor_reduce(mx[:, task, kc:kc + 1], scores, AX.X, ALU.max)\
                       .then_inc(mm_used.sem, 1)

                def chunk_maxima(c, n):
                    dve.wait_ge(mm_used.sem, mm_used.at(g + 1, n))
                    dve.wait_ge(nt_done.sem, nt_done.at(g + 1, c - 1))
                    dve.tensor_reduce(negm[:, c % 2], mx[:, :, 0:c + 1], AX.X, ALU.max, negate=True)\
                       .then_inc(negm_ready.sem, 1)
                    dve.wait_ge(negm_ready.sem, negm_ready.at(g + 1, c + 1))

                def out(c):
                    dve.wait_ge(otr_done.sem, otr_done.at(g, c + 1))
                    dve.reciprocal(rden[:, :, :], tr[:, :, :, A_HD]).then_inc(rden_ready.sem, 1)
                    dve.wait_ge(rden_ready.sem, rden_ready.at(g, c + 1))
                    dve.wait_ge(o_stored[c % 2].sem, o_stored[c % 2].at(g, 16 * (c // 2)))
                    dve.tensor_tensor(out=otok[:, c % 2].rearrange("p t h d -> p (t h) d"),
                                      in0=tr[:, :, :, 0:A_HD].rearrange("p t h d -> p (t h) d"),
                                      in1=rden[:, :, :].rearrange("p t h -> p (t h)").unsqueeze(2)
                                      .broadcast_to([P, TPC * GH, A_HD]),
                                      op=ALU.mult).then_inc(otok_ready.sem, 1)

                body(lambda *a: None, unit, chunk_maxima, lambda c: None, out, main, mx_)

            groups(dve, run)

        @block.tensor
        def _(pe):
            pe.wait_ge(consts, 32)
            pe.wait_ge(ones_set, 3)
            for t in (pv_done, nt_done, otr_done):
                t.open(pe)

            def run(g, u, r, main, mx_):
                v, rv = following(u, r)
                steps = [(c, kt) for c in range(CPB) for kt in range(TPC * (c + 1))]

                def weigh(s):
                    c, kt = steps[s]
                    q0 = first_column(c, kt)
                    if kt == 0:
                        pe.wait_ge(os_ready.sem, os_ready.at(g, c))
                    if kt >= TPC * c:
                        pe.wait_ge(masked.sem, masked.at(g, 2 * kt + 2))
                    else:
                        pe.wait_ge(exp_done.sem, exp_done.at(g, 2 * s + 2))
                    for j in range(GH):
                        mm = pe.matmul(ot[j * VW:(j + 1) * VW, q0:CHUNK],
                                       vt[:, u, kt, j * VW:(j + 1) * VW],
                                       pt[:, (STEPS * u + s) % NPT, j, q0:CHUNK],
                                       start=kt == 0, stop=kt == TPC * (c + 1) - 1)
                    mm.then_inc(pv_done.sem, 1)

                def step(c, kt, s, piece):
                    q0 = first_column(c, kt)
                    if kt == 0 and piece == 0:
                        pe.wait_ge(m_stored[c].sem, m_stored[c].at(g))
                    if piece < 2:
                        pe.wait_ge(exp_done.sem, exp_done.at(g, 2 * s + piece - 1))
                        for j in (2 * piece, 2 * piece + 1):
                            mm = pe.matmul(st[:, j, q0:CHUNK], ks[0:SROWS + 1, u, j, kt * P:(kt + 1) * P],
                                           qs[0:SROWS + 1, u, j, c * CHUNK + q0:(c + 1) * CHUNK],
                                           start=True, stop=True)
                        mm.then_inc(st_done.sem, 1)
                    if piece == 3 and s:
                        weigh(s - 1)

                def unit(c, task, kc, n):
                    j, t = divmod(task, TPC)
                    q0, w = c * CHUNK + t * P, CHUNK if kc < c else (t + 1) * P
                    pe.wait_ge(mm_used.sem, mm_used.at(g + 1, n - 1))
                    mm = pe.matmul(mm_[:, n % 2, 0:w], qs[0:SROWS, v, j, q0:q0 + P],
                              ks[0:SROWS, v, j, kc * CHUNK:kc * CHUNK + w],
                              start=True, stop=kc < c)
                    if kc == c:
                        mm = pe.matmul(mm_[:, n % 2, w - P:w], identb[:, :], mask[:, :],
                                       start=False, stop=True)
                    mm.then_inc(mm_done.sem, 1)

                def row_out(c):
                    pe.wait_ge(negm_ready.sem, negm_ready.at(g + 1, c + 1))
                    pe.wait_ge(ntb_ready.sem, ntb_ready.at(g + 1, c))
                    if main:
                        pe.wait_ge(otok_ready.sem, otok_ready.at(g, c))
                    pe.transpose(tr[0:TASKS, 0].rearrange("p h w -> p (h w)"), negm[:, c % 2],
                                 ident[:, :]).then_inc(nt_done.sem, 1)

                def out(c):
                    if c == CPB - 1:
                        weigh(STEPS - 1)
                    pe.wait_ge(os_ready.sem, os_ready.at(g, c + 1))
                    if mx_:
                        pe.wait_ge(ntb_ready.sem, ntb_ready.at(g + 1, c + 1))
                    else:
                        pe.wait_ge(otok_ready.sem, otok_ready.at(g, c))
                    for t in range(TPC):
                        mm = pe.transpose(tr[:, t].rearrange("p h w -> p (h w)"),
                                          os_[:, t * P:(t + 1) * P], ident[:, :])
                    mm.then_inc(otr_done.sem, 1)

                if mx_:
                    pe.wait_ge(loaded[v].sem, loaded[v].per * (rv + 1))
                body(step, unit, lambda c, n: None, row_out, out, main, mx_)

            groups(pe, run)


def layers(nc, x_d, wqkv_d, wo_d, w1_d, w2_d, b1_d, b2_d, lng_d, lnb_d, scales_d, rotary_d, wmask_d,
           ident_d):
    with ExitStack() as ctx:
        def sb(name, shape, dt=F32):
            return ctx.enter_context(nc.sbuf_tensor("l_" + name, shape, dt))

        def tally(name, per=1, spare=0):
            return Tally(ctx.enter_context(nc.semaphore("l_" + name)), per, spare)

        TILES = SEQ // P
        PAIRS = HEADS // 2
        UNITS = TILES * PAIRS
        HT = INNER // P
        RING = 4

        ident = sb("ident", [P, P])
        mean_col = sb("mean_col", [P, 1])
        half = sb("half", [P, 2 * HEADS])
        gate = sb("gate", [P, 2])
        wmask = sb("wmask", [P, 2, 2 * P])
        wqkv_hi = sb("wqkv_hi", [P, KT, 3 * INNER], F32R)
        wqkv_lo = sb("wqkv_lo", [P, KT, 3 * INNER], F32R)
        wo_hi = sb("wo_hi", [P, HT, DIM], F32R)
        wo_lo = sb("wo_lo", [P, HT, DIM], F32R)
        w1_hi = sb("w1_hi", [P, KT, 2 * MT * MW], F32R)
        w1_lo = sb("w1_lo", [P, KT, 2 * MT * MW], F32R)
        w2_hi = sb("w2_hi", [MW, MT, DIM], F32R)
        w2_lo = sb("w2_lo", [MW, MT, DIM], F32R)
        rot = sb("rot", [P, TILES, 4, HD])
        scales = sb("scales", [P, 4 * HD])
        b1 = sb("b1", [MW, 2 * MT])
        b1raw = sb("b1raw", [MW, 2 * MT])
        b2 = sb("b2", [P, KT])
        lng = sb("lng", [P, KT])
        lnb = sb("lnb", [P, KT])
        xt = sb("xt", [P, 2, KT, 1 + CHUNK])
        h_hi = sb("h_hi", [P, KT, CHUNK], F32R)
        h_lo = sb("h_lo", [P, KT, CHUNK], F32R)
        work = sb("work", [P, 3, 2 * HEADS, HD])
        sq, qn, rt = work[:, 0], work[:, 1], work[:, 2]
        stage = work[:, :, :, :].rearrange("p a h d -> p (a h d)")
        ss = sb("ss", [P, 2 * HEADS])
        ssm = sb("ssm", [P, 2 * HEADS])
        rn = sb("rn", [P, 2 * HEADS])
        qh = sb("qh", [P, 2, HEADS, P], F32R)
        ql = sb("ql", [P, 2, HEADS, P], F32R)
        kh = sb("kh", [P, PAIRS, RING, P], F32R)
        kl = sb("kl", [P, PAIRS, RING, P], F32R)
        vr = sb("vr", [P, RING, INNER])
        pr = sb("pr", [P, 3, 2, 2 * P])
        negm = sb("negm", [P, 3, 2])
        den = sb("den", [P, 3, 2])
        rden = sb("rden", [P, 3, 2])
        pts = sb("pts", [P, 2, 4, P])
        o_hi = sb("o_hi", [P, HT, CHUNK], F32R)
        o_lo = sb("o_lo", [P, HT, CHUNK], F32R)
        u_hi = sb("u_hi", [MW, 2, CHUNK], F32R)
        u_lo = sb("u_lo", [MW, 2, CHUNK], F32R)
        x1 = sb("x1", [P, KT, 1 + CHUNK])
        dx = sb("dx", [P, KT, CHUNK])
        gl = sb("gl", [P, 2, CHUNK])
        var = sb("var", [P, TPC])
        rstd = sb("rstd", [P, TPC])
        n_hi = sb("n_hi", [P, KT, CHUNK], F32R)
        n_lo = sb("n_lo", [P, KT, CHUNK], F32R)

        banks = ctx.enter_context(nc.psum_tensor("l_banks", [P, 8, CHUNK], F32))
        qkp, vp, xp, net = banks[:, 0:2], banks[:, 2], banks[:, 3], banks[:, 4]
        sp_, ptp, otp = banks[:, 5], banks[:, 6], banks[:, 7]
        w2p = banks[:, 3:5]
        ag = [(banks[:, 2], banks[:, 6]), (banks[:, 0], banks[:, 1])]

        consts = tally("consts", 48).sem
        init = tally("init").sem
        staged = tally("staged", 16 * 10)
        split = tally("split", 11)
        folded = tally("folded")
        fold_done = tally("fold_done")
        x_loaded = [tally(f"x_loaded{u}", 16 * CPB // 2) for u in range(2)]
        x_stored = tally("x_stored", 16 * CPB, 1)
        names = dict(
            h_hi_ready=CPB * KT, h_ready=CPB * KT, qk_done=2 * TILES, v_done=TILES, sq_ready=2 * TILES,
            sum_ready=2 * TILES, ssm_ready=2 * TILES, rn_ready=2 * TILES, qn_ready=2 * TILES,
            rt_ready=2 * TILES, cos_ready=2 * TILES, r_ready=2 * TILES, v_ready=TILES, xq_done=TILES, xk_done=TILES, qh_ready=TILES,
            ql_ready=TILES, kh_ready=TILES, k_ready=TILES, s_done=UNITS, sm_ready=UNITS,
            exp_done=UNITS, rden_ready=UNITS, p_ready=UNITS, pt_done=UNITS, pts_ready=UNITS,
            pv_done=UNITS, oh_ready=TILES, ol_ready=TILES, wo_done=CPB * KT, x1_ready=CPB * KT,
            mean_done=CPB, dx_ready=CPB, sq2_ready=CPB, var_done=CPB, var_ready=CPB, rstd_ready=CPB,
            bc_done=CPB, nx_ready=CPB, n_hi_ready=CPB, n_ready=CPB, ag_done=CPB * MT,
            gelu_ready=CPB * MT, u_ready=CPB * MT, u_hi_ready=CPB * MT, u_lo_ready=CPB * MT,
            w2m_done=CPB * MT, x2_ready=CPB)
        S = {n: tally(n, per, 1) for n, per in names.items()}
        block = ctx.enter_context(nc.Block())

        x_v = x_d.rearrange("l k p (b n) -> p l b k n", n=SEQ)

        def key_tiles(T):
            if T == 0:
                return [0], slice(0, 1), wmask[:, 0, P:2 * P]
            if T % RING:
                return [T % RING - 1, T % RING], slice(T % RING - 1, T % RING + 1), wmask[:, 0]
            return [0, RING - 1], slice(0, RING, RING - 1), wmask[:, 1]

        def sequence(do):
            do("fetch", 0)
            do("load", 0)
            for T in range(-2, TILES + 2):
                ahead, chunk = T + 2 < TILES, T // TPC - 1
                for p in range(PAIRS):
                    i = T * PAIRS + p
                    if 0 <= i < UNITS:
                        do("scores", i)
                    if 0 <= i - 1 < UNITS:
                        do("norm", i - 1)
                    if chunk >= 0 and T % TPC == 0 and p == 3:
                        do("part_x1", chunk * KT)
                    if chunk >= 0 and T % TPC == 1 and p < 3:
                        do(("mean", "variance", "spread")[p], chunk)
                    if (T + 3) % TPC == 0 and 0 < (T + 3) // TPC < CPB:
                        if p == 0:
                            do("fetch", (T + 3) // TPC)
                        if p == 3:
                            do("load", (T + 3) // TPC)
                    if 0 <= T + 1 < TILES and 0 < p < 3:
                        do(("turn_q", "turn_k")[p - 1], T + 1)
                    if ahead and p < 2:
                        do("project", 2 * (T + 2) + p)
                    if ahead and p == 2:
                        do("project_v", T + 2)
                    if 0 <= T + 1 < TILES and p == 0:
                        do("rotated", 2 * (T + 1) + 1)
                    if 0 <= i - 2 < UNITS:
                        do("turn_p", i - 2)
                    if 0 <= i - 3 < UNITS:
                        do("weigh", i - 3)
                        if (i - 3) % PAIRS == PAIRS - 1:
                            do("part_o", (i - 3) // PAIRS)
                    if ahead and p < 2:
                        do("square", 2 * (T + 2) + p)
                    if ahead and 0 < p < 3:
                        do("sums", 2 * (T + 2) + p - 1)
                    if ahead and p > 1:
                        do("rotate", 2 * (T + 2) + p - 2)
                    if ahead and p == 3:
                        do("rotated", 2 * (T + 2))
                    if ahead and p == 3:
                        do("keep_v", T + 2)
                    if chunk >= 0 and T % TPC == 0 and p == 3:
                        do("part_x1", chunk * KT + 1)
                if chunk >= 0 and T % TPC == 1:
                    do("network", chunk)

        def program(eng, prepare_layer, events):
            with eng.Fori(0, DEPTH) as l:
                prepare_layer(l)
                with eng.Fori(0, BATCH) as b:
                    B = l * BATCH + b

                    def do(event, n):
                        if event in events:
                            events[event](B, l, b, n)

                    sequence(do)

        def wait(eng, name, B, k):
            eng.wait_ge(S[name].sem, S[name].at(B, k))

        @block.sync
        def _(sp):
            sp.dma_start(ident[:, :], ident_d).then_inc(consts, 16)
            sp.dma_start(wmask[:, :, :], wmask_d).then_inc(consts, 16)
            x_stored.open(sp)

            def prepare_layer(l):
                def get(dst, src):
                    sp.dma_start(dst, src).then_inc(staged.sem, 16)

                sp.wait_ge(x_stored.sem, x_stored.at(l * BATCH - 1))
                get(stage[:, 0:KT * 3 * INNER].rearrange("p (k n) -> p k n", k=KT),
                    wqkv_d[:, l].rearrange("(k p) n -> p k n", p=P))
                get(rot[:, :, :, :].rearrange("p t a d -> p t (a d)"),
                    rotary_d.rearrange("(t p) n -> p t n", p=P))
                get(scales[:, :], scales_d[l].partition_broadcast(P))
                get(b1raw[:, :], b1_d[:, l])
                get(b2[:, :], b2_d[:, l])
                get(lng[:, :], lng_d[:, l])
                get(lnb[:, :], lnb_d[:, l])
                sp.wait_ge(split.sem, split.at(l, 3))
                get(stage[:, 0:KT * 2 * MT * MW].rearrange("p (k n) -> p k n", k=KT),
                    w1_d[:, l].rearrange("(k p) n -> p k n", p=P))
                sp.wait_ge(split.sem, split.at(l, 7))
                get(stage[:, 0:HT * DIM].rearrange("p (k n) -> p k n", k=HT),
                    wo_d[:, l].rearrange("(k p) n -> p k n", p=P))
                get(stage[0:MW, HT * DIM:(HT + MT) * DIM].rearrange("p (k n) -> p k n", k=MT),
                    w2_d[:, l].rearrange("(k p) n -> p k n", p=MW))

            def fetch(B, l, b, c):
                wait(sp, "x1_ready", B, (c - 1) * KT)
                first = 0 if c else 1
                sp.dma_start(xt[:, c % 2, :, first:], x_v[:, l, b, :, c * CHUNK - 1 + first:(c + 1) * CHUNK])\
                  .then_inc(x_loaded[c % 2].sem, 16)

            def network(B, l, b, c):
                wait(sp, "x2_ready", B, c + 1)
                sp.dma_start(x_v[:, l + 1, b, :, c * CHUNK:(c + 1) * CHUNK], dx[:, :, :])\
                  .then_inc(x_stored.sem, 16)

            program(sp, prepare_layer, dict(fetch=fetch, network=network))
            sp.wait_ge(x_stored.sem, x_stored.at(DEPTH * BATCH - 1))

        @block.gpsimd
        def _(pool):
            pool.memset(half[:, :], -0.5).then_inc(init, 1)
            pool.memset(mean_col[:, :], 1.0 / DIM).then_inc(init, 1)
            pool.memset(qh[:, :, :, :].bitcast(F32), 0.0).then_inc(init, 1)
            pool.memset(ql[:, :, :, :].bitcast(F32), 0.0).then_inc(init, 1)
            pool.wait_ge(init, 5)
            for n in ("h_ready", "rn_ready", "cos_ready", "rstd_ready", "n_ready", "u_lo_ready"):
                S[n].open(pool)

            def prepare_layer(l):
                pass

            def load(B, l, b, c):
                wait(pool, "h_hi_ready", B, c * KT + 1)
                pool.tensor_tensor(out=h_lo[:, 0], in0=xt[:, c % 2, 0, 1:], in1=h_hi[:, 0].bitcast(F32),
                                   op=ALU.subtract).then_inc(S["h_ready"].sem, 1)
                if c == 0:
                    pool.memset(h_lo[:, 1, 0:1].bitcast(F32), 0.0)
                wait(pool, "h_hi_ready", B, (c + 1) * KT)
                f = 0 if c else 1
                pool.tensor_tensor(out=h_lo[:, 1, f:], in0=xt[:, c % 2, 1, f:CHUNK],
                                   in1=h_hi[:, 1, f:].bitcast(F32), op=ALU.subtract)\
                    .then_inc(S["h_ready"].sem, 1)

            def sums(B, l, b, n):
                a = n % 2
                wait(pool, "qn_ready", B, n - 1)
                wait(pool, "ssm_ready", B, n + 1)
                pool.tensor_tensor(out=rn[:, a * HEADS:(a + 1) * HEADS], in0=ssm[:, a * HEADS:(a + 1) * HEADS],
                                   in1=half[:, 0:HEADS], op=ALU.pow).then_inc(S["rn_ready"].sem, 1)

            def rotate(B, l, b, n):
                T, a = divmod(n, 2)
                part = slice(a * HEADS, (a + 1) * HEADS)
                wait(pool, "qn_ready", B, n + 1)
                pool.tensor_tensor(out=sq[:, part], in0=qn[:, part],
                                   in1=rot[:, T, a].unsqueeze(1).broadcast_to([P, HEADS, HD]),
                                   op=ALU.mult).then_inc(S["cos_ready"].sem, 1)

            def spread(B, l, b, c):
                wait(pool, "n_hi_ready", B, c + 1)
                pool.tensor_tensor(out=n_lo[:, :, :], in0=dx[:, :, :], in1=n_hi[:, :, :].bitcast(F32),
                                   op=ALU.subtract).then_inc(S["n_ready"].sem, 1)

            def variance(B, l, b, c):
                wait(pool, "var_ready", B, c + 1)
                pool.tensor_tensor(out=rstd[:, :], in0=var[:, :], in1=half[:, 0:TPC], op=ALU.pow)\
                    .then_inc(S["rstd_ready"].sem, 1)

            def network(B, l, b, c):
                for m in range(MT):
                    k = c * MT + m
                    wait(pool, "u_hi_ready", B, k + 1)
                    pool.tensor_tensor(out=u_lo[:, k % 2], in0=gl[0:MW, k % 2],
                                       in1=u_hi[:, k % 2].bitcast(F32), op=ALU.subtract)\
                        .then_inc(S["u_lo_ready"].sem, 1)

            program(pool, prepare_layer, dict(load=load, sums=sums, rotate=rotate, spread=spread,
                                              variance=variance, network=network))

        @block.scalar
        def _(act):
            for n in ("h_hi_ready", "sq_ready", "v_ready", "qh_ready", "kh_ready", "exp_done", "pts_ready",
                      "oh_ready", "sq2_ready", "n_hi_ready", "gelu_ready", "u_hi_ready"):
                S[n].open(act)

            def load(B, l, b, c):
                act.wait_ge(x_loaded[c % 2].sem, x_loaded[c % 2].at(B, 16 * (c // 2 + 1)))
                wait(act, "v_done", B, c * TPC)
                f = 0 if c else 1
                if c == 0:
                    act.activation(h_hi[:, 1, 0:1], gate[:, 0:1], ACT.Copy)
                act.activation(h_hi[:, 0], xt[:, c % 2, 0, 1:], ACT.Copy).then_inc(S["h_hi_ready"].sem, 1)
                act.activation(h_hi[:, 1, f:], xt[:, c % 2, 1, f:CHUNK], ACT.Copy)\
                   .then_inc(S["h_hi_ready"].sem, 1)

            def square(B, l, b, n):
                a = n % 2
                wait(act, "r_ready", B, n - 1)
                wait(act, "qk_done", B, n + 1)
                act.activation(sq[:, a * HEADS:(a + 1) * HEADS].rearrange("p h d -> p (h d)"), qkp[:, a],
                               ACT.Square).then_inc(S["sq_ready"].sem, 1)

            def keep_v(B, l, b, T):
                wait(act, "v_done", B, T + 1)
                wait(act, "pv_done", B, (T - RING + 2) * PAIRS)
                act.activation(vr[:, T % RING], vp, ACT.Copy).then_inc(S["v_ready"].sem, 1)

            def turn_q(B, l, b, T):
                wait(act, "xq_done", B, T + 1)
                for h, half_ in enumerate((slice(0, HD), slice(HD, P))):
                    q = act.activation(qh[half_, T % 2, h::2], xp[half_].rearrange("p (a n) -> p a n", n=P),
                                       ACT.Copy)
                q.then_inc(S["qh_ready"].sem, 1)

            def turn_k(B, l, b, T):
                wait(act, "xk_done", B, T + 1)
                act.activation(kh[:, :, T % RING], xp.rearrange("p (a n) -> p a n", n=P), ACT.Copy)\
                   .then_inc(S["kh_ready"].sem, 1)

            def scores(B, l, b, i):
                n = len(key_tiles(i // PAIRS)[0]) * P
                wait(act, "sm_ready", B, i + 1)
                for h in range(2):
                    e = act.activation(pr[:, i % 3, h, 0:n], pr[:, i % 3, h, 0:n], ACT.Exp, scale=-1.0,
                                       bias=negm[:, i % 3, h:h + 1], accum_out=den[:, i % 3, h:h + 1])
                e.then_inc(S["exp_done"].sem, 1)

            def turn_p(B, l, b, i):
                n = 2 * len(key_tiles(i // PAIRS)[0])
                wait(act, "pv_done", B, i - 1)
                wait(act, "pt_done", B, i + 1)
                act.activation(pts[:, i % 2, 0:n].rearrange("p a n -> p (a n)"), ptp[:, 0:n * P], ACT.Copy)\
                   .then_inc(S["pts_ready"].sem, 1)

            def part_o(B, l, b, T):
                t = T % TPC
                wait(act, "pv_done", B, (T + 1) * PAIRS)
                act.activation(o_hi[:, :, t * P:(t + 1) * P], otp.rearrange("p (a n) -> p a n", n=P), ACT.Copy)\
                   .then_inc(S["oh_ready"].sem, 1)

            def mean(B, l, b, c):
                wait(act, "u_lo_ready", B, c * MT)
                wait(act, "dx_ready", B, c + 1)
                act.activation(gl[:, :, :], dx[:, :, :], ACT.Square).then_inc(S["sq2_ready"].sem, 1)

            def spread(B, l, b, c):
                wait(act, "ag_done", B, c * MT)
                wait(act, "nx_ready", B, c + 1)
                act.activation(n_hi[:, :, :], dx[:, :, :], ACT.Copy).then_inc(S["n_hi_ready"].sem, 1)

            def network(B, l, b, c):
                for m in range(MT):
                    k = c * MT + m
                    wait(act, "u_lo_ready", B, k - 1)
                    wait(act, "ag_done", B, k + 1)
                    act.activation(gl[0:MW, k % 2], ag[k % 2][1][0:MW], ACT.Gelu,
                                   bias=b1[:, MT + m:MT + m + 1]).then_inc(S["gelu_ready"].sem, 1)
                    wait(act, "w2m_done", B, k - 1)
                    wait(act, "u_ready", B, k + 1)
                    act.activation(u_hi[:, k % 2], gl[0:MW, k % 2], ACT.Copy)\
                       .then_inc(S["u_hi_ready"].sem, 1)

            act.wait_ge(init, 5)
            program(act, lambda l: act.wait_ge(split.sem, split.at(l)), dict(
                load=load, square=square, keep_v=keep_v, turn_q=turn_q, turn_k=turn_k, scores=scores,
                turn_p=turn_p, part_o=part_o, mean=mean, spread=spread, network=network))

        @block.vector
        def _(dve):
            dve.memset(gate[:, :], 0.0).then_inc(init, 1)
            dve.wait_ge(init, 5)
            dve.wait_ge(consts, 32)
            for n in ("sum_ready", "ssm_ready", "qn_ready", "rt_ready", "r_ready", "ql_ready", "k_ready",
                      "sm_ready", "rden_ready", "p_ready", "ol_ready", "x1_ready", "dx_ready", "var_ready", "nx_ready",
                      "u_ready", "x2_ready"):
                S[n].open(dve)

            def prepare_layer(l):
                def parts(hi, lo, raw, k):
                    dve.tensor_copy(hi, raw).then_inc(split.sem, 1)
                    dve.wait_ge(split.sem, split.at(l, k + 1))
                    dve.tensor_tensor(out=lo, in0=raw, in1=hi.bitcast(F32), op=ALU.subtract)\
                       .then_inc(split.sem, 1)
                    if k + 2 < split.per:
                        dve.wait_ge(split.sem, split.at(l, k + 2))

                dve.wait_ge(staged.sem, staged.at(l, 7 * 16))
                parts(wqkv_hi[:, :, :], wqkv_lo[:, :, :],
                      stage[:, 0:KT * 3 * INNER].rearrange("p (k n) -> p k n", k=KT), 0)
                dve.tensor_tensor(out=rot[:, :, :, :].rearrange("p t a d -> p t (a d)"),
                                  in0=rot[:, :, :, :].rearrange("p t a d -> p t (a d)"),
                                  in1=scales[:, :].unsqueeze(1).broadcast_to([P, TILES, 4 * HD]),
                                  op=ALU.mult).then_inc(split.sem, 1)
                w1s = stage[:, 0:KT * 2 * MT * MW].rearrange("p (k n) -> p k n", k=KT)
                dve.wait_ge(fold_done.sem, fold_done.at(l))
                dve.tensor_tensor(out=b1[:, :], in0=banks[0:MW, 0, 0:2 * MT], in1=b1raw[:, :], op=ALU.add)\
                   .then_inc(split.sem, 1)
                for k in range(KT):
                    f = dve.tensor_scalar(w1s[:, k], w1s[:, k], lng[:, k:k + 1], None, ALU.mult)
                f.then_inc(folded.sem, 1)
                dve.wait_ge(folded.sem, folded.at(l))
                parts(w1_hi[:, :, :], w1_lo[:, :, :], w1s, 4)
                dve.tensor_copy(gate[:, 1:2], gate[:, 0:1]).then_inc(split.sem, 1)
                dve.wait_ge(staged.sem, staged.at(l, 10 * 16))
                parts(wo_hi[:, :, :], wo_lo[:, :, :],
                      stage[:, 0:HT * DIM].rearrange("p (k n) -> p k n", k=HT), 7)
                parts(w2_hi[:, :, :], w2_lo[:, :, :],
                      stage[0:MW, HT * DIM:(HT + MT) * DIM].rearrange("p (k n) -> p k n", k=MT), 9)

            def sums(B, l, b, n):
                half_ = slice(n % 2 * HEADS, (n % 2 + 1) * HEADS)
                wait(dve, "rn_ready", B, n - 1)
                wait(dve, "sq_ready", B, n + 1)
                dve.tensor_reduce(ss[:, half_], sq[:, half_], AX.X, ALU.add).then_inc(S["sum_ready"].sem, 1)
                wait(dve, "sum_ready", B, n + 1)
                dve.tensor_scalar(ssm[:, half_], ss[:, half_], 1e-24, None, ALU.max)\
                   .then_inc(S["ssm_ready"].sem, 1)

            def rotate(B, l, b, n):
                T, a = divmod(n, 2)
                part = slice(a * HEADS, (a + 1) * HEADS)
                wait(dve, "cos_ready", B, n - 1)
                wait(dve, "rn_ready", B, n + 1)
                dve.tensor_tensor(out=qn[:, part], in0=qkp[:, a].rearrange("p (h d) -> p h d", d=HD),
                                  in1=rn[:, part].unsqueeze(2).broadcast_to([P, HEADS, HD]),
                                  op=ALU.mult).then_inc(S["qn_ready"].sem, 1)
                wait(dve, ("xq_done", "xk_done")[a], B, T)
                wait(dve, "qn_ready", B, n + 1)
                for s in range(2):
                    dst, src = slice(s * HD // 2, (s + 1) * HD // 2), slice((1 - s) * HD // 2, (2 - s) * HD // 2)
                    r = dve.tensor_tensor(out=rt[:, part, dst], in0=qn[:, part, src],
                                          in1=rot[:, T, 2 + a, dst].unsqueeze(1)
                                          .broadcast_to([P, HEADS, HD // 2]), op=ALU.mult)
                r.then_inc(S["rt_ready"].sem, 1)

            def rotated(B, l, b, n):
                part = slice(n % 2 * HEADS, (n % 2 + 1) * HEADS)
                wait(dve, "rt_ready", B, n + 1)
                wait(dve, "cos_ready", B, n + 1)
                dve.tensor_tensor(out=rt[:, part], in0=rt[:, part], in1=sq[:, part], op=ALU.add)\
                   .then_inc(S["r_ready"].sem, 1)

            def turn_q(B, l, b, T):
                wait(dve, "qh_ready", B, T + 1)
                for h, half_ in enumerate((slice(0, HD), slice(HD, P))):
                    q = dve.tensor_tensor(out=ql[half_, T % 2, h::2],
                                          in0=xp[half_].rearrange("p (a n) -> p a n", n=P),
                                          in1=qh[half_, T % 2, h::2].bitcast(F32), op=ALU.subtract)
                q.then_inc(S["ql_ready"].sem, 1)

            def turn_k(B, l, b, T):
                wait(dve, "kh_ready", B, T + 1)
                dve.tensor_tensor(out=kl[:, :, T % RING], in0=xp.rearrange("p (a n) -> p a n", n=P),
                                  in1=kh[:, :, T % RING].bitcast(F32), op=ALU.subtract)\
                   .then_inc(S["k_ready"].sem, 1)

            def scores(B, l, b, i):
                tiles, _, m = key_tiles(i // PAIRS)
                n = len(tiles) * P
                wait(dve, "pt_done", B, max(i - 2, 0))
                wait(dve, "sm_ready", B, i)
                wait(dve, "s_done", B, i + 1)
                dve.tensor_copy(gate[:, 1:2], gate[:, 0:1])
                for h in range(2):
                    r = dve.tensor_tensor_reduce(pr[:, i % 3, h, 0:n], sp_[:, h * 2 * P:h * 2 * P + n], m,
                                                 -1.0, 3e38, ALU.add, ALU.min, negm[:, i % 3, h:h + 1])
                r.then_inc(S["sm_ready"].sem, 1)

            def norm(B, l, b, i):
                wait(dve, "exp_done", B, i + 1)
                dve.reciprocal(rden[:, i % 3], den[:, i % 3]).then_inc(S["rden_ready"].sem, 1)
                n = len(key_tiles(i // PAIRS)[0]) * P
                wait(dve, "rden_ready", B, i + 1)
                for h in range(2):
                    r = dve.tensor_scalar(pr[:, i % 3, h, 0:n], pr[:, i % 3, h, 0:n],
                                          rden[:, i % 3, h:h + 1], None, ALU.mult)
                r.then_inc(S["p_ready"].sem, 1)

            def part_o(B, l, b, T):
                t = T % TPC
                wait(dve, "oh_ready", B, T + 1)
                dve.tensor_tensor(out=o_lo[:, :, t * P:(t + 1) * P], in0=otp.rearrange("p (a n) -> p a n", n=P),
                                  in1=o_hi[:, :, t * P:(t + 1) * P].bitcast(F32), op=ALU.subtract)\
                   .then_inc(S["ol_ready"].sem, 1)

            def part_x1(B, l, b, n):
                c, k = divmod(n, KT)
                if k == 0:
                    wait(dve, "x2_ready", B, c)
                    if c:
                        dve.tensor_copy(x1[:, 1, 0:1], x1[:, 1, CHUNK:])
                    else:
                        dve.memset(x1[:, 1, 0:1], 0.0)
                wait(dve, "wo_done", B, n + 1)
                dve.tensor_tensor(out=x1[:, k, 1:], in0=net, in1=xt[:, c % 2, k, 1:], op=ALU.add)\
                   .then_inc(S["x1_ready"].sem, 1)

            def mean(B, l, b, c):
                dve.wait_ge(x_stored.sem, x_stored.at(B, 16 * c))
                wait(dve, "mean_done", B, c + 1)
                for k, rows in enumerate((x1[:, 0, 1:], x1[:, 1, 0:CHUNK])):
                    d = dve.tensor_tensor(out=dx[:, k], in0=rows, in1=net, op=ALU.subtract)
                d.then_inc(S["dx_ready"].sem, 1)

            def variance(B, l, b, c):
                wait(dve, "var_done", B, c + 1)
                dve.tensor_scalar(var[:, :], net[:, 0:TPC], EPS, None, ALU.add)\
                   .then_inc(S["var_ready"].sem, 1)

            def spread(B, l, b, c):
                wait(dve, "bc_done", B, c + 1)
                for k in range(KT):
                    d = dve.tensor_tensor(out=dx[:, k], in0=dx[:, k], in1=net, op=ALU.mult)
                d.then_inc(S["nx_ready"].sem, 1)

            def network(B, l, b, c):
                for m in range(MT):
                    k = c * MT + m
                    wait(dve, "gelu_ready", B, k + 1)
                    dve.scalar_tensor_tensor(out=gl[0:MW, k % 2], in0=ag[k % 2][0][0:MW],
                                             scalar=b1[:, m:m + 1], in1=gl[0:MW, k % 2],
                                             op0=ALU.add, op1=ALU.mult).then_inc(S["u_ready"].sem, 1)
                wait(dve, "w2m_done", B, (c + 1) * MT)
                wait(dve, "n_ready", B, c + 1)
                for k in range(KT):
                    d = dve.scalar_tensor_tensor(out=dx[:, k], in0=w2p[:, k], scalar=b2[:, k:k + 1],
                                                 in1=x1[:, k, 1:], op0=ALU.add, op1=ALU.add)
                d.then_inc(S["x2_ready"].sem, 1)

            program(dve, prepare_layer, dict(
                sums=sums, rotate=rotate, rotated=rotated, turn_q=turn_q, turn_k=turn_k, scores=scores,
                norm=norm, part_o=part_o, part_x1=part_x1, mean=mean, variance=variance, spread=spread,
                network=network))

        @block.tensor
        def _(pe):
            pe.wait_ge(consts, 32)
            pe.wait_ge(init, 5)
            for n in ("qk_done", "v_done", "xq_done", "xk_done", "s_done", "pt_done", "pv_done", "wo_done",
                      "mean_done", "var_done", "bc_done", "ag_done", "w2m_done"):
                S[n].open(pe)

            def products(out, steps):
                for j, (w, x_) in enumerate(steps):
                    mm = pe.matmul(out, w, x_, start=j == 0, stop=j == len(steps) - 1)
                return mm

            def three(w_hi, w_lo, x_hi_, x_lo_):
                return [(w_lo, x_hi_), (w_hi, x_lo_), (w_hi, x_hi_)]

            def prepare_layer(l):
                pe.wait_ge(staged.sem, staged.at(l, 8 * 16))
                pe.wait_ge(split.sem, split.at(l, 3))
                for m in range(2 * MT):
                    for k in range(KT):
                        o = k * 2 * MT * MW + m * MW
                        mm = pe.matmul(banks[0:MW, 0, m:m + 1], stage[:, o:o + MW], lnb[:, k:k + 1],
                                       start=k == 0, stop=k == KT - 1)
                mm.then_inc(fold_done.sem, 1)

            def project(B, l, b, n):
                T, a = divmod(n, 2)
                c, t = divmod(T, TPC)
                if n == 0:
                    pe.wait_ge(split.sem, split.at(l))
                wait(pe, "qn_ready", B, n - 1)
                rows, cols = slice(t * P, (t + 1) * P), slice(a * INNER, (a + 1) * INNER)
                for k in range(KT):
                    if t == 0 and a == 0:
                        wait(pe, "h_ready", B, c * KT + k + 1)
                    steps = three(h_hi[:, k, rows], h_lo[:, k, rows], wqkv_hi[:, k, cols], wqkv_lo[:, k, cols])
                    for j, (w, x_) in enumerate(steps):
                        mm = pe.matmul(qkp[:, a], w, x_, start=k == 0 and j == 0,
                                       stop=k == KT - 1 and j == len(steps) - 1)
                mm.then_inc(S["qk_done"].sem, 1)

            def project_v(B, l, b, T):
                t = T % TPC
                rows, cols = slice(t * P, (t + 1) * P), slice(2 * INNER, 3 * INNER)
                wait(pe, "v_ready", B, T)
                products(vp, [s for k in range(KT) for s in three(
                    h_hi[:, k, rows], h_lo[:, k, rows], wqkv_hi[:, k, cols], wqkv_lo[:, k, cols])])\
                    .then_inc(S["v_done"].sem, 1)

            def turn(first, sem):
                for p in range(PAIRS):
                    mm = pe.transpose(xp[:, p * P:(p + 1) * P],
                                      rt[:, first + 2 * p:first + 2 * p + 2].rearrange("p h d -> p (h d)"),
                                      ident[:, :])
                mm.then_inc(sem, 1)

            def turn_q(B, l, b, T):
                wait(pe, "r_ready", B, 2 * T + 1)
                wait(pe, "k_ready", B, T)
                if T % TPC == TPC - 1:
                    wait(pe, "x2_ready", B, T // TPC)
                turn(0, S["xq_done"].sem)

            def turn_k(B, l, b, T):
                wait(pe, "r_ready", B, 2 * (T + 1))
                wait(pe, "ql_ready", B, T + 1)
                turn(HEADS, S["xk_done"].sem)

            def scores(B, l, b, i):
                T, p = divmod(i, PAIRS)
                tiles, at, _ = key_tiles(T)
                n = len(tiles) * P
                if p == 0:
                    wait(pe, "k_ready", B, T + 1)
                wait(pe, "sm_ready", B, i)
                for h in range(2):
                    mm = products(sp_[:, h * 2 * P:h * 2 * P + n], three(
                        qh[:, T % 2, 2 * p + h], ql[:, T % 2, 2 * p + h], kh[:, p, at], kl[:, p, at]))
                mm.then_inc(S["s_done"].sem, 1)

            def turn_p(B, l, b, i):
                n = len(key_tiles(i // PAIRS)[0])
                wait(pe, "pts_ready", B, i)
                wait(pe, "p_ready", B, i + 1)
                for h in range(2):
                    for k in range(n):
                        mm = pe.transpose(ptp[:, (h * n + k) * P:(h * n + k + 1) * P],
                                          pr[:, i % 3, h, k * P:(k + 1) * P], ident[:, :])
                mm.then_inc(S["pt_done"].sem, 1)

            def weigh(B, l, b, i):
                T, p = divmod(i, PAIRS)
                tiles = key_tiles(T)[0]
                if p == 0:
                    wait(pe, "ol_ready", B, T)
                    wait(pe, "v_ready", B, T + 1)
                wait(pe, "pts_ready", B, i + 1)
                for k, slot in enumerate(tiles):
                    for h in range(2):
                        mm = pe.matmul(otp[h * HD:(h + 1) * HD, p * P:(p + 1) * P],
                                       vr[:, slot, (2 * p + h) * HD:(2 * p + h + 1) * HD],
                                       pts[:, i % 2, h * len(tiles) + k], start=k == 0,
                                       stop=k == len(tiles) - 1)
                mm.then_inc(S["pv_done"].sem, 1)

            def part_x1(B, l, b, n):
                c, k = divmod(n, KT)
                if k == 0:
                    wait(pe, "x2_ready", B, c)
                    wait(pe, "ol_ready", B, (c + 1) * TPC)
                wait(pe, "x1_ready", B, n)
                cols = slice(k * P, (k + 1) * P)
                products(net, [s for j in range(HT) for s in three(
                    wo_hi[:, j, cols], wo_lo[:, j, cols], o_hi[:, j], o_lo[:, j])])\
                    .then_inc(S["wo_done"].sem, 1)

            def mean(B, l, b, c):
                wait(pe, "x1_ready", B, (c + 1) * KT)
                products(net, [(mean_col[:, :].broadcast_to([P, P]), x1[:, 0, 1:]),
                               (mean_col[:, :].broadcast_to([P, P]), x1[:, 1, 0:CHUNK])])\
                    .then_inc(S["mean_done"].sem, 1)

            def variance(B, l, b, c):
                wait(pe, "sq2_ready", B, c + 1)
                for t in range(TPC):
                    mm = products(net[:, t:t + 1], [(gl[:, k, t * P:(t + 1) * P], mean_col[:, :])
                                                    for k in range(KT)])
                mm.then_inc(S["var_done"].sem, 1)

            def spread(B, l, b, c):
                wait(pe, "rstd_ready", B, c + 1)
                for t in range(TPC):
                    mm = pe.matmul(net[:, t * P:(t + 1) * P], rstd[:, t:t + 1].broadcast_to([P, P]),
                                   ident[:, :], start=True, stop=True)
                mm.then_inc(S["bc_done"].sem, 1)

            def network(B, l, b, c):
                T = c * TPC + TPC + 1
                wait(pe, "n_ready", B, c + 1)
                wait(pe, "v_ready", B, min(T + 3, TILES))
                wait(pe, "pts_ready", B, min(T * PAIRS + 2, UNITS))
                lag = 2
                for m in range(MT + lag):
                    k = c * MT + m
                    if m < MT:
                        if m == 1:
                            wait(pe, "qn_ready", B, 2 * min(T + 3, TILES))
                        wait(pe, "u_ready", B, k - 1)
                        for half_, bank in ((0, 0), (1, 1)):
                            cols = slice((half_ * MT + m) * MW, (half_ * MT + m + 1) * MW)
                            mm = products(ag[k % 2][bank][0:MW], [s for j in range(KT) for s in three(
                                w1_hi[:, j, cols], w1_lo[:, j, cols], n_hi[:, j], n_lo[:, j])])
                        mm.then_inc(S["ag_done"].sem, 1)
                    if m >= lag:
                        k, m_ = k - lag, m - lag
                        if m_ == 0:
                            wait(pe, "k_ready", B, min(T + 2, TILES))
                        wait(pe, "u_lo_ready", B, k + 1)
                        for o in range(KT):
                            cols = slice(o * P, (o + 1) * P)
                            steps = three(w2_hi[:, m_, cols], w2_lo[:, m_, cols],
                                          u_hi[:, k % 2], u_lo[:, k % 2])
                            for j, (w, x_) in enumerate(steps):
                                mm = pe.matmul(w2p[:, o], w, x_, start=m_ == 0 and j == 0,
                                               stop=m_ == MT - 1 and j == 2)
                        mm.then_inc(S["w2m_done"].sem, 1)

            program(pe, prepare_layer, dict(
                project=project, project_v=project_v, turn_q=turn_q, turn_k=turn_k, scores=scores,
                turn_p=turn_p, weigh=weigh, part_x1=part_x1, mean=mean, variance=variance,
                spread=spread, network=network))


def combine(nc, x, x2_d, o_d, wo_d, bo_d, ident_d, out):
    with ExitStack() as ctx:
        def sb(name, shape, dt=F32):
            return ctx.enter_context(nc.sbuf_tensor("c_" + name, shape, dt))

        def tally(name, per=1, spare=0):
            return Tally(ctx.enter_context(nc.semaphore("c_" + name)), per, spare)

        ident = sb("ident", [P, P])
        w_raw = sb("w_raw", [P, KT, DIM])
        w_hi = sb("w_hi", [P, KT, DIM], F32R)
        w_lo = sb("w_lo", [P, KT, DIM], F32R)
        bo = sb("bo", [P, DIM])
        o_in = sb("o_in", [P, 2, TPC, DIM])
        x2 = sb("x2", [P, 2, KT, CHUNK])
        x_in = sb("x_in", [P, 2, TPC, DIM])
        o_hi = sb("o_hi", [P, 2, KT, CHUNK], F32R)
        o_lo = sb("o_lo", [P, 2, KT, CHUNK], F32R)
        g = sb("g", [P, 2, TPC, DIM])
        y = sb("y", [P, 2, TPC, DIM])
        otp = ctx.enter_context(nc.psum_tensor("c_otp", [P, KT, CHUNK], F32))
        x2p = ctx.enter_context(nc.psum_tensor("c_x2p", [P, TPC, DIM], F32))
        sp_ = ctx.enter_context(nc.psum_tensor("c_sp", [P, TPC, DIM], F32))

        consts = tally("consts").sem
        w_split = tally("w_split").sem
        loaded = [tally(f"loaded{u}", 48) for u in range(2)]
        stored = [tally(f"stored{u}", 16, 1) for u in range(2)]
        tr_done = tally("tr_done", 1, 2)
        oh_ready = tally("oh_ready")
        ol_ready = tally("ol_ready", 1, 1)
        g_ready = tally("g_ready", 1, 1)
        s_done = tally("s_done", 1, 2)
        y1_ready = tally("y1_ready", 1, 1)
        y2_ready = tally("y2_ready")
        y_ready = tally("y_ready", 1, 2)
        block = ctx.enter_context(nc.Block())

        rows = lambda a: a.rearrange("(c t p) d -> p c t d", p=P, t=TPC)
        x_v, out_v = (a.rearrange("b (c t p) d -> p (b c) t d", p=P, t=TPC) for a in (x, out))
        o_v = rows(o_d)
        x2_v = x2_d.rearrange("k p (c n) -> p c k n", n=CHUNK)

        @block.sync
        def _(sp):
            sp.dma_start(ident[:, :], ident_d).then_inc(consts, 16)
            sp.dma_start(w_raw[:, :, :], wo_d.rearrange("(k p) n -> p k n", p=P)).then_inc(consts, 16)
            sp.dma_start(bo[:, :], bo_d.partition_broadcast(P)).then_inc(consts, 16)
            for t in stored:
                t.open(sp)

            def load(n, u):
                sp.wait_ge(tr_done.sem, tr_done.at(n - 2))
                sp.wait_ge(y_ready.sem, y_ready.at(n - 2))
                sp.dma_start(o_in[:, u], o_v[:, n]).then_inc(loaded[u].sem, 16)
                sp.dma_start(x2[:, u], x2_v[:, n]).then_inc(loaded[u].sem, 16)
                sp.dma_start(x_in[:, u], x_v[:, n]).then_inc(loaded[u].sem, 16)

            def store(n, u):
                sp.wait_ge(y_ready.sem, y_ready.at(n))
                sp.dma_start(out_v[:, n], y[:, u]).then_inc(stored[u].sem, 16)

            staggered(sp, NCHUNK, load, lambda n, u: None, store)
            for u in range(2):
                sp.wait_ge(stored[u].sem, stored[u].at_turn(NCHUNK - 2 + u, u))

        @block.scalar
        def _(act):
            g_ready.open(act)

            def first(n, u):
                act.wait_ge(tr_done.sem, tr_done.at(n))
                act.wait_ge(s_done.sem, s_done.at(n - 2))
                act.activation(o_hi[:, u], otp[:, :, :], ACT.Copy).then_inc(oh_ready.sem, 1)
                act.wait_ge(y_ready.sem, y_ready.at(n - 2))
                act.activation(g[:, u], x2p[:, :, :], ACT.Silu).then_inc(g_ready.sem, 1)

            staggered(act, NCHUNK, lambda n, u: None, first, lambda n, u: None)

        @block.vector
        def _(dve):
            dve.wait_ge(consts, 48)
            dve.tensor_copy(w_hi[:, :, :], w_raw[:, :, :]).then_inc(w_split, 1)
            dve.wait_ge(w_split, 1)
            dve.tensor_tensor(out=w_lo[:, :, :], in0=w_raw[:, :, :], in1=w_hi[:, :, :].bitcast(F32),
                              op=ALU.subtract).then_inc(w_split, 1)
            for t in (ol_ready, y1_ready, y_ready):
                t.open(dve)

            def first(n, u):
                dve.wait_ge(oh_ready.sem, oh_ready.at(n))
                dve.tensor_tensor(out=o_lo[:, u], in0=otp[:, :, :], in1=o_hi[:, u].bitcast(F32),
                                  op=ALU.subtract).then_inc(ol_ready.sem, 1)

            def second(n, u):
                dve.wait_ge(stored[u].sem, stored[u].before_turn(n, u))
                dve.wait_ge(s_done.sem, s_done.at(n))
                dve.tensor_tensor(out=y[:, u], in0=sp_[:, :, :],
                                  in1=bo[:, :].unsqueeze(1).broadcast_to([P, TPC, DIM]),
                                  op=ALU.add).then_inc(y1_ready.sem, 1)
                dve.wait_ge(g_ready.sem, g_ready.at(n))
                dve.wait_ge(y1_ready.sem, y1_ready.at(n))
                dve.tensor_tensor(out=y[:, u], in0=y[:, u], in1=g[:, u], op=ALU.mult).then_inc(y2_ready.sem, 1)
                dve.wait_ge(y2_ready.sem, y2_ready.at(n))
                dve.tensor_tensor(out=y[:, u], in0=y[:, u], in1=x_in[:, u], op=ALU.add)\
                   .then_inc(y_ready.sem, 1)

            staggered(dve, NCHUNK, lambda n, u: None, first, second)

        @block.tensor
        def _(pe):
            pe.wait_ge(consts, 48)
            pe.wait_ge(w_split, 2)
            tr_done.open(pe)
            s_done.open(pe)

            def first(n, u):
                pe.wait_ge(loaded[u].sem, loaded[u].at_turn(n, u))
                pe.wait_ge(ol_ready.sem, ol_ready.at(n - 1))
                pe.wait_ge(g_ready.sem, g_ready.at(n - 1))
                for t in range(TPC):
                    for k in range(KT):
                        pe.transpose(otp[:, k, t * P:(t + 1) * P], o_in[:, u, t, k * P:(k + 1) * P],
                                     ident[:, :])
                        mm = pe.transpose(x2p[:, t, k * P:(k + 1) * P], x2[:, u, k, t * P:(t + 1) * P],
                                          ident[:, :])
                mm.then_inc(tr_done.sem, 1)

            def second(n, u):
                pe.wait_ge(ol_ready.sem, ol_ready.at(n))
                pe.wait_ge(y1_ready.sem, y1_ready.at(n - 1))
                for t in range(TPC):
                    r = slice(t * P, (t + 1) * P)
                    steps = [(o, w, k) for k in range(KT)
                             for o, w in ((o_lo, w_hi), (o_hi, w_lo), (o_hi, w_hi))]
                    for j, (o, w, k) in enumerate(steps):
                        mm = pe.matmul(sp_[:, t], o[:, u, k, r], w[:, k],
                                       start=j == 0, stop=j == len(steps) - 1)
                mm.then_inc(s_done.sem, 1)

            staggered(pe, NCHUNK, lambda n, u: None, first, second)


def program(nc, i, out):
    def scratch(name, shape, dt=F32):
        return nc.dram_tensor(name, shape, dt).ap()

    x_d = scratch("x_d", (DEPTH + 1, KT, P, ROWS))
    qk_d = scratch("qk_d", (3, 4, P, ROWS), BF16)
    v_d = scratch("v_d", (ROWS, A_HEADS * VW))
    o_d = scratch("o_d", (ROWS, DIM))
    prepare(nc, i["x"], [i["wq"], i["wk"], i["wv"]], i["bqk"], i["bv"], i["ident"], x_d[0], qk_d, v_d)
    attend(nc, qk_d, v_d, i["causal"], i["ident"], o_d)
    layers(nc, x_d, i["wqkv"], i["wo_l"], i["w1"], i["w2"], i["b1"], i["b2"], i["ln_g"], i["ln_b"],
           i["scales"], i["rotary"], i["window"], i["ident"])
    combine(nc, i["x"], x_d[DEPTH], o_d, i["wo"], i["bo"], i["ident"], out)


def constants():
    f = np.float32
    at = np.arange(P)
    causal = np.where(at[None] > at[:, None], -BIG, 0.0)
    previous = np.where(at[None] >= at[:, None], 0.0, -BIG)
    own = np.where(at[None] <= at[:, None], 0.0, -BIG)
    window = np.stack([np.concatenate([previous, own], 1), np.concatenate([own, previous], 1)], 1)
    pos = np.arange(SEQ, dtype=f)
    even = np.arange(0, HD, 2, dtype=f)
    freq = pos[:, None] * (f(1.0) / f(10000.0) ** (even / f(HD)))[None]
    base = (even + f(0.4 * HD)) / f(1.4 * HD)
    xpos = base[None] ** ((pos - f(SEQ // 2)) / f(WINDOW // 2))[:, None]
    freq, xpos = (np.concatenate([a, a], 1) for a in (freq, xpos))
    turned = np.where(np.arange(HD) < HD // 2, f(-1.0), f(1.0))
    cos, sin = np.cos(freq), np.sin(freq) * turned
    tables = [cos * xpos * f(QK_SCALE), cos / xpos, sin * xpos * f(QK_SCALE), sin / xpos]
    return {"ident": np.eye(P, dtype=f), "causal": causal.astype(f), "window": window.astype(f),
            "rotary": np.concatenate(tables, 1).astype(f)}


def lay_out(a):
    def columns(v):
        return v.reshape(DEPTH, KT, P).transpose(2, 0, 1)

    q, k = a["L0_ffn_q_scale"], a["L0_ffn_k_scale"]
    swap = lambda s: np.concatenate([s[:, HD // 2:], s[:, :HD // 2]], 1)
    w1 = np.zeros((DIM, DEPTH, 2, MT * MW), np.float32)
    w1[..., :HID] = a["L0_ffn_w1"].reshape(DEPTH, DIM, 2, HID).transpose(1, 0, 2, 3)
    b1 = np.zeros((DEPTH, 2, MT * MW), np.float32)
    b1[..., :HID] = a["L0_ffn_b1"].reshape(DEPTH, 2, HID)
    w2 = np.zeros((MT * MW, DEPTH, DIM), np.float32)
    w2[:HID] = a["L0_ffn_w2"].transpose(1, 0, 2)
    return {
        "x": a["L0_attn_x"], "wq": a["L0_attn_Wq"].T, "wk": a["L0_attn_Wk"].T, "wv": a["L0_attn_Wv"].T,
        "bqk": np.concatenate([a["L0_attn_bq"], a["L0_attn_bk"]]).reshape(4, P).T,
        "bv": a["L0_attn_bv"], "wo": a["L0_attn_Wo"].T, "bo": a["L0_attn_bo"],
        "wqkv": a["L0_ffn_wqkv"].transpose(1, 0, 2), "wo_l": a["L0_ffn_wo"].transpose(1, 0, 2),
        "w1": w1.reshape(DIM, DEPTH, 2 * MT * MW), "w2": w2,
        "b1": b1.reshape(DEPTH, 2 * MT, MW).transpose(2, 0, 1), "b2": columns(a["L0_ffn_b2"]),
        "ln_g": columns(a["L0_ffn_ln_g"]), "ln_b": columns(a["L0_ffn_ln_b"]),
        "scales": np.concatenate([q, k, swap(q), swap(k)], 1),
    }


def kernel(**inputs):
    import concourse.bacc as bacc
    from concourse.bass_utils import run_bass_kernel_spmd

    nc = bacc.Bacc("TRN2", target_bir_lowering=False, num_devices=1)
    arrays = {**lay_out({n: np.asarray(v) for n, v in inputs.items()}), **constants()}
    arrays = {n: np.ascontiguousarray(v) for n, v in arrays.items()}
    tensors = {n: nc.dram_tensor(n, v.shape, mybir.dt.from_np(v.dtype), kind="ExternalInput").ap()
               for n, v in arrays.items()}
    out = nc.dram_tensor("out", (BATCH, SEQ, DIM), F32, kind="ExternalOutput")
    program(nc, tensors, out.ap())
    r = run_bass_kernel_spmd(nc, [arrays], core_ids=[0])
    return r.results[0]["out"]
```

```python
from contextlib import ExitStack

import numpy as np

import concourse.bass as bass
from concourse import mybir

F32 = mybir.dt.float32
F32R = mybir.dt.float32r
BF16 = mybir.dt.bfloat16
ALU = mybir.AluOpType
ACT = mybir.ActivationFunctionType
AX = mybir.AxisListType

P = 128
BATCH, SEQ, DIM = 4, 2048, 256
ROWS = BATCH * SEQ
KT = DIM // P
CHUNK = 512
TPC = CHUNK // P
NCHUNK = ROWS // CHUNK
CPB = SEQ // CHUNK
EPS = 1e-5

A_HEADS, A_HD = 16, 16
GH = 4
NGROUP = A_HEADS // GH
A_SCALE = A_HD ** -0.5
STACK_Q = [0, 0, 1, 1, 0, 2]
STACK_K = [0, 1, 0, 1, 2, 0]
NSTACK = len(STACK_Q)
SROWS = NSTACK * A_HD
VW = 32

DEPTH, HEADS, HD = 2, 8, 64
WINDOW = 128
INNER = HEADS * HD
HID = 682
QK_SCALE = 8.0
MT = 6
MW = -(-HID // MT)
BIG = 1e30



class Tally:

    def __init__(self, sem, per=1, spare=0):
        self.sem, self.per, self.spare = sem, per, spare

    def at(self, n, k=None):
        return n * self.per + (self.per if k is None else k) + self.spare * self.per

    def at_turn(self, n, u):
        return (n - u) * (self.per // 2) + self.per + self.spare * self.per

    def before_turn(self, n, u):
        return (n - u) * (self.per // 2) + self.spare * self.per

    def open(self, eng):
        eng.sem_inc(self.sem, self.spare * self.per)


def staggered(eng, count, *stages):
    last = len(stages) - 1

    def turn(n, u):
        for j, stage in enumerate(stages):
            if not isinstance(n, int) or 0 <= n - j < count:
                stage(n - j, (u - j) % 2)

    lead = last + last % 2
    rounds = (count - lead) // 2
    for n in range(lead):
        turn(n, n % 2)
    with eng.Fori(0, rounds) as i:
        for u in range(2):
            turn(i * 2 + (lead + u), u)
    for n in range(lead + 2 * rounds, count + last):
        turn(n, n % 2)


def prepare(nc, x, wT, bias_cols, bv, ident_d, xn_d, qk_d, v_d):
    with ExitStack() as ctx:
        def sb(name, shape, dt=F32):
            return ctx.enter_context(nc.sbuf_tensor("p_" + name, shape, dt))

        def tally(name, per=1, spare=0):
            return Tally(ctx.enter_context(nc.semaphore("p_" + name)), per, spare)

        ident = sb("ident", [P, P])
        w_raw = sb("w_raw", [P, KT, 3 * DIM])
        w_hi = sb("w_hi", [P, KT, 3 * DIM], F32R)
        w_lo = sb("w_lo", [P, KT, 3 * DIM], F32R)
        bcol = sb("bcol", [P, 4])
        bcol_s = sb("bcol_s", [P, 4])
        bv_row = sb("bv_row", [P, DIM])
        half = sb("half", [P, TPC])
        gate = sb("gate", [P, 2])
        x_in = sb("x_in", [P, 2, TPC, DIM])
        stats = sb("stats", [P, 2, TPC, 6])
        mv = sb("mv", [P, 2, TPC, 2])
        var = sb("var", [P, 2, TPC])
        rstd = sb("rstd", [P, 2, TPC])
        xn = sb("xn", [P, 2, TPC, DIM])
        xt = sb("xt", [P, 2, KT, CHUNK])
        x_hi = sb("x_hi", [P, 2, KT, CHUNK], F32R)
        x_lo = sb("x_lo", [P, 2, KT, CHUNK], F32R)
        qf = sb("qf", [P, 2, 4, CHUNK])
        rest = sb("rest", [P, 2, 4, CHUNK])
        parts = sb("parts", [P, 2, 3, 4, CHUNK], BF16)
        vt = sb("vt", [P, 2, TPC, A_HEADS, VW])
        trp = ctx.enter_context(nc.psum_tensor("p_trp", [P, KT, CHUNK], F32))
        qkp = ctx.enter_context(nc.psum_tensor("p_qkp", [P, 4, CHUNK], F32))
        vp = ctx.enter_context(nc.psum_tensor("p_vp", [P, TPC, DIM], F32))

        consts = tally("consts").sem
        w_split = tally("w_split").sem
        init = tally("init").sem
        x_loaded = [tally(f"x_loaded{u}", 16) for u in range(2)]
        x_stored = [tally(f"x_stored{u}", 16, 1) for u in range(2)]
        parts_stored = [tally(f"parts_stored{u}", 16, 1) for u in range(2)]
        v_stored = [tally(f"v_stored{u}", 16, 1) for u in range(2)]
        stat_done = tally("stat_done", TPC)
        aggr_done = tally("aggr_done", TPC)
        var_ready = tally("var_ready")
        rstd_ready = tally("rstd_ready")
        xn_ready = tally("xn_ready", TPC, 2)
        tr_done = tally("tr_done")
        xt_ready = tally("xt_ready", 1, 1)
        hi_ready = tally("hi_ready")
        lo_ready = tally("lo_ready", 1, 2)
        qk_done = tally("qk_done")
        qf_ready = tally("qf_ready", 2, 1)
        part1 = tally("part1", 2)
        rest_ready = tally("rest_ready", 2, 2)
        part2 = tally("part2", 2)
        part3 = tally("part3", 1, 2)
        v_done = tally("v_done")
        v_ready = tally("v_ready", 1, 1)
        block = ctx.enter_context(nc.Block())

        x_v = x.rearrange("b (c t p) d -> p (b c) t d", p=P, t=TPC)
        xn_v = xn_d.rearrange("k p (c n) -> p k c n", n=CHUNK)
        qk_v = qk_d.rearrange("s o p (c n) -> p (s o) c n", n=CHUNK)
        v_v = v_d.rearrange("(c t p) d -> p c t d", p=P, t=TPC)

        @block.sync
        def _(sp):
            sp.dma_start(ident[:, :], ident_d).then_inc(consts, 16)
            for j in range(3):
                sp.dma_start(w_raw[:, :, j * DIM:(j + 1) * DIM],
                             wT[j].rearrange("(k p) n -> p k n", p=P)).then_inc(consts, 16)
            sp.dma_start(bcol[:, :], bias_cols).then_inc(consts, 16)
            sp.dma_start(bv_row[:, :], bv.partition_broadcast(P)).then_inc(consts, 16)
            for t in x_stored + parts_stored + v_stored:
                t.open(sp)

            def load(n, u):
                sp.wait_ge(xn_ready.sem, xn_ready.at(n - 2))
                sp.dma_start(x_in[:, u], x_v[:, n]).then_inc(x_loaded[u].sem, 16)

            def store_x(n, u):
                sp.wait_ge(xt_ready.sem, xt_ready.at(n))
                sp.dma_start(xn_v[:, :, n], xt[:, u]).then_inc(x_stored[u].sem, 16)

            def store(n, u):
                sp.wait_ge(part3.sem, part3.at(n))
                sp.wait_ge(v_ready.sem, v_ready.at(n))
                sp.dma_start(v_v[:, n], vt[:, u].rearrange("p t h w -> p t (h w)"))\
                  .then_inc(v_stored[u].sem, 16)
                sp.dma_start(qk_v[:, :, n], parts[:, u].rearrange("p s o n -> p (s o) n"))\
                  .then_inc(parts_stored[u].sem, 16)

            staggered(sp, NCHUNK, load, lambda n, u: None, store_x, lambda n, u: None, store)
            for u in range(2):
                for t in (x_stored[u], v_stored[u], parts_stored[u]):
                    sp.wait_ge(t.sem, t.at_turn(NCHUNK - 2 + u, u))

        @block.gpsimd
        def _(pool):
            pool.memset(half[:, :], -0.5).then_inc(init, 1)
            pool.memset(vt[:, :, :, :, A_HD:A_HD + 1], 1.0).then_inc(init, 1)
            pool.memset(vt[:, :, :, :, A_HD + 1:VW], 0.0).then_inc(init, 1)
            pool.wait_ge(init, 3)
            lo_ready.open(pool)
            part3.open(pool)

            def root(n, u):
                pool.wait_ge(var_ready.sem, var_ready.at(n))
                pool.tensor_tensor(out=rstd[:, u], in0=var[:, u], in1=half[:, :],
                                   op=ALU.pow).then_inc(rstd_ready.sem, 1)

            def low(n, u):
                pool.wait_ge(hi_ready.sem, hi_ready.at(n))
                pool.tensor_tensor(out=x_lo[:, u], in0=xt[:, u], in1=x_hi[:, u].bitcast(F32),
                                   op=ALU.subtract).then_inc(lo_ready.sem, 1)

            def last_part(n, u):
                pool.wait_ge(part2.sem, part2.at(n))
                pool.tensor_tensor(out=parts[:, u, 2], in0=rest[:, u], in1=parts[:, u, 1],
                                   op=ALU.subtract).then_inc(part3.sem, 1)

            staggered(pool, NCHUNK, root, low, lambda n, u: None, last_part)

        @block.scalar
        def _(act):
            xt_ready.open(act)
            qf_ready.open(act)
            act.wait_ge(w_split, 4)

            def first(n, u):
                act.wait_ge(tr_done.sem, tr_done.at(n))
                act.wait_ge(x_stored[u].sem, x_stored[u].before_turn(n, u))
                act.wait_ge(lo_ready.sem, lo_ready.at(n - 2))
                act.activation(xt[:, u], trp[:, :, :], ACT.Copy).then_inc(xt_ready.sem, 1)

            def second(n, u):
                act.wait_ge(qk_done.sem, qk_done.at(n))
                act.wait_ge(rest_ready.sem, rest_ready.at(n - 2))
                act.wait_ge(parts_stored[u].sem, parts_stored[u].before_turn(n, u))
                for a in range(2):
                    both = slice(2 * a, 2 * a + 2)
                    for o in (2 * a, 2 * a + 1):
                        q = act.activation(qf[:, u, o], qkp[:, o], ACT.Identity, bias=bcol_s[:, o:o + 1],
                                           scale=(A_SCALE, 1.0)[a])
                    q.then_inc(qf_ready.sem, 1)
                    act.wait_ge(qf_ready.sem, qf_ready.at(n, a + 1))
                    act.activation(parts[:, u, 0, both], qf[:, u, both], ACT.Copy).then_inc(part1.sem, 1)
                for a in range(2):
                    both = slice(2 * a, 2 * a + 2)
                    act.wait_ge(rest_ready.sem, rest_ready.at(n, a + 1))
                    act.activation(parts[:, u, 1, both], rest[:, u, both], ACT.Copy).then_inc(part2.sem, 1)

            staggered(act, NCHUNK, lambda n, u: None, first, second)

        @block.vector
        def _(dve):
            dve.wait_ge(consts, 96)
            dve.tensor_copy(w_hi[:, :, :], w_raw[:, :, :]).then_inc(w_split, 1)
            dve.tensor_copy(bcol_s[:, 2:4], bcol[:, 2:4]).then_inc(w_split, 1)
            dve.tensor_scalar(bcol_s[:, 0:2], bcol[:, 0:2], A_SCALE, None, ALU.mult).then_inc(w_split, 1)
            dve.memset(gate[:, 0:1], 0.0).then_inc(w_split, 1)
            dve.wait_ge(w_split, 4)
            dve.tensor_tensor(out=w_lo[:, :, :], in0=w_raw[:, :, :], in1=w_hi[:, :, :].bitcast(F32),
                              op=ALU.subtract).then_inc(w_split, 1)
            dve.wait_ge(init, 3)
            for t in (xn_ready, rest_ready, v_ready):
                t.open(dve)

            def norm(n, u):
                dve.wait_ge(x_loaded[u].sem, x_loaded[u].at_turn(n, u))
                for t in range(TPC):
                    dve.bn_stats(stats[:, u, t], x_in[:, u, t]).then_inc(stat_done.sem, 1)
                dve.wait_ge(stat_done.sem, stat_done.at(n))
                dve.tensor_copy(gate[:, 1:2], gate[:, 0:1])
                for t in range(TPC):
                    dve.bn_aggr(mv[:, u, t], stats[:, u, t]).then_inc(aggr_done.sem, 1)
                dve.wait_ge(aggr_done.sem, aggr_done.at(n))
                dve.tensor_scalar(var[:, u], mv[:, u, :, 1], EPS, None, ALU.add).then_inc(var_ready.sem, 1)
                dve.wait_ge(rstd_ready.sem, rstd_ready.at(n))
                for t in range(TPC):
                    dve.tensor_scalar(xn[:, u, t], x_in[:, u, t], mv[:, u, t, 0:1], rstd[:, u, t:t + 1],
                                      ALU.subtract, ALU.mult).then_inc(xn_ready.sem, 1)

            def first(n, u):
                dve.wait_ge(xt_ready.sem, xt_ready.at(n))
                dve.tensor_copy(x_hi[:, u], xt[:, u]).then_inc(hi_ready.sem, 1)

            def second(n, u):
                dve.wait_ge(part3.sem, part3.at(n - 2))
                for a in range(2):
                    both = slice(2 * a, 2 * a + 2)
                    dve.wait_ge(part1.sem, part1.at(n, a + 1))
                    dve.tensor_tensor(out=rest[:, u, both], in0=qf[:, u, both], in1=parts[:, u, 0, both],
                                      op=ALU.subtract).then_inc(rest_ready.sem, 1)
                dve.wait_ge(v_done.sem, v_done.at(n))
                dve.wait_ge(v_stored[u].sem, v_stored[u].before_turn(n, u))
                for t in range(TPC):
                    v = dve.tensor_tensor(out=vt[:, u, t, :, 0:A_HD],
                                          in0=vp[:, t].rearrange("p (h d) -> p h d", d=A_HD),
                                          in1=bv_row[:, :].rearrange("p (h d) -> p h d", d=A_HD),
                                          op=ALU.add)
                v.then_inc(v_ready.sem, 1)

            staggered(dve, NCHUNK, norm, first, second)

        @block.tensor
        def _(pe):
            pe.wait_ge(consts, 96)
            pe.wait_ge(w_split, 5)

            def first(n, u):
                pe.wait_ge(xn_ready.sem, xn_ready.at(n))
                pe.wait_ge(xt_ready.sem, xt_ready.at(n - 1))
                for t in range(TPC):
                    for k in range(KT):
                        mm = pe.transpose(trp[:, k, t * P:(t + 1) * P], xn[:, u, t, k * P:(k + 1) * P],
                                          ident[:, :])
                mm.then_inc(tr_done.sem, 1)

            def second(n, u):
                pe.wait_ge(lo_ready.sem, lo_ready.at(n))
                pe.wait_ge(qf_ready.sem, qf_ready.at(n - 1))
                for o in range(4):
                    cols = slice(o * P, (o + 1) * P)
                    steps = [(w, x_, k) for k in range(KT)
                             for w, x_ in ((w_lo, x_hi), (w_hi, x_lo), (w_hi, x_hi))]
                    for j, (w, x_, k) in enumerate(steps):
                        mm = pe.matmul(qkp[:, o], w[:, k, cols], x_[:, u, k],
                                       start=j == 0, stop=j == len(steps) - 1)
                mm.then_inc(qk_done.sem, 1)
                pe.wait_ge(v_ready.sem, v_ready.at(n - 1))
                for t in range(TPC):
                    rows = slice(t * P, (t + 1) * P)
                    steps = [(x_, w, k) for k in range(KT)
                             for x_, w in ((x_lo, w_hi), (x_hi, w_lo), (x_hi, w_hi))]
                    for j, (x_, w, k) in enumerate(steps):
                        mm = pe.matmul(vp[:, t], x_[:, u, k, rows], w[:, k, 2 * DIM:3 * DIM],
                                       start=j == 0, stop=j == len(steps) - 1)
                mm.then_inc(v_done.sem, 1)

            staggered(pe, NCHUNK, lambda n, u: None, first, second)


def attend(nc, qk_d, v_d, mask_d, ident_d, o_d):
    with ExitStack() as ctx:
        def sb(name, shape, dt=F32):
            return ctx.enter_context(nc.sbuf_tensor("a_" + name, shape, dt))

        def tally(name, per=1, spare=0):
            return Tally(ctx.enter_context(nc.semaphore("a_" + name)), per, spare)

        TASKS = TPC * GH
        STEPS = sum(TPC * (c + 1) for c in range(CPB))
        UNITS = sum(TASKS * (c + 1) for c in range(CPB))
        NG = BATCH * NGROUP
        NSLOT = 3
        NPT = 3

        ident = sb("ident", [P, P])
        identb = sb("identb", [P, P], BF16)
        maskf = sb("maskf", [P, P])
        mask = sb("mask", [P, P], BF16)
        qs = sb("qs", [P, NSLOT, GH, SEQ], BF16)
        ks = sb("ks", [P, NSLOT, GH, SEQ], BF16)
        vt = sb("vt", [P, NSLOT, SEQ // P, GH * VW])
        pt = sb("pt", [P, NPT, GH, CHUNK])
        gate = sb("gate", [P, 2])
        mx = sb("mx", [P, TASKS, CPB])
        negm = sb("negm", [P, 2, TASKS])
        ntb = sb("ntb", [TASKS, CPB, P], BF16)
        os_ = sb("os", [P, CHUNK])
        rden = sb("rden", [P, TPC, GH])
        otok = sb("otok", [P, 2, TPC, GH, A_HD])
        st = ctx.enter_context(nc.psum_tensor("a_st", [P, GH, CHUNK], F32))
        turns = ctx.enter_context(nc.psum_tensor("a_turns", [P, 3, CHUNK], F32))
        ot = ctx.enter_context(nc.psum_tensor("a_ot", [P, CHUNK], F32))

        consts = tally("consts").sem
        ones_set = tally("ones_set").sem
        gate_set = tally("gate_set").sem
        loaded = [tally(f"loaded{u}", 16 * (2 * NSTACK + 1)) for u in range(NSLOT)]
        m_stored = [tally(f"m_stored{c}", 16 * GH, 1) for c in range(CPB)]
        o_stored = [tally(f"o_stored{c}", 16 * CPB // 2, 1) for c in range(2)]
        st_done = tally("st_done", 2 * STEPS)
        exp_done = tally("exp_done", 2 * STEPS, 1)
        masked = tally("masked", 2 * TPC * CPB, 1)
        pv_done = tally("pv_done", STEPS, 1)
        mm_done = tally("mm_done", UNITS)
        mm_used = tally("mm_used", UNITS, 1)
        negm_ready = tally("negm_ready", CPB, 1)
        nt_done = tally("nt_done", CPB, 1)
        ntb_ready = tally("ntb_ready", CPB, 1)
        os_ready = tally("os_ready", CPB, 1)
        otr_done = tally("otr_done", CPB, 1)
        rden_ready = tally("rden_ready", CPB)
        otok_ready = tally("otok_ready", CPB, 1)
        block = ctx.enter_context(nc.Block())

        parts_v = qk_d.rearrange("s o (h d) (b n) -> s d (o h) b n", d=A_HD, n=SEQ)
        v_v = v_d.rearrange("(b t p) (g w) -> p b g t w", p=P, b=BATCH, g=NGROUP)
        o_v = o_d.rearrange("(b c t p) (g w) -> p b g c t w", p=P, t=TPC, b=BATCH, g=NGROUP)

        def body(step, unit, chunk_maxima, row_out, out, main, mx_):
            s = n = 0
            for c in range(CPB):
                for kt in range(TPC * (c + 1)):
                    for piece in range(TPC):
                        if main:
                            step(c, kt, s, piece)
                        if mx_:
                            task, kc = divmod(n - TASKS * c * (c + 1) // 2, c + 1)
                            unit(c, task, kc, n)
                            n += 1
                    if mx_ and kt == TPC * (c + 1) - 1:
                        chunk_maxima(c, n)
                    if kt == 1 and c and mx_:
                        row_out(c - 1)
                    if kt == 2 and c and main:
                        out(c - 1)
                    s += 1
            if mx_:
                row_out(CPB - 1)
            if main:
                out(CPB - 1)

        users = []
        body(lambda *a: None, lambda c, task, kc, n: users.append(("unit", n)), lambda *a: None,
             lambda c: users.append(("row", c)), lambda c: users.append(("out", c)), True, True)
        assert len(users) % 3 == 0
        turn_of = {user: r for r, user in enumerate(users)}

        def bank(kind, n):
            return turns[:, turn_of[kind, n] % 3]

        def bank_read(g, kind, n, main, mx_):
            r = turn_of[kind, n] - 3
            while r >= 0 and not (main if users[r][0] == "out" else mx_):
                r -= 3
            before, m = users[r]
            g = g if r >= 0 else g - 1
            if before == "unit":
                return mm_used.sem, mm_used.at(g + 1, m + 1)
            if before == "row":
                return ntb_ready.sem, ntb_ready.at(g + 1, m + 1)
            return otok_ready.sem, otok_ready.at(g, m + 1)

        def rows_of(bank_):
            return bank_.rearrange("p (t h w) -> p t h w", t=TPC, h=GH)

        def groups(eng, run, last_looped=NG - 1):
            run(-1, NSLOT - 1, -1, False, True)
            rounds = last_looped // NSLOT
            with eng.Fori(0, rounds) as i:
                for u in range(NSLOT):
                    run(i * NSLOT + u, u, i, True, True)
            for g in range(rounds * NSLOT, NG):
                run(g, g % NSLOT, g // NSLOT, True, g < NG - 1)

        def following(u, r):
            return (u + 1) % NSLOT, r + (u + 1) // NSLOT

        def first_column(c, kt):
            return max(0, kt - TPC * c) * P

        @block.sync
        def _(sp):
            sp.dma_start(ident[:, :], ident_d).then_inc(consts, 16)
            sp.dma_start(maskf[:, :], mask_d).then_inc(consts, 16)
            for t in m_stored + o_stored:
                t.open(sp)

            def load(g, u):
                b, hg = g // NGROUP, g % NGROUP
                sp.dma_start(vt[:, u], v_v[:, b, hg]).then_inc(loaded[u].sem, 16)
                for dst, pick, o in ((qs, STACK_Q, 0), (ks, STACK_K, A_HEADS)):
                    for j, s in enumerate(pick):
                        src = parts_v[s, :, :, b][:, bass.ds(hg * GH + o, GH)]
                        sp.dma_start(dst[j * A_HD:(j + 1) * A_HD, u], src).then_inc(loaded[u].sem, 16)

            load(0, 0)
            load(1, 1)

            def run(g, u, r, main, mx_):
                if main and (not isinstance(g, int) or g + 2 < NG):
                    sp.wait_ge(pv_done.sem, pv_done.at(g - 1))
                    load(g + 2, (u + 2) % NSLOT)
                v, _ = following(u, r)

                def row_out(c):
                    sp.wait_ge(ntb_ready.sem, ntb_ready.at(g + 1, c + 1))
                    for j in range(GH):
                        sp.dma_start(qs[SROWS:SROWS + 1, v, j, c * CHUNK:(c + 1) * CHUNK],
                                     ntb[j * TPC:(j + 1) * TPC, c])\
                          .then_inc(m_stored[c].sem, 16)

                def out(c):
                    sp.wait_ge(otok_ready.sem, otok_ready.at(g, c + 1))
                    sp.dma_start(o_v[:, g // NGROUP, g % NGROUP, c],
                                 otok[:, c % 2].rearrange("p t h d -> p t (h d)"))\
                      .then_inc(o_stored[c % 2].sem, 16)

                none = lambda *a: None
                body(none, none, none, row_out, out, main, mx_)

            groups(sp, run, NG - 2)
            for t in o_stored:
                sp.wait_ge(t.sem, t.at(NG - 1))

        @block.gpsimd
        def _(pool):
            pool.memset(gate[:, :], 0.0).then_inc(gate_set, 1)
            pool.wait_ge(gate_set, 1)
            masked.open(pool)

            def run(g, u, r, main, mx_):
                def step(c, kt, s, piece):
                    if piece or kt < TPC * c:
                        return
                    q0 = first_column(c, kt)
                    for h in range(2):
                        pool.wait_ge(masked.sem, masked.at(g, 2 * kt + h))
                        tile = pt[:, (STEPS * u + s) % NPT, 2 * h:2 * h + 2, q0:q0 + P]
                        pool.wait_ge(exp_done.sem, exp_done.at(g, 2 * s + h + 1))
                        pool.tensor_tensor(out=gate[:, 1:2], in0=gate[:, 0:1], in1=gate[:, 0:1], op=ALU.add)
                        pool.affine_select(out=tile, in_=tile, compare_op=ALU.is_ge, fill=0.0, base=0,
                                           pattern=[[0, 2], [1, P]], channel_multiplier=-1)\
                            .then_inc(masked.sem, 1)

                none = lambda *a: None
                body(step, none, none, none, none, main, mx_)

            groups(pool, run)

        @block.scalar
        def _(act):
            for t in (exp_done, os_ready, ntb_ready):
                t.open(act)

            def run(g, u, r, main, mx_):
                def step(c, kt, s, piece):
                    if piece:
                        return
                    q0 = first_column(c, kt)
                    act.wait_ge(pv_done.sem, pv_done.at(g, s - NPT + 1))
                    for h in range(2):
                        act.wait_ge(st_done.sem, st_done.at(g, 2 * s + h + 1))
                        act.activation(pt[:, (STEPS * u + s) % NPT, 2 * h:2 * h + 2, q0:CHUNK],
                                       st[:, 2 * h:2 * h + 2, q0:CHUNK], ACT.Exp).then_inc(exp_done.sem, 1)
                    if kt == 0 and c:
                        raw_out(c - 1, s)

                def raw_out(c, s):
                    act.wait_ge(pv_done.sem, pv_done.at(g, s))
                    act.wait_ge(otr_done.sem, otr_done.at(g, c))
                    act.activation(os_[:, :], ot[:, :], ACT.Copy).then_inc(os_ready.sem, 1)

                def row_out(c):
                    act.wait_ge(nt_done.sem, nt_done.at(g + 1, c + 1))
                    act.wait_ge(m_stored[c].sem, m_stored[c].at(g))
                    act.activation(ntb[:, c], bank("row", c)[0:TASKS, 0:P], ACT.Copy).then_inc(ntb_ready.sem, 1)

                none = lambda *a: None
                body(step, none, none, row_out, none, main, mx_)
                if main:
                    raw_out(CPB - 1, STEPS)

            groups(act, run)

        @block.vector
        def _(dve):
            two_ones = float(np.array([0x3F803F80], np.uint32).view(np.float32)[0])
            dve.memset(ks[SROWS:SROWS + 1, :, :, :].bitcast(F32), two_ones).then_inc(ones_set, 1)
            dve.wait_ge(consts, 32)
            dve.tensor_copy(identb[:, :], ident[:, :]).then_inc(ones_set, 1)
            dve.tensor_copy(mask[:, :], maskf[:, :]).then_inc(ones_set, 1)
            for t in (mm_used, negm_ready, otok_ready):
                t.open(dve)

            def run(g, u, r, main, mx_):
                def unit(c, task, kc, n):
                    w = CHUNK if kc < c else (task % TPC + 1) * P
                    scores = bank("unit", n)[:, 0:w]
                    dve.wait_ge(mm_done.sem, mm_done.at(g + 1, n + 1))
                    dve.tensor_reduce(mx[:, task, kc:kc + 1], scores, AX.X, ALU.max)\
                       .then_inc(mm_used.sem, 1)

                def chunk_maxima(c, n):
                    dve.wait_ge(mm_used.sem, mm_used.at(g + 1, n))
                    dve.wait_ge(nt_done.sem, nt_done.at(g + 1, c - 1))
                    dve.tensor_reduce(negm[:, c % 2], mx[:, :, 0:c + 1], AX.X, ALU.max, negate=True)\
                       .then_inc(negm_ready.sem, 1)
                    dve.wait_ge(negm_ready.sem, negm_ready.at(g + 1, c + 1))

                def out(c):
                    dve.wait_ge(otok_ready.sem, otok_ready.at(g, c))
                    dve.wait_ge(otr_done.sem, otr_done.at(g, c + 1))
                    tr = rows_of(bank("out", c))
                    dve.reciprocal(rden[:, :, :], tr[:, :, :, A_HD]).then_inc(rden_ready.sem, 1)
                    dve.wait_ge(rden_ready.sem, rden_ready.at(g, c + 1))
                    dve.wait_ge(o_stored[c % 2].sem, o_stored[c % 2].at(g, 16 * (c // 2)))
                    dve.tensor_tensor(out=otok[:, c % 2].rearrange("p t h d -> p (t h) d"),
                                      in0=tr[:, :, :, 0:A_HD].rearrange("p t h d -> p (t h) d"),
                                      in1=rden[:, :, :].rearrange("p t h -> p (t h)").unsqueeze(2)
                                      .broadcast_to([P, TPC * GH, A_HD]),
                                      op=ALU.mult).then_inc(otok_ready.sem, 1)

                body(lambda *a: None, unit, chunk_maxima, lambda c: None, out, main, mx_)

            groups(dve, run)

        @block.tensor
        def _(pe):
            pe.wait_ge(consts, 32)
            pe.wait_ge(ones_set, 3)
            for t in (pv_done, nt_done, otr_done):
                t.open(pe)

            def run(g, u, r, main, mx_):
                v, rv = following(u, r)
                steps = [(c, kt) for c in range(CPB) for kt in range(TPC * (c + 1))]

                def weigh(s, half_):
                    c, kt = steps[s]
                    q0 = first_column(c, kt)
                    if kt == 0 and half_ == 0:
                        pe.wait_ge(os_ready.sem, os_ready.at(g, c))
                    if kt >= TPC * c:
                        pe.wait_ge(masked.sem, masked.at(g, 2 * kt + half_ + 1))
                    else:
                        pe.wait_ge(exp_done.sem, exp_done.at(g, 2 * s + half_ + 1))
                    for j in (2 * half_, 2 * half_ + 1):
                        mm = pe.matmul(ot[j * VW:(j + 1) * VW, q0:CHUNK],
                                       vt[:, u, kt, j * VW:(j + 1) * VW],
                                       pt[:, (STEPS * u + s) % NPT, j, q0:CHUNK],
                                       start=kt == 0, stop=kt == TPC * (c + 1) - 1)
                    if half_:
                        mm.then_inc(pv_done.sem, 1)

                def step(c, kt, s, piece):
                    q0 = first_column(c, kt)
                    if kt == 0 and piece == 0:
                        pe.wait_ge(m_stored[c].sem, m_stored[c].at(g))
                    if piece < 2:
                        pe.wait_ge(exp_done.sem, exp_done.at(g, 2 * s + piece - 1))
                        for j in (2 * piece, 2 * piece + 1):
                            mm = pe.matmul(st[:, j, q0:CHUNK], ks[0:SROWS + 1, u, j, kt * P:(kt + 1) * P],
                                           qs[0:SROWS + 1, u, j, c * CHUNK + q0:(c + 1) * CHUNK],
                                           start=True, stop=True)
                        mm.then_inc(st_done.sem, 1)
                    if piece >= 2 and s:
                        weigh(s - 1, piece - 2)

                def unit(c, task, kc, n):
                    j, t = divmod(task, TPC)
                    q0, w = c * CHUNK + t * P, CHUNK if kc < c else (t + 1) * P
                    pe.wait_ge(*bank_read(g, "unit", n, main, mx_))
                    mm = pe.matmul(bank("unit", n)[:, 0:w], qs[0:SROWS, v, j, q0:q0 + P],
                              ks[0:SROWS, v, j, kc * CHUNK:kc * CHUNK + w],
                              start=True, stop=kc < c)
                    if kc == c:
                        mm = pe.matmul(bank("unit", n)[:, w - P:w], identb[:, :], mask[:, :],
                                       start=False, stop=True)
                    mm.then_inc(mm_done.sem, 1)

                def row_out(c):
                    pe.wait_ge(negm_ready.sem, negm_ready.at(g + 1, c + 1))
                    pe.wait_ge(*bank_read(g, "row", c, main, mx_))
                    pe.transpose(bank("row", c)[0:TASKS, 0:P], negm[:, c % 2],
                                 ident[:, :]).then_inc(nt_done.sem, 1)

                def out(c):
                    if c == CPB - 1:
                        weigh(STEPS - 1, 0)
                        weigh(STEPS - 1, 1)
                    pe.wait_ge(os_ready.sem, os_ready.at(g, c + 1))
                    pe.wait_ge(*bank_read(g, "out", c, main, mx_))
                    for t in range(TPC):
                        mm = pe.transpose(bank("out", c)[:, t * P:(t + 1) * P],
                                          os_[:, t * P:(t + 1) * P], ident[:, :])
                    mm.then_inc(otr_done.sem, 1)

                if mx_:
                    pe.wait_ge(loaded[v].sem, loaded[v].per * (rv + 1))
                body(step, unit, lambda c, n: None, row_out, out, main, mx_)

            groups(pe, run)


def layers(nc, x_d, wqkv_d, wo_d, w1_d, w2_d, b1_d, b2_d, lng_d, lnb_d, scales_d, rotary_d, wmask_d,
           ident_d):
    with ExitStack() as ctx:
        def sb(name, shape, dt=F32):
            return ctx.enter_context(nc.sbuf_tensor("l_" + name, shape, dt))

        def tally(name, per=1, spare=0):
            return Tally(ctx.enter_context(nc.semaphore("l_" + name)), per, spare)

        TILES = SEQ // P
        PAIRS = HEADS // 2
        UNITS = TILES * PAIRS
        HT = INNER // P
        RING = 4

        ident = sb("ident", [P, P])
        mean_col = sb("mean_col", [P, 1])
        half = sb("half", [P, 2 * HEADS])
        gate = sb("gate", [P, 2])
        wmask = sb("wmask", [P, 2, 2 * P])
        wqkv_hi = sb("wqkv_hi", [P, KT, 3 * INNER], F32R)
        wqkv_lo = sb("wqkv_lo", [P, KT, 3 * INNER], F32R)
        wo_hi = sb("wo_hi", [P, HT, DIM], F32R)
        wo_lo = sb("wo_lo", [P, HT, DIM], F32R)
        w1_hi = sb("w1_hi", [P, KT, 2 * MT * MW], F32R)
        w1_lo = sb("w1_lo", [P, KT, 2 * MT * MW], F32R)
        w2_hi = sb("w2_hi", [MW, MT, DIM], F32R)
        w2_lo = sb("w2_lo", [MW, MT, DIM], F32R)
        rot = sb("rot", [P, TILES, 4, HD])
        b1 = sb("b1", [MW, 2 * MT])
        b1raw = sb("b1raw", [MW, 2 * MT])
        b2 = sb("b2", [P, KT])
        lng = sb("lng", [P, KT])
        lnb = sb("lnb", [P, KT])
        xt = sb("xt", [P, 2, KT, 1 + CHUNK])
        h_hi = sb("h_hi", [P, KT, CHUNK], F32R)
        h_lo = sb("h_lo", [P, KT, CHUNK], F32R)
        work = sb("work", [P, 3, 2 * HEADS, HD])
        sq, qn, rt = work[:, 0], work[:, 1], work[:, 2]
        stage = work[:, :, :, :].rearrange("p a h d -> p (a h d)")
        ss = sb("ss", [P, 2 * HEADS])
        ssm = sb("ssm", [P, 2 * HEADS])
        rn = sb("rn", [P, 2 * HEADS])
        qh = sb("qh", [P, 2, HEADS, P], F32R)
        ql = sb("ql", [P, 2, HEADS, P], F32R)
        kh = sb("kh", [P, PAIRS, RING, P], F32R)
        kl = sb("kl", [P, PAIRS, RING, P], F32R)
        vr = sb("vr", [P, RING, INNER])
        pr = sb("pr", [P, 3, 2, 2 * P])
        pr0 = sb("pr0", [P, 2, P])
        negm = sb("negm", [P, 4, 2])
        den = sb("den", [P, 4, 2])
        rden = sb("rden", [P, 4, 2])
        pts = sb("pts", [P, 2, 4, P])
        stage_o = vr[:, :, :].rearrange("p a n -> p (a n)")[:, 0:HT * DIM]
        stage_2 = pr[0:MW, :, :, :].rearrange("p a h n -> p (a h n)")[:, 0:MT * DIM]
        scales = pts[:, :, :, :].rearrange("p a b n -> p (a b n)")[:, 0:4 * HD]
        o_hi = sb("o_hi", [P, HT, CHUNK], F32R)
        o_lo = sb("o_lo", [P, HT, CHUNK], F32R)
        u_hi = sb("u_hi", [MW, 2, CHUNK], F32R)
        u_lo = sb("u_lo", [MW, 2, CHUNK], F32R)
        x1 = sb("x1", [P, KT, 1 + CHUNK])
        dx = sb("dx", [P, KT, CHUNK])
        gl = sb("gl", [P, 2, CHUNK])
        var = sb("var", [P, TPC])
        rstd = sb("rstd", [P, TPC])
        n_hi = sb("n_hi", [P, KT, CHUNK], F32R)
        n_lo = sb("n_lo", [P, KT, CHUNK], F32R)

        banks = ctx.enter_context(nc.psum_tensor("l_banks", [P, 8, CHUNK], F32))
        qkp, vp, xp, net = banks[:, 0:2], banks[:, 2], banks[:, 3], banks[:, 4]
        ptp, otp = banks[:, 6], banks[:, 7]
        w2p = banks[:, 3:5]
        ag = [(banks[:, 2], banks[:, 6]), (banks[:, 0], banks[:, 1])]

        consts = tally("consts", 48).sem
        init = tally("init").sem
        staged = tally("staged", 16 * 10)
        split = tally("split", 11)
        folded = tally("folded")
        fold_done = tally("fold_done")
        x_loaded = [tally(f"x_loaded{u}", 16 * CPB // 2) for u in range(2)]
        x_stored = tally("x_stored", 16 * CPB, 1)
        names = dict(
            h_hi_ready=CPB * KT, h_ready=CPB * KT, qk_done=2 * TILES, v_done=TILES, sq_ready=2 * TILES,
            sum_ready=2 * TILES, ssm_ready=2 * TILES, rn_ready=2 * TILES, qn_ready=2 * TILES,
            rt_ready=2 * TILES, cos_ready=2 * TILES, r_ready=2 * TILES, v_ready=TILES, xq_done=TILES, xk_done=TILES, qh_ready=TILES,
            ql_ready=TILES, kh_ready=TILES, k_ready=TILES, s_done=UNITS, sm_ready=UNITS,
            exp_done=UNITS, rden_ready=UNITS, p_ready=UNITS, pt_done=UNITS, pts_ready=UNITS,
            pv_done=UNITS, oh_ready=TILES, ol_ready=TILES, wo_done=CPB * KT, x1_ready=CPB * KT,
            mean_done=CPB, dx_ready=CPB, sq2_ready=CPB, var_done=CPB, var_ready=CPB, rstd_ready=CPB,
            bc_done=CPB, nx_ready=CPB * KT, n_hi_ready=CPB * KT, n_ready=CPB * KT, ag_done=CPB * MT,
            gelu_ready=CPB * MT, u_ready=CPB * MT, u_hi_ready=CPB * MT, u_lo_ready=CPB * MT,
            w2m_done=CPB * MT, x2_ready=CPB)
        S = {n: tally(n, per, 1) for n, per in names.items()}
        block = ctx.enter_context(nc.Block())

        x_v = x_d.rearrange("l k p (b n) -> p l b k n", n=SEQ)

        def key_tiles(T):
            if T == 0:
                return [0], slice(0, 1), wmask[:, 0, P:2 * P]
            if T % RING:
                return [T % RING - 1, T % RING], slice(T % RING - 1, T % RING + 1), wmask[:, 0]
            return [0, RING - 1], slice(0, RING, RING - 1), wmask[:, 1]

        def probabilities(i):
            if i == 0:
                return 3, pr0[:, :, :], -UNITS
            return (i - 1) % 3, pr[:, (i - 1) % 3], i - 3 if i > 3 else i - 4

        def score_bank(i):
            T, p = divmod(i % UNITS, PAIRS)
            net_used = T % TPC == 1 or T % TPC == 0 and p == 3
            return 4 if p % 2 and not net_used else 5

        def last_of_bank(i):
            return next(j for j in range(i - 1, i - 1 - UNITS, -1) if score_bank(j) == score_bank(i))

        per_sequence = dict(
            fetch=CPB, load=CPB, scores=UNITS, norm=UNITS, turn_p=UNITS, keep_p=UNITS, weigh=UNITS, part_o=TILES,
            project=2 * TILES, square=2 * TILES, sums=2 * TILES, rotate=2 * TILES, rotated=2 * TILES,
            project_v=TILES, keep_v=TILES, turn_q=TILES, turn_k=TILES, high_q=TILES,
            high_k=TILES,  part_x1=CPB * KT, mean=CPB,
            squares=CPB, variance=CPB, spread=CPB, high=CPB, low=CPB, network=CPB, last_network=CPB)

        def order(do, first, end, following):
            def there(n, count):
                return 0 <= n and (following or n < count)

            for T in range(first, end):
                ahead, chunk, t = there(T + 2, TILES), T // TPC - 1, T % TPC
                coming = (T + 3) // TPC
                for p in range(PAIRS):
                    i = T * PAIRS + p
                    if ahead and p == 3:
                        do("keep_v", T + 2)
                    if p == 3 and there(i - 2, UNITS):
                        do("keep_p", i - 2)
                    if chunk >= 0 and t == 1 and p == 3:
                        do("low", chunk)
                    if there(T + 1, TILES) and 0 < p < 3:
                        do(("high_q", "high_k")[p - 1], T + 1)
                    if there(i, UNITS):
                        do("scores", i)
                    if there(i - 1, UNITS):
                        do("norm", i - 1)
                    if chunk >= 0 and t == 0 and p == 3:
                        do("part_x1", chunk * KT)
                    if chunk >= 0 and t == 1 and p == 2:
                        do("spread", chunk)
                    if t == 1 and p == 0 and coming > 0 and there(coming, CPB):
                        do("fetch", coming)
                    if there(T + 1, TILES) and p == 0:
                        do("rotated", 2 * (T + 1) + 1)
                    if there(T + 1, TILES) and 0 < p < 3:
                        do(("turn_q", "turn_k")[p - 1], T + 1)
                    if ahead and p < 2:
                        do("project", 2 * (T + 2) + p)
                    if chunk >= 0 and t == 1 and p == 0:
                        do("mean", chunk)
                    if chunk >= 0 and t == 1 and p == 1:
                        do("variance", chunk)
                    if ahead and p < 2:
                        do("square", 2 * (T + 2) + p)
                    if there(i - 3, UNITS):
                        do("weigh", i - 3)
                        if (i - 3) % PAIRS == PAIRS - 1:
                            do("part_o", (i - 3) // PAIRS)
                    if there(i - 2, UNITS):
                        do("turn_p", i - 2)
                        if p < 3:
                            do("keep_p", i - 2)
                    if chunk >= 0 and t == 1 and p == 0:
                        do("squares", chunk)
                    if chunk >= 0 and t == 1 and p == 2:
                        do("high", chunk)
                    if ahead and p == 2:
                        do("project_v", T + 2)
                    if ahead and 0 < p < 3:
                        do("sums", 2 * (T + 2) + p - 1)
                    if t == 1 and p == 2 and coming > 0 and there(coming, CPB):
                        do("load", coming)
                    if ahead and p == (3 if t == 1 else 2):
                        do("rotate", 2 * (T + 2))
                    if ahead and p == 3:
                        do("rotate", 2 * (T + 2) + 1)
                        do("rotated", 2 * (T + 2))
                    if chunk >= 0 and t == 0 and p == 3:
                        do("part_x1", chunk * KT + 1)
                if chunk >= 0 and t == 1:
                    do("last_network" if T >= TILES and not following else "network", chunk)

        def program(eng, prepare_layer, events):
            def part(l, b, first, end, following):
                def do(event, n):
                    if event in events:
                        d, n = divmod(n, per_sequence[event])
                        events[event](l * BATCH + (b + d), l, b + d, n)

                if first < 0:
                    do("fetch", 0)
                    do("load", 0)
                order(do, first, end, following)

            with eng.Fori(0, DEPTH) as l:
                prepare_layer(l)
                part(l, 0, -2, 2, True)
                with eng.Fori(0, BATCH - 1) as b:
                    part(l, b, 2, TILES + 2, True)
                part(l, BATCH - 1, 2, TILES + 2, False)

        def wait(eng, name, B, k):
            eng.wait_ge(S[name].sem, S[name].at(B, k))

        @block.sync
        def _(sp):
            sp.dma_start(ident[:, :], ident_d).then_inc(consts, 16)
            sp.dma_start(wmask[:, :, :], wmask_d).then_inc(consts, 16)
            x_stored.open(sp)

            def prepare_layer(l):
                def get(dst, src):
                    sp.dma_start(dst, src).then_inc(staged.sem, 16)

                sp.wait_ge(x_stored.sem, x_stored.at(l * BATCH - 1))
                get(stage[:, 0:KT * 3 * INNER].rearrange("p (k n) -> p k n", k=KT),
                    wqkv_d[:, l].rearrange("(k p) n -> p k n", p=P))
                get(rot[:, :, :, :].rearrange("p t a d -> p t (a d)"),
                    rotary_d.rearrange("(t p) n -> p t n", p=P))
                get(scales, scales_d[l].partition_broadcast(P))
                get(b1raw[:, :], b1_d[:, l])
                get(b2[:, :], b2_d[:, l])
                get(lng[:, :], lng_d[:, l])
                get(lnb[:, :], lnb_d[:, l])
                get(stage_o.rearrange("p (k n) -> p k n", k=HT), wo_d[:, l].rearrange("(k p) n -> p k n", p=P))
                get(stage_2.rearrange("p (k n) -> p k n", k=MT), w2_d[:, l].rearrange("(k p) n -> p k n", p=MW))
                sp.wait_ge(split.sem, split.at(l, 2))
                get(stage[:, 0:KT * 2 * MT * MW].rearrange("p (k n) -> p k n", k=KT),
                    w1_d[:, l].rearrange("(k p) n -> p k n", p=P))

            def fetch(B, l, b, c):
                wait(sp, "x1_ready", B, (c - 1) * KT)
                first = 0 if c else 1
                sp.dma_start(xt[:, c % 2, :, first:], x_v[:, l, b, :, c * CHUNK - 1 + first:(c + 1) * CHUNK])\
                  .then_inc(x_loaded[c % 2].sem, 16)

            def network(B, l, b, c):
                wait(sp, "x2_ready", B, c + 1)
                sp.dma_start(x_v[:, l + 1, b, :, c * CHUNK:(c + 1) * CHUNK], dx[:, :, :])\
                  .then_inc(x_stored.sem, 16)

            program(sp, prepare_layer, dict(fetch=fetch, network=network, last_network=network))
            sp.wait_ge(x_stored.sem, x_stored.at(DEPTH * BATCH - 1))

        @block.gpsimd
        def _(pool):
            pool.memset(half[:, :], -0.5).then_inc(init, 1)
            pool.memset(mean_col[:, :], 1.0 / DIM).then_inc(init, 1)
            pool.memset(qh[:, :, :, :].bitcast(F32), 0.0).then_inc(init, 1)
            pool.memset(ql[:, :, :, :].bitcast(F32), 0.0).then_inc(init, 1)
            pool.wait_ge(init, 5)
            for n in ("h_ready", "rn_ready", "cos_ready", "rstd_ready"):
                S[n].open(pool)

            def prepare_layer(l):
                pass

            def load(B, l, b, c):
                wait(pool, "h_hi_ready", B, c * KT + 1)
                pool.tensor_tensor(out=h_lo[:, 0], in0=xt[:, c % 2, 0, 1:], in1=h_hi[:, 0].bitcast(F32),
                                   op=ALU.subtract).then_inc(S["h_ready"].sem, 1)
                if c == 0:
                    pool.memset(h_lo[:, 1, 0:1].bitcast(F32), 0.0)
                wait(pool, "h_hi_ready", B, (c + 1) * KT)
                f = 0 if c else 1
                pool.tensor_tensor(out=h_lo[:, 1, f:], in0=xt[:, c % 2, 1, f:CHUNK],
                                   in1=h_hi[:, 1, f:].bitcast(F32), op=ALU.subtract)\
                    .then_inc(S["h_ready"].sem, 1)

            def sums(B, l, b, n):
                a = n % 2
                wait(pool, "qn_ready", B, n - 1)
                wait(pool, "ssm_ready", B, n + 1)
                pool.tensor_tensor(out=rn[:, a * HEADS:(a + 1) * HEADS], in0=ssm[:, a * HEADS:(a + 1) * HEADS],
                                   in1=half[:, 0:HEADS], op=ALU.pow).then_inc(S["rn_ready"].sem, 1)

            def rotate(B, l, b, n):
                T, a = divmod(n, 2)
                part = slice(a * HEADS, (a + 1) * HEADS)
                wait(pool, "qn_ready", B, n + 1)
                pool.tensor_tensor(out=sq[:, part], in0=qn[:, part],
                                   in1=rot[:, T, a].unsqueeze(1).broadcast_to([P, HEADS, HD]),
                                   op=ALU.mult).then_inc(S["cos_ready"].sem, 1)

            def variance(B, l, b, c):
                wait(pool, "var_ready", B, c + 1)
                pool.tensor_tensor(out=rstd[:, :], in0=var[:, :], in1=half[:, 0:TPC], op=ALU.pow)\
                    .then_inc(S["rstd_ready"].sem, 1)

            program(pool, prepare_layer, dict(load=load, sums=sums, rotate=rotate, variance=variance))

        @block.scalar
        def _(act):
            for n in ("h_hi_ready", "sq_ready", "v_ready", "qh_ready", "kh_ready", "exp_done", "pts_ready",
                      "oh_ready", "sq2_ready", "n_hi_ready", "gelu_ready", "u_hi_ready"):
                S[n].open(act)

            def load(B, l, b, c):
                act.wait_ge(x_loaded[c % 2].sem, x_loaded[c % 2].at(B, 16 * (c // 2 + 1)))
                wait(act, "v_done", B, c * TPC)
                f = 0 if c else 1
                if c == 0:
                    act.activation(h_hi[:, 1, 0:1], gate[:, 0:1], ACT.Copy)
                act.activation(h_hi[:, 0], xt[:, c % 2, 0, 1:], ACT.Copy).then_inc(S["h_hi_ready"].sem, 1)
                act.activation(h_hi[:, 1, f:], xt[:, c % 2, 1, f:CHUNK], ACT.Copy)\
                   .then_inc(S["h_hi_ready"].sem, 1)

            def square(B, l, b, n):
                a = n % 2
                if n == 0:
                    act.wait_ge(split.sem, split.at(l))
                wait(act, "r_ready", B, n - 1)
                wait(act, "qk_done", B, n + 1)
                act.activation(sq[:, a * HEADS:(a + 1) * HEADS].rearrange("p h d -> p (h d)"), qkp[:, a],
                               ACT.Square).then_inc(S["sq_ready"].sem, 1)

            def keep_v(B, l, b, T):
                wait(act, "v_done", B, T + 1)
                wait(act, "pv_done", B, (T - RING + 2) * PAIRS)
                act.activation(vr[:, T % RING], vp, ACT.Copy).then_inc(S["v_ready"].sem, 1)

            def high_q(B, l, b, T):
                wait(act, "xq_done", B, T + 1)
                for h, half_ in enumerate((slice(0, HD), slice(HD, P))):
                    q = act.activation(qh[half_, T % 2, h::2], xp[half_].rearrange("p (a n) -> p a n", n=P),
                                       ACT.Copy)
                q.then_inc(S["qh_ready"].sem, 1)

            def high_k(B, l, b, T):
                wait(act, "xk_done", B, T + 1)
                act.activation(kh[:, :, T % RING], xp.rearrange("p (a n) -> p a n", n=P), ACT.Copy)\
                   .then_inc(S["kh_ready"].sem, 1)

            def scores(B, l, b, i):
                n = len(key_tiles(i // PAIRS)[0]) * P
                wait(act, "sm_ready", B, i + 1)
                s, p_, _ = probabilities(i)
                for h in range(2):
                    e = act.activation(p_[:, h, 0:n], p_[:, h, 0:n], ACT.Exp, scale=-1.0,
                                       bias=negm[:, s, h:h + 1], accum_out=den[:, s, h:h + 1])
                e.then_inc(S["exp_done"].sem, 1)

            def keep_p(B, l, b, i):
                n = 2 * len(key_tiles(i // PAIRS)[0])
                wait(act, "pv_done", B, i - 1)
                wait(act, "pt_done", B, i + 1)
                act.activation(pts[:, i % 2, 0:n].rearrange("p a n -> p (a n)"), ptp[:, 0:n * P], ACT.Copy)\
                   .then_inc(S["pts_ready"].sem, 1)

            def part_o(B, l, b, T):
                t = T % TPC
                wait(act, "pv_done", B, (T + 1) * PAIRS)
                act.activation(o_hi[:, :, t * P:(t + 1) * P], otp.rearrange("p (a n) -> p a n", n=P), ACT.Copy)\
                   .then_inc(S["oh_ready"].sem, 1)

            def squares(B, l, b, c):
                wait(act, "u_lo_ready", B, c * MT)
                wait(act, "dx_ready", B, c + 1)
                act.activation(gl[:, :, :], dx[:, :, :], ACT.Square).then_inc(S["sq2_ready"].sem, 1)

            def high(B, l, b, c):
                wait(act, "ag_done", B, c * MT)
                for k in range(KT):
                    wait(act, "nx_ready", B, c * KT + k + 1)
                    act.activation(n_hi[:, k], dx[:, k], ACT.Copy).then_inc(S["n_hi_ready"].sem, 1)

            def network(B, l, b, c):
                for m in range(MT):
                    k = c * MT + m
                    wait(act, "u_lo_ready", B, k - 1)
                    wait(act, "ag_done", B, k + 1)
                    act.activation(gl[0:MW, k % 2], ag[k % 2][1][0:MW], ACT.Gelu,
                                   bias=b1[:, MT + m:MT + m + 1]).then_inc(S["gelu_ready"].sem, 1)
                    wait(act, "w2m_done", B, k - 1)
                    wait(act, "u_ready", B, k + 1)
                    act.activation(u_hi[:, k % 2], gl[0:MW, k % 2], ACT.Copy)\
                       .then_inc(S["u_hi_ready"].sem, 1)

            act.wait_ge(init, 5)
            program(act, lambda l: None, dict(
                load=load, square=square, keep_v=keep_v, high_q=high_q, high_k=high_k, scores=scores,
                keep_p=keep_p, part_o=part_o, squares=squares, high=high, network=network,
                last_network=network))

        @block.vector
        def _(dve):
            dve.memset(gate[:, :], 0.0).then_inc(init, 1)
            dve.wait_ge(init, 5)
            dve.wait_ge(consts, 32)
            for n in ("sum_ready", "ssm_ready", "qn_ready", "rt_ready", "r_ready", "ql_ready", "k_ready",
                      "sm_ready", "rden_ready", "p_ready", "ol_ready", "x1_ready", "dx_ready", "var_ready", "nx_ready",
                      "n_ready", "u_ready", "u_lo_ready", "x2_ready"):
                S[n].open(dve)

            def prepare_layer(l):
                def parts(hi, lo, raw, k):
                    dve.tensor_copy(hi, raw).then_inc(split.sem, 1)
                    dve.wait_ge(split.sem, split.at(l, k + 1))
                    dve.tensor_tensor(out=lo, in0=raw, in1=hi.bitcast(F32), op=ALU.subtract)\
                       .then_inc(split.sem, 1)
                    if k + 2 < split.per:
                        dve.wait_ge(split.sem, split.at(l, k + 2))

                dve.wait_ge(staged.sem, staged.at(l, 9 * 16))
                parts(wqkv_hi[:, :, :], wqkv_lo[:, :, :],
                      stage[:, 0:KT * 3 * INNER].rearrange("p (k n) -> p k n", k=KT), 0)
                dve.tensor_tensor(out=rot[:, :, :, :].rearrange("p t a d -> p t (a d)"),
                                  in0=rot[:, :, :, :].rearrange("p t a d -> p t (a d)"),
                                  in1=scales.unsqueeze(1).broadcast_to([P, TILES, 4 * HD]),
                                  op=ALU.mult).then_inc(split.sem, 1)
                parts(wo_hi[:, :, :], wo_lo[:, :, :], stage_o.rearrange("p (k n) -> p k n", k=HT), 3)
                parts(w2_hi[:, :, :], w2_lo[:, :, :], stage_2.rearrange("p (k n) -> p k n", k=MT), 5)
                w1s = stage[:, 0:KT * 2 * MT * MW].rearrange("p (k n) -> p k n", k=KT)
                dve.wait_ge(fold_done.sem, fold_done.at(l))
                dve.tensor_tensor(out=b1[:, :], in0=banks[0:MW, 0, 0:2 * MT], in1=b1raw[:, :], op=ALU.add)\
                   .then_inc(split.sem, 1)
                for k in range(KT):
                    f = dve.tensor_scalar(w1s[:, k], w1s[:, k], lng[:, k:k + 1], None, ALU.mult)
                f.then_inc(folded.sem, 1)
                dve.wait_ge(folded.sem, folded.at(l))
                parts(w1_hi[:, :, :], w1_lo[:, :, :], w1s, 8)
                dve.tensor_copy(gate[:, 1:2], gate[:, 0:1]).then_inc(split.sem, 1)

            def sums(B, l, b, n):
                half_ = slice(n % 2 * HEADS, (n % 2 + 1) * HEADS)
                wait(dve, "rn_ready", B, n - 1)
                wait(dve, "sq_ready", B, n + 1)
                dve.tensor_reduce(ss[:, half_], sq[:, half_], AX.X, ALU.add).then_inc(S["sum_ready"].sem, 1)
                wait(dve, "sum_ready", B, n + 1)
                dve.tensor_scalar(ssm[:, half_], ss[:, half_], 1e-24, None, ALU.max)\
                   .then_inc(S["ssm_ready"].sem, 1)

            def rotate(B, l, b, n):
                T, a = divmod(n, 2)
                part = slice(a * HEADS, (a + 1) * HEADS)
                wait(dve, "cos_ready", B, n - 1)
                wait(dve, "rn_ready", B, n + 1)
                dve.tensor_tensor(out=qn[:, part], in0=qkp[:, a].rearrange("p (h d) -> p h d", d=HD),
                                  in1=rn[:, part].unsqueeze(2).broadcast_to([P, HEADS, HD]),
                                  op=ALU.mult).then_inc(S["qn_ready"].sem, 1)
                wait(dve, ("xq_done", "xk_done")[a], B, T)
                wait(dve, "qn_ready", B, n + 1)
                for s in range(2):
                    dst, src = slice(s * HD // 2, (s + 1) * HD // 2), slice((1 - s) * HD // 2, (2 - s) * HD // 2)
                    r = dve.tensor_tensor(out=rt[:, part, dst], in0=qn[:, part, src],
                                          in1=rot[:, T, 2 + a, dst].unsqueeze(1)
                                          .broadcast_to([P, HEADS, HD // 2]), op=ALU.mult)
                r.then_inc(S["rt_ready"].sem, 1)

            def rotated(B, l, b, n):
                part = slice(n % 2 * HEADS, (n % 2 + 1) * HEADS)
                wait(dve, "rt_ready", B, n + 1)
                wait(dve, "cos_ready", B, n + 1)
                dve.tensor_tensor(out=rt[:, part], in0=rt[:, part], in1=sq[:, part], op=ALU.add)\
                   .then_inc(S["r_ready"].sem, 1)

            def turn_q(B, l, b, T):
                wait(dve, "qh_ready", B, T + 1)
                for h, half_ in enumerate((slice(0, HD), slice(HD, P))):
                    q = dve.tensor_tensor(out=ql[half_, T % 2, h::2],
                                          in0=xp[half_].rearrange("p (a n) -> p a n", n=P),
                                          in1=qh[half_, T % 2, h::2].bitcast(F32), op=ALU.subtract)
                q.then_inc(S["ql_ready"].sem, 1)

            def turn_k(B, l, b, T):
                wait(dve, "kh_ready", B, T + 1)
                dve.tensor_tensor(out=kl[:, :, T % RING], in0=xp.rearrange("p (a n) -> p a n", n=P),
                                  in1=kh[:, :, T % RING].bitcast(F32), op=ALU.subtract)\
                   .then_inc(S["k_ready"].sem, 1)

            def scores(B, l, b, i):
                tiles, _, m = key_tiles(i // PAIRS)
                n = len(tiles) * P
                s, p_, before = probabilities(i)
                wait(dve, "pt_done", B, before + 1)
                wait(dve, "sm_ready", B, i)
                wait(dve, "s_done", B, i + 1)
                dve.tensor_copy(gate[:, 1:2], gate[:, 0:1])
                for h in range(2):
                    r = dve.tensor_tensor_reduce(p_[:, h, 0:n], banks[:, score_bank(i), h * 2 * P:h * 2 * P + n],
                                                 m, -1.0, 3e38, ALU.add, ALU.min, negm[:, s, h:h + 1])
                r.then_inc(S["sm_ready"].sem, 1)

            def norm(B, l, b, i):
                wait(dve, "exp_done", B, i + 1)
                s, p_, _ = probabilities(i)
                dve.reciprocal(rden[:, s], den[:, s]).then_inc(S["rden_ready"].sem, 1)
                n = len(key_tiles(i // PAIRS)[0]) * P
                wait(dve, "rden_ready", B, i + 1)
                for h in range(2):
                    r = dve.tensor_scalar(p_[:, h, 0:n], p_[:, h, 0:n], rden[:, s, h:h + 1], None, ALU.mult)
                r.then_inc(S["p_ready"].sem, 1)

            def part_o(B, l, b, T):
                t = T % TPC
                wait(dve, "oh_ready", B, T + 1)
                dve.tensor_tensor(out=o_lo[:, :, t * P:(t + 1) * P], in0=otp.rearrange("p (a n) -> p a n", n=P),
                                  in1=o_hi[:, :, t * P:(t + 1) * P].bitcast(F32), op=ALU.subtract)\
                   .then_inc(S["ol_ready"].sem, 1)

            def part_x1(B, l, b, n):
                c, k = divmod(n, KT)
                if k == 0:
                    wait(dve, "x2_ready", B, c)
                    if c:
                        dve.tensor_copy(x1[:, 1, 0:1], x1[:, 1, CHUNK:])
                    else:
                        dve.memset(x1[:, 1, 0:1], 0.0)
                wait(dve, "wo_done", B, n + 1)
                dve.tensor_tensor(out=x1[:, k, 1:], in0=net, in1=xt[:, c % 2, k, 1:], op=ALU.add)\
                   .then_inc(S["x1_ready"].sem, 1)

            def mean(B, l, b, c):
                dve.wait_ge(x_stored.sem, x_stored.at(B, 16 * c))
                wait(dve, "mean_done", B, c + 1)
                for k, rows in enumerate((x1[:, 0, 1:], x1[:, 1, 0:CHUNK])):
                    d = dve.tensor_tensor(out=dx[:, k], in0=rows, in1=net, op=ALU.subtract)
                d.then_inc(S["dx_ready"].sem, 1)

            def variance(B, l, b, c):
                wait(dve, "var_done", B, c + 1)
                dve.tensor_scalar(var[:, :], net[:, 0:TPC], EPS, None, ALU.add)\
                   .then_inc(S["var_ready"].sem, 1)

            def spread(B, l, b, c):
                wait(dve, "bc_done", B, c + 1)
                for k in range(KT):
                    dve.tensor_tensor(out=dx[:, k], in0=dx[:, k], in1=net, op=ALU.mult)\
                       .then_inc(S["nx_ready"].sem, 1)

            def low(B, l, b, c):
                for k in range(KT):
                    wait(dve, "n_hi_ready", B, c * KT + k + 1)
                    dve.tensor_tensor(out=n_lo[:, k], in0=dx[:, k], in1=n_hi[:, k].bitcast(F32),
                                      op=ALU.subtract).then_inc(S["n_ready"].sem, 1)

            def network(B, l, b, c):
                for m in range(MT):
                    k = c * MT + m
                    wait(dve, "gelu_ready", B, k + 1)
                    dve.scalar_tensor_tensor(out=gl[0:MW, k % 2], in0=ag[k % 2][0][0:MW],
                                             scalar=b1[:, m:m + 1], in1=gl[0:MW, k % 2],
                                             op0=ALU.add, op1=ALU.mult).then_inc(S["u_ready"].sem, 1)
                    wait(dve, "u_hi_ready", B, k + 1)
                    dve.tensor_tensor(out=u_lo[:, k % 2], in0=gl[0:MW, k % 2],
                                      in1=u_hi[:, k % 2].bitcast(F32), op=ALU.subtract)\
                       .then_inc(S["u_lo_ready"].sem, 1)
                wait(dve, "w2m_done", B, (c + 1) * MT)
                for k in range(KT):
                    d = dve.scalar_tensor_tensor(out=dx[:, k], in0=w2p[:, k], scalar=b2[:, k:k + 1],
                                                 in1=x1[:, k, 1:], op0=ALU.add, op1=ALU.add)
                d.then_inc(S["x2_ready"].sem, 1)

            program(dve, prepare_layer, dict(
                sums=sums, rotate=rotate, rotated=rotated, turn_q=turn_q, turn_k=turn_k, scores=scores,
                norm=norm, part_o=part_o, part_x1=part_x1, mean=mean, variance=variance, spread=spread,
                low=low, network=network, last_network=network))

        @block.tensor
        def _(pe):
            pe.wait_ge(consts, 32)
            pe.wait_ge(init, 5)
            for n in ("qk_done", "v_done", "xq_done", "xk_done", "s_done", "pt_done", "pv_done", "wo_done",
                      "mean_done", "var_done", "bc_done", "ag_done", "w2m_done"):
                S[n].open(pe)

            def products(out, steps):
                for j, (w, x_) in enumerate(steps):
                    mm = pe.matmul(out, w, x_, start=j == 0, stop=j == len(steps) - 1)
                return mm

            def three(w_hi, w_lo, x_hi_, x_lo_):
                return [(w_lo, x_hi_), (w_hi, x_lo_), (w_hi, x_hi_)]

            def prepare_layer(l):
                pe.wait_ge(staged.sem, staged.at(l))
                for m in range(2 * MT):
                    for k in range(KT):
                        o = k * 2 * MT * MW + m * MW
                        mm = pe.matmul(banks[0:MW, 0, m:m + 1], stage[:, o:o + MW], lnb[:, k:k + 1],
                                       start=k == 0, stop=k == KT - 1)
                mm.then_inc(fold_done.sem, 1)

            def project(B, l, b, n):
                T, a = divmod(n, 2)
                c, t = divmod(T, TPC)
                if n == 0:
                    pe.wait_ge(split.sem, split.at(l, 8))
                wait(pe, "qn_ready", B, n - 1)
                rows, cols = slice(t * P, (t + 1) * P), slice(a * INNER, (a + 1) * INNER)
                for k in range(KT):
                    if t == 0 and a == 0:
                        wait(pe, "h_ready", B, c * KT + k + 1)
                    steps = three(h_hi[:, k, rows], h_lo[:, k, rows], wqkv_hi[:, k, cols], wqkv_lo[:, k, cols])
                    for j, (w, x_) in enumerate(steps):
                        mm = pe.matmul(qkp[:, a], w, x_, start=k == 0 and j == 0,
                                       stop=k == KT - 1 and j == len(steps) - 1)
                mm.then_inc(S["qk_done"].sem, 1)

            def project_v(B, l, b, T):
                t = T % TPC
                rows, cols = slice(t * P, (t + 1) * P), slice(2 * INNER, 3 * INNER)
                wait(pe, "v_ready", B, T)
                products(vp, [s for k in range(KT) for s in three(
                    h_hi[:, k, rows], h_lo[:, k, rows], wqkv_hi[:, k, cols], wqkv_lo[:, k, cols])])\
                    .then_inc(S["v_done"].sem, 1)

            def turn(first, sem):
                for p in range(PAIRS):
                    mm = pe.transpose(xp[:, p * P:(p + 1) * P],
                                      rt[:, first + 2 * p:first + 2 * p + 2].rearrange("p h d -> p (h d)"),
                                      ident[:, :])
                mm.then_inc(sem, 1)

            def turn_q(B, l, b, T):
                wait(pe, "r_ready", B, 2 * T + 1)
                wait(pe, "k_ready", B, T)
                if T % TPC == TPC - 1:
                    wait(pe, "x2_ready", B, T // TPC)
                turn(0, S["xq_done"].sem)

            def turn_k(B, l, b, T):
                wait(pe, "r_ready", B, 2 * (T + 1))
                wait(pe, "ql_ready", B, T + 1)
                turn(HEADS, S["xk_done"].sem)

            def scores(B, l, b, i):
                T, p = divmod(i, PAIRS)
                tiles, at, _ = key_tiles(T)
                n = len(tiles) * P
                if p == 0:
                    wait(pe, "k_ready", B, T + 1)
                wait(pe, "sm_ready", B, last_of_bank(i) + 1)
                if T % TPC == 2 and p == 1:
                    wait(pe, "x2_ready", B, T // TPC)
                for h in range(2):
                    mm = products(banks[:, score_bank(i), h * 2 * P:h * 2 * P + n], three(
                        qh[:, T % 2, 2 * p + h], ql[:, T % 2, 2 * p + h], kh[:, p, at], kl[:, p, at]))
                mm.then_inc(S["s_done"].sem, 1)

            def turn_p(B, l, b, i):
                n = len(key_tiles(i // PAIRS)[0])
                wait(pe, "pts_ready", B, i)
                wait(pe, "p_ready", B, i + 1)
                for h in range(2):
                    for k in range(n):
                        mm = pe.transpose(ptp[:, (h * n + k) * P:(h * n + k + 1) * P],
                                          probabilities(i)[1][:, h, k * P:(k + 1) * P], ident[:, :])
                mm.then_inc(S["pt_done"].sem, 1)

            def weigh(B, l, b, i):
                T, p = divmod(i, PAIRS)
                tiles = key_tiles(T)[0]
                if p == 0:
                    wait(pe, "ol_ready", B, T)
                    wait(pe, "v_ready", B, T + 1)
                wait(pe, "pts_ready", B, i + 1)
                for k, slot in enumerate(tiles):
                    for h in range(2):
                        mm = pe.matmul(otp[h * HD:(h + 1) * HD, p * P:(p + 1) * P],
                                       vr[:, slot, (2 * p + h) * HD:(2 * p + h + 1) * HD],
                                       pts[:, i % 2, h * len(tiles) + k], start=k == 0,
                                       stop=k == len(tiles) - 1)
                mm.then_inc(S["pv_done"].sem, 1)

            def part_x1(B, l, b, n):
                c, k = divmod(n, KT)
                if k == 0:
                    wait(pe, "ol_ready", B, (c + 1) * TPC)
                wait(pe, "x1_ready", B, n)
                cols = slice(k * P, (k + 1) * P)
                products(net, [s for j in range(HT) for s in three(
                    wo_hi[:, j, cols], wo_lo[:, j, cols], o_hi[:, j], o_lo[:, j])])\
                    .then_inc(S["wo_done"].sem, 1)

            def mean(B, l, b, c):
                wait(pe, "x1_ready", B, (c + 1) * KT)
                products(net, [(mean_col[:, :].broadcast_to([P, P]), x1[:, 0, 1:]),
                               (mean_col[:, :].broadcast_to([P, P]), x1[:, 1, 0:CHUNK])])\
                    .then_inc(S["mean_done"].sem, 1)

            def variance(B, l, b, c):
                wait(pe, "sq2_ready", B, c + 1)
                for t in range(TPC):
                    mm = products(net[:, t:t + 1], [(gl[:, k, t * P:(t + 1) * P], mean_col[:, :])
                                                    for k in range(KT)])
                mm.then_inc(S["var_done"].sem, 1)

            def spread(B, l, b, c):
                wait(pe, "rstd_ready", B, c + 1)
                for t in range(TPC):
                    mm = pe.matmul(net[:, t * P:(t + 1) * P], rstd[:, t:t + 1].broadcast_to([P, P]),
                                   ident[:, :], start=True, stop=True)
                mm.then_inc(S["bc_done"].sem, 1)

            def network(B, l, b, c, last=False):
                T = c * TPC + TPC + 1
                tiles, pairs = (TILES, UNITS) if last else (T + 3, T * PAIRS + 2)
                wait(pe, "v_ready", B, tiles)
                wait(pe, "pts_ready", B, pairs)
                lag = 2
                for m in range(MT + lag):
                    k = c * MT + m
                    if m < MT:
                        if m == 1:
                            wait(pe, "qn_ready", B, 2 * tiles)
                        wait(pe, "u_ready", B, k - 1)
                        for half_, bank in ((0, 0), (1, 1)):
                            cols = slice((half_ * MT + m) * MW, (half_ * MT + m + 1) * MW)
                            for j in range(KT):
                                if m == 0 and bank == 0:
                                    wait(pe, "n_ready", B, c * KT + j + 1)
                                for q, (w, x_) in enumerate(three(
                                        w1_hi[:, j, cols], w1_lo[:, j, cols], n_hi[:, j], n_lo[:, j])):
                                    mm = pe.matmul(ag[k % 2][bank][0:MW], w, x_, start=j == 0 and q == 0,
                                                   stop=j == KT - 1 and q == 2)
                        mm.then_inc(S["ag_done"].sem, 1)
                    if m >= lag:
                        k, m_ = k - lag, m - lag
                        if m_ == 0:
                            wait(pe, "k_ready", B, TILES if last else T + 2)
                        wait(pe, "u_lo_ready", B, k + 1)
                        for o in range(KT):
                            cols = slice(o * P, (o + 1) * P)
                            steps = three(w2_hi[:, m_, cols], w2_lo[:, m_, cols],
                                          u_hi[:, k % 2], u_lo[:, k % 2])
                            for j, (w, x_) in enumerate(steps):
                                mm = pe.matmul(w2p[:, o], w, x_, start=m_ == 0 and j == 0,
                                               stop=m_ == MT - 1 and j == 2)
                        mm.then_inc(S["w2m_done"].sem, 1)

            program(pe, prepare_layer, dict(
                project=project, project_v=project_v, turn_q=turn_q, turn_k=turn_k, scores=scores,
                turn_p=turn_p, weigh=weigh, part_x1=part_x1, mean=mean, variance=variance,
                spread=spread, network=network,
                last_network=lambda B, l, b, c: network(B, l, b, c, True)))


def combine(nc, x, x2_d, o_d, wo_d, bo_d, ident_d, out):
    with ExitStack() as ctx:
        def sb(name, shape, dt=F32):
            return ctx.enter_context(nc.sbuf_tensor("c_" + name, shape, dt))

        def tally(name, per=1, spare=0):
            return Tally(ctx.enter_context(nc.semaphore("c_" + name)), per, spare)

        ident = sb("ident", [P, P])
        w_raw = sb("w_raw", [P, KT, DIM])
        w_hi = sb("w_hi", [P, KT, DIM], F32R)
        w_lo = sb("w_lo", [P, KT, DIM], F32R)
        bo = sb("bo", [P, DIM])
        o_in = sb("o_in", [P, 2, TPC, DIM])
        x2 = sb("x2", [P, 2, KT, CHUNK])
        x_in = sb("x_in", [P, 2, TPC, DIM])
        o_hi = sb("o_hi", [P, 2, KT, CHUNK], F32R)
        o_lo = sb("o_lo", [P, 2, KT, CHUNK], F32R)
        g = sb("g", [P, 2, TPC, DIM])
        y = sb("y", [P, 2, TPC, DIM])
        otp = ctx.enter_context(nc.psum_tensor("c_otp", [P, KT, CHUNK], F32))
        x2p = ctx.enter_context(nc.psum_tensor("c_x2p", [P, TPC, DIM], F32))
        sp_ = ctx.enter_context(nc.psum_tensor("c_sp", [P, TPC, DIM], F32))

        consts = tally("consts").sem
        w_split = tally("w_split").sem
        loaded = [tally(f"loaded{u}", 32) for u in range(2)]
        x_loaded = [tally(f"x_loaded{u}", 16) for u in range(2)]
        stored = [tally(f"stored{u}", 16, 1) for u in range(2)]
        tr_done = tally("tr_done", 1, 2)
        oh_ready = tally("oh_ready")
        ol_ready = tally("ol_ready", 1, 1)
        g_ready = tally("g_ready", 1, 1)
        s_done = tally("s_done", 1, 2)
        y1_ready = tally("y1_ready", 1, 1)
        y2_ready = tally("y2_ready")
        y_ready = tally("y_ready", 1, 2)
        block = ctx.enter_context(nc.Block())

        rows = lambda a: a.rearrange("(c t p) d -> p c t d", p=P, t=TPC)
        x_v, out_v = (a.rearrange("b (c t p) d -> p (b c) t d", p=P, t=TPC) for a in (x, out))
        o_v = rows(o_d)
        x2_v = x2_d.rearrange("k p (c n) -> p c k n", n=CHUNK)

        @block.sync
        def _(sp):
            sp.dma_start(ident[:, :], ident_d).then_inc(consts, 16)
            sp.dma_start(w_raw[:, :, :], wo_d.rearrange("(k p) n -> p k n", p=P)).then_inc(consts, 16)
            sp.dma_start(bo[:, :], bo_d.partition_broadcast(P)).then_inc(consts, 16)
            for t in stored:
                t.open(sp)

            def load(n, u):
                sp.wait_ge(tr_done.sem, tr_done.at(n - 2))
                sp.dma_start(o_in[:, u], o_v[:, n]).then_inc(loaded[u].sem, 16)
                sp.dma_start(x2[:, u], x2_v[:, n]).then_inc(loaded[u].sem, 16)

            def load_x(n, u):
                sp.wait_ge(y_ready.sem, y_ready.at(n - 2))
                sp.dma_start(x_in[:, u], x_v[:, n]).then_inc(x_loaded[u].sem, 16)

            def store(n, u):
                sp.wait_ge(y_ready.sem, y_ready.at(n))
                sp.dma_start(out_v[:, n], y[:, u]).then_inc(stored[u].sem, 16)

            staggered(sp, NCHUNK, load, load_x, lambda n, u: None, store)
            for u in range(2):
                sp.wait_ge(stored[u].sem, stored[u].at_turn(NCHUNK - 2 + u, u))

        @block.scalar
        def _(act):
            g_ready.open(act)

            def first(n, u):
                act.wait_ge(tr_done.sem, tr_done.at(n))
                act.wait_ge(s_done.sem, s_done.at(n - 2))
                act.activation(o_hi[:, u], otp[:, :, :], ACT.Copy).then_inc(oh_ready.sem, 1)
                act.wait_ge(y_ready.sem, y_ready.at(n - 2))
                act.activation(g[:, u], x2p[:, :, :], ACT.Silu).then_inc(g_ready.sem, 1)

            staggered(act, NCHUNK, lambda n, u: None, first, lambda n, u: None)

        @block.vector
        def _(dve):
            dve.wait_ge(consts, 48)
            dve.tensor_copy(w_hi[:, :, :], w_raw[:, :, :]).then_inc(w_split, 1)
            dve.wait_ge(w_split, 1)
            dve.tensor_tensor(out=w_lo[:, :, :], in0=w_raw[:, :, :], in1=w_hi[:, :, :].bitcast(F32),
                              op=ALU.subtract).then_inc(w_split, 1)
            for t in (ol_ready, y1_ready, y_ready):
                t.open(dve)

            def first(n, u):
                dve.wait_ge(oh_ready.sem, oh_ready.at(n))
                dve.tensor_tensor(out=o_lo[:, u], in0=otp[:, :, :], in1=o_hi[:, u].bitcast(F32),
                                  op=ALU.subtract).then_inc(ol_ready.sem, 1)

            def second(n, u):
                dve.wait_ge(stored[u].sem, stored[u].before_turn(n, u))
                dve.wait_ge(s_done.sem, s_done.at(n))
                dve.tensor_tensor(out=y[:, u], in0=sp_[:, :, :],
                                  in1=bo[:, :].unsqueeze(1).broadcast_to([P, TPC, DIM]),
                                  op=ALU.add).then_inc(y1_ready.sem, 1)
                dve.wait_ge(g_ready.sem, g_ready.at(n))
                dve.wait_ge(y1_ready.sem, y1_ready.at(n))
                dve.tensor_tensor(out=y[:, u], in0=y[:, u], in1=g[:, u], op=ALU.mult).then_inc(y2_ready.sem, 1)
                dve.wait_ge(y2_ready.sem, y2_ready.at(n))
                dve.wait_ge(x_loaded[u].sem, x_loaded[u].at_turn(n, u))
                dve.tensor_tensor(out=y[:, u], in0=y[:, u], in1=x_in[:, u], op=ALU.add)\
                   .then_inc(y_ready.sem, 1)

            staggered(dve, NCHUNK, lambda n, u: None, first, second)

        @block.tensor
        def _(pe):
            pe.wait_ge(consts, 48)
            pe.wait_ge(w_split, 2)
            tr_done.open(pe)
            s_done.open(pe)

            def first(n, u):
                pe.wait_ge(loaded[u].sem, loaded[u].at_turn(n, u))
                pe.wait_ge(ol_ready.sem, ol_ready.at(n - 1))
                pe.wait_ge(g_ready.sem, g_ready.at(n - 1))
                for t in range(TPC):
                    for k in range(KT):
                        pe.transpose(otp[:, k, t * P:(t + 1) * P], o_in[:, u, t, k * P:(k + 1) * P],
                                     ident[:, :])
                        mm = pe.transpose(x2p[:, t, k * P:(k + 1) * P], x2[:, u, k, t * P:(t + 1) * P],
                                          ident[:, :])
                mm.then_inc(tr_done.sem, 1)

            def second(n, u):
                pe.wait_ge(ol_ready.sem, ol_ready.at(n))
                pe.wait_ge(y1_ready.sem, y1_ready.at(n - 1))
                for t in range(TPC):
                    r = slice(t * P, (t + 1) * P)
                    steps = [(o, w, k) for k in range(KT)
                             for o, w in ((o_lo, w_hi), (o_hi, w_lo), (o_hi, w_hi))]
                    for j, (o, w, k) in enumerate(steps):
                        mm = pe.matmul(sp_[:, t], o[:, u, k, r], w[:, k],
                                       start=j == 0, stop=j == len(steps) - 1)
                mm.then_inc(s_done.sem, 1)

            staggered(pe, NCHUNK, lambda n, u: None, first, second)


def program(nc, i, out):
    def scratch(name, shape, dt=F32):
        return nc.dram_tensor(name, shape, dt).ap()

    x_d = scratch("x_d", (DEPTH + 1, KT, P, ROWS))
    qk_d = scratch("qk_d", (3, 4, P, ROWS), BF16)
    v_d = scratch("v_d", (ROWS, A_HEADS * VW))
    o_d = scratch("o_d", (ROWS, DIM))
    prepare(nc, i["x"], [i["wq"], i["wk"], i["wv"]], i["bqk"], i["bv"], i["ident"], x_d[0], qk_d, v_d)
    attend(nc, qk_d, v_d, i["causal"], i["ident"], o_d)
    layers(nc, x_d, i["wqkv"], i["wo_l"], i["w1"], i["w2"], i["b1"], i["b2"], i["ln_g"], i["ln_b"],
           i["scales"], i["rotary"], i["window"], i["ident"])
    combine(nc, i["x"], x_d[DEPTH], o_d, i["wo"], i["bo"], i["ident"], out)


def constants():
    f = np.float32
    at = np.arange(P)
    causal = np.where(at[None] > at[:, None], -BIG, 0.0)
    previous = np.where(at[None] >= at[:, None], 0.0, -BIG)
    own = np.where(at[None] <= at[:, None], 0.0, -BIG)
    window = np.stack([np.concatenate([previous, own], 1), np.concatenate([own, previous], 1)], 1)
    pos = np.arange(SEQ, dtype=f)
    even = np.arange(0, HD, 2, dtype=f)
    freq = pos[:, None] * (f(1.0) / f(10000.0) ** (even / f(HD)))[None]
    base = (even + f(0.4 * HD)) / f(1.4 * HD)
    xpos = base[None] ** ((pos - f(SEQ // 2)) / f(WINDOW // 2))[:, None]
    freq, xpos = (np.concatenate([a, a], 1) for a in (freq, xpos))
    turned = np.where(np.arange(HD) < HD // 2, f(-1.0), f(1.0))
    cos, sin = np.cos(freq), np.sin(freq) * turned
    tables = [cos * xpos * f(QK_SCALE), cos / xpos, sin * xpos * f(QK_SCALE), sin / xpos]
    return {"ident": np.eye(P, dtype=f), "causal": causal.astype(f), "window": window.astype(f),
            "rotary": np.concatenate(tables, 1).astype(f)}


def lay_out(a):
    def columns(v):
        return v.reshape(DEPTH, KT, P).transpose(2, 0, 1)

    q, k = a["L0_ffn_q_scale"], a["L0_ffn_k_scale"]
    swap = lambda s: np.concatenate([s[:, HD // 2:], s[:, :HD // 2]], 1)
    w1 = np.zeros((DIM, DEPTH, 2, MT * MW), np.float32)
    w1[..., :HID] = a["L0_ffn_w1"].reshape(DEPTH, DIM, 2, HID).transpose(1, 0, 2, 3)
    b1 = np.zeros((DEPTH, 2, MT * MW), np.float32)
    b1[..., :HID] = a["L0_ffn_b1"].reshape(DEPTH, 2, HID)
    w2 = np.zeros((MT * MW, DEPTH, DIM), np.float32)
    w2[:HID] = a["L0_ffn_w2"].transpose(1, 0, 2)
    return {
        "x": a["L0_attn_x"], "wq": a["L0_attn_Wq"].T, "wk": a["L0_attn_Wk"].T, "wv": a["L0_attn_Wv"].T,
        "bqk": np.concatenate([a["L0_attn_bq"], a["L0_attn_bk"]]).reshape(4, P).T,
        "bv": a["L0_attn_bv"], "wo": a["L0_attn_Wo"].T, "bo": a["L0_attn_bo"],
        "wqkv": a["L0_ffn_wqkv"].transpose(1, 0, 2), "wo_l": a["L0_ffn_wo"].transpose(1, 0, 2),
        "w1": w1.reshape(DIM, DEPTH, 2 * MT * MW), "w2": w2,
        "b1": b1.reshape(DEPTH, 2 * MT, MW).transpose(2, 0, 1), "b2": columns(a["L0_ffn_b2"]),
        "ln_g": columns(a["L0_ffn_ln_g"]), "ln_b": columns(a["L0_ffn_ln_b"]),
        "scales": np.concatenate([q, k, swap(q), swap(k)], 1),
    }


def kernel(**inputs):
    import concourse.bacc as bacc
    from concourse.bass_utils import run_bass_kernel_spmd

    nc = bacc.Bacc("TRN2", target_bir_lowering=False, num_devices=1)
    arrays = {**lay_out({n: np.asarray(v) for n, v in inputs.items()}), **constants()}
    arrays = {n: np.ascontiguousarray(v) for n, v in arrays.items()}
    tensors = {n: nc.dram_tensor(n, v.shape, mybir.dt.from_np(v.dtype), kind="ExternalInput").ap()
               for n, v in arrays.items()}
    out = nc.dram_tensor("out", (BATCH, SEQ, DIM), F32, kind="ExternalOutput")
    program(nc, tensors, out.ap())
    r = run_bass_kernel_spmd(nc, [arrays], core_ids=[0])
    return r.results[0]["out"]
```
